# Optimizing a Trainium2 kernel written in Bass

```python
import numpy as np
import jax
import jax.numpy as jnp

def _softmax(x, axis=-1):
    return jax.nn.softmax(x, axis=axis)

def _gelu(x):
    return jax.nn.gelu(x, approximate=True)

def _silu(x):
    return jax.nn.silu(x)

def _sigmoid(x):
    return jax.nn.sigmoid(x)

def _layernorm(x, axis=-1, eps=1e-05):
    m = jnp.mean(x, axis=axis, keepdims=True)
    v = jnp.var(x, axis=axis, keepdims=True)
    return (x - m) / jnp.sqrt(v + eps)

def _scatter_add(tgt, idx, src, axis=0):
    return tgt.at[idx].add(src)

def _segment_sum(src, seg, n):
    return jax.ops.segment_sum(src, seg, n)
kernel_name = 'mk_flamingo_gated_d2_seqx_r4_29f782'

def setup_inputs(seed: int=0):
    np.random.seed(seed)
    _w = jnp.asarray

    def _rec_inputs():
        import jax
        import jax.numpy as jnp
        _rk = jax.random.key(seed)
        x = 7.22e-05 + 1 * jax.random.normal(jax.random.fold_in(_rk, 1), (8, 256, 256), jnp.float32)
        _lenS = 256 - jax.random.randint(jax.random.fold_in(_rk, 7), (8,), 0, max(1, 256 // 4) + 1, jnp.int32)
        _lenS2 = 77 - jax.random.randint(jax.random.fold_in(_rk, 8), (8,), 0, max(1, 77 // 4) + 1, jnp.int32)
        _ctx_1024P = jax.random.normal(jax.random.fold_in(_rk, 11), (8, 16, 256), jnp.float32)
        _ctx_1024c = jax.random.dirichlet(jax.random.fold_in(_rk, 511), 0.3 * jnp.ones((16,), jnp.float32), (8, 77))
        _ctx_1024t = jnp.einsum('bsk,bkd->bsd', _ctx_1024c, _ctx_1024P)
        _ctx_1024t = _ctx_1024t * jax.lax.rsqrt(jnp.mean(jnp.square(_ctx_1024t)) + 1e-12) * 0.953939
        ctx_1024 = 4.13588e-05 + 0.999923 * (_ctx_1024t + 0.3 * jax.random.normal(jax.random.fold_in(_rk, 611), (8, 77, 256), jnp.float32))
        _validS = jnp.arange(256)[None, :] < _lenS[:, None]
        _validS2 = jnp.arange(77)[None, :] < _lenS2[:, None]
        _causal = jnp.tril(jnp.ones((256, 256), dtype=bool))
        mask_1x1xSxS2_bk1 = jnp.broadcast_to(_validS2[0:1, None, None, :], (1, 1, 256, 77))
        _g = jax.random.normal(jax.random.fold_in(_rk, 9001), (2, 2), jnp.float32)
        _g = jnp.sign(_g) * jnp.maximum(jnp.abs(_g), 1.0) + (_g == 0) * 1.0
        g_xattn = _g[0]
        g_ffn = _g[1]
        return (x, ctx_1024, mask_1x1xSxS2_bk1, g_xattn, g_ffn)
    x, ctx_1024, mask_1x1xSxS2_bk1, g_xattn, g_ffn = _rec_inputs()

    def _L0_xattn_setup():
        import jax, jax.numpy as jnp
        import numpy as np
        DIM = 256
        N_HEADS = 16
        HEAD_DIM = DIM // N_HEADS
        SCALE = HEAD_DIM ** (-0.5)
        B, S = (4, 512)

        def _split_heads(t):
            Bc, Sc, _ = t.shape
            return t.reshape(Bc, Sc, N_HEADS, HEAD_DIM).transpose(0, 2, 1, 3)
        key = jax.random.key(seed)
        ks = jax.random.split(key, 12)
        w = lambda k, shp: jax.random.normal(k, shp, dtype=jnp.float32) * 0.02
        return {'x0': jax.random.normal(ks[0], (B, S, DIM), dtype=jnp.float32), 'x1': jax.random.normal(ks[1], (B, S, DIM), dtype=jnp.float32), 'x2': jax.random.normal(ks[2], (B, S, DIM), dtype=jnp.float32), 'Wq': w(ks[3], (DIM, DIM)), 'bq': w(ks[4], (DIM,)), 'Wk': w(ks[5], (DIM, DIM)), 'bk': w(ks[6], (DIM,)), 'Wv': w(ks[7], (DIM, DIM)), 'bv': w(ks[8], (DIM,)), 'Wp': w(ks[9], (DIM, DIM)), 'bp': w(ks[10], (DIM,))}
    _L0_xattn_all = _L0_xattn_setup()
    _L0_xattn_in = {k: v for k, v in _L0_xattn_all.items() if k in ('Wq', 'bq', 'Wk', 'bk', 'Wv', 'bv', 'Wp', 'bp')}
    del _L0_xattn_all

    def _L0_ffn_setup():
        import jax, jax.numpy as jnp
        import numpy as np

        def gelu(x):
            return jax.nn.gelu(x, approximate=False)
        key = jax.random.key(seed)
        ks = jax.random.split(key, 6)
        B, S, d_model = (4, 512, 256)
        n_input, n_process, n_output, d_pv = (2048, 1024, 2048, 128)
        s = 0.02
        return {'x': jax.random.normal(ks[0], (B, S, d_model), jnp.float32), 'input_patterns': jax.random.normal(ks[1], (n_input, d_model), jnp.float32) * s, 'process_input_weights': jax.random.normal(ks[2], (n_process, n_input), jnp.float32) * s, 'process_values': jax.random.normal(ks[3], (n_process, d_pv), jnp.float32) * s, 'output_input_weights': jax.random.normal(ks[4], (n_output, d_pv), jnp.float32) * s, 'output_patterns': jax.random.normal(ks[5], (n_output, d_model), jnp.float32) * s}
    _L0_ffn_all = _L0_ffn_setup()
    _L0_ffn_in = {k: v for k, v in _L0_ffn_all.items() if k in ('input_patterns', 'process_input_weights', 'process_values', 'output_input_weights', 'output_patterns')}
    del _L0_ffn_all

    def _L1_xattn_setup():
        import jax, jax.numpy as jnp
        import numpy as np
        B, S, D, H = (2, 512, 256, 16)
        DH = D // H

        def _rope(x):
            s, dh = (x.shape[2], x.shape[3])
            inv = jnp.exp(jnp.arange(0, dh, 2, dtype=jnp.float32) * (-(4.0 * jnp.log(jnp.float32(10.0))) / dh))
            pos = jnp.arange(s, dtype=jnp.float32)[:, None]
            sin = jnp.sin(pos * inv)
            cos = jnp.cos(pos * inv)
            x1 = x[..., 0::2]
            x2 = x[..., 1::2]
            out = jnp.stack([x1 * sin - x2 * cos, -x1 * cos - x2 * sin], axis=-1)
            return out.reshape(x.shape)
        key = jax.random.key(seed)
        ks = jax.random.split(key, 12)
        f = lambda k, sh: jax.random.normal(k, sh, dtype=jnp.float32)
        inp = {'q': f(ks[0], (B, S, D)), 'k': f(ks[1], (B, S, D)), 'v': f(ks[2], (B, S, D))}
        scale = 1.0 / np.sqrt(D)
        names = ['q', 'k', 'v', 'o']
        for i, n in enumerate(names):
            inp['W' + n] = f(ks[3 + i], (D, D)) * scale
            inp['b' + n] = f(ks[7 + i], (D,)) * scale
        inp['mask'] = jnp.triu(jnp.ones((S, S), dtype=bool), k=1)[None, None]
        return inp
    _L1_xattn_all = _L1_xattn_setup()
    _L1_xattn_in = {k: v for k, v in _L1_xattn_all.items() if k in ('Wq', 'bq', 'Wk', 'bk', 'Wv', 'bv', 'Wo', 'bo')}
    del _L1_xattn_all

    def _L1_ffn_setup():
        import jax, jax.numpy as jnp
        import numpy as np
        B, S, D = (4, 1024, 256)
        E, F_EXP = (16, 512)
        F_C = 2.0
        F_SH = 512
        key = jax.random.key(seed)
        ks = jax.random.split(key, 8)
        s = 0.02
        return {'hidden_states': jax.random.normal(ks[0], (B, S, D), jnp.float32), 'gate_w': jax.random.normal(ks[1], (E, D), jnp.float32) * s, 'Wg': jax.random.normal(ks[2], (E, F_EXP, D), jnp.float32) * s, 'Wu': jax.random.normal(ks[3], (E, F_EXP, D), jnp.float32) * s, 'Wd': jax.random.normal(ks[4], (E, D, F_EXP), jnp.float32) * s, 'Ws_g': jax.random.normal(ks[5], (F_SH, D), jnp.float32) * s, 'Ws_u': jax.random.normal(ks[6], (F_SH, D), jnp.float32) * s, 'Ws_d': jax.random.normal(ks[7], (D, F_SH), jnp.float32) * s}
    _L1_ffn_all = _L1_ffn_setup()
    _L1_ffn_in = {k: v for k, v in _L1_ffn_all.items() if k in ('gate_w', 'Wg', 'Wu', 'Wd', 'Ws_g', 'Ws_u', 'Ws_d')}
    del _L1_ffn_all
    return {'x': x, 'ctx_1024': ctx_1024, 'mask_1x1xSxS2_bk1': mask_1x1xSxS2_bk1, 'g_xattn': g_xattn, 'g_ffn': g_ffn, 'L0_xattn_Wq': _L0_xattn_in['Wq'], 'L0_xattn_bq': _L0_xattn_in['bq'], 'L0_xattn_Wk': _L0_xattn_in['Wk'], 'L0_xattn_bk': _L0_xattn_in['bk'], 'L0_xattn_Wv': _L0_xattn_in['Wv'], 'L0_xattn_bv': _L0_xattn_in['bv'], 'L0_xattn_Wp': _L0_xattn_in['Wp'], 'L0_xattn_bp': _L0_xattn_in['bp'], 'L0_ffn_input_patterns': _L0_ffn_in['input_patterns'], 'L0_ffn_process_input_weights': _L0_ffn_in['process_input_weights'], 'L0_ffn_process_values': _L0_ffn_in['process_values'], 'L0_ffn_output_input_weights': _L0_ffn_in['output_input_weights'], 'L0_ffn_output_patterns': _L0_ffn_in['output_patterns'], 'L1_xattn_Wq': _L1_xattn_in['Wq'], 'L1_xattn_bq': _L1_xattn_in['bq'], 'L1_xattn_Wk': _L1_xattn_in['Wk'], 'L1_xattn_bk': _L1_xattn_in['bk'], 'L1_xattn_Wv': _L1_xattn_in['Wv'], 'L1_xattn_bv': _L1_xattn_in['bv'], 'L1_xattn_Wo': _L1_xattn_in['Wo'], 'L1_xattn_bo': _L1_xattn_in['bo'], 'L1_ffn_gate_w': _L1_ffn_in['gate_w'], 'L1_ffn_Wg': _L1_ffn_in['Wg'], 'L1_ffn_Wu': _L1_ffn_in['Wu'], 'L1_ffn_Wd': _L1_ffn_in['Wd'], 'L1_ffn_Ws_g': _L1_ffn_in['Ws_g'], 'L1_ffn_Ws_u': _L1_ffn_in['Ws_u'], 'L1_ffn_Ws_d': _L1_ffn_in['Ws_d']}

def reference(x, ctx_1024, mask_1x1xSxS2_bk1, g_xattn, g_ffn, L0_xattn_Wq, L0_xattn_bq, L0_xattn_Wk, L0_xattn_bk, L0_xattn_Wv, L0_xattn_bv, L0_xattn_Wp, L0_xattn_bp, L0_ffn_input_patterns, L0_ffn_process_input_weights, L0_ffn_process_values, L0_ffn_output_input_weights, L0_ffn_output_patterns, L1_xattn_Wq, L1_xattn_bq, L1_xattn_Wk, L1_xattn_bk, L1_xattn_Wv, L1_xattn_bv, L1_xattn_Wo, L1_xattn_bo, L1_ffn_gate_w, L1_ffn_Wg, L1_ffn_Wu, L1_ffn_Wd, L1_ffn_Ws_g, L1_ffn_Ws_u, L1_ffn_Ws_d):
    import jax
    import jax.numpy as jnp

    def _L0_xattn_ref(x0, x1, x2, Wq, bq, Wk, bk, Wv, bv, Wp, bp):
        import jax, jax.numpy as jnp
        import numpy as np
        DIM = 256
        N_HEADS = 16
        HEAD_DIM = DIM // N_HEADS
        SCALE = HEAD_DIM ** (-0.5)
        B, S = (4, 512)

        def _split_heads(t):
            Bc, Sc, _ = t.shape
            return t.reshape(Bc, Sc, N_HEADS, HEAD_DIM).transpose(0, 2, 1, 3)
        q = _split_heads(x0 @ Wq.T + bq)
        k = _split_heads(x1 @ Wk.T + bk)
        v = _split_heads(x2 @ Wv.T + bv)
        dp = -SCALE * jnp.einsum('bhqd,bhkd->bhqk', q, k)
        attn = jax.nn.softmax(dp, axis=-1)
        out = jnp.einsum('bhqk,bhkd->bhqd', attn, v)
        out = out.transpose(0, 2, 1, 3).reshape(x0.shape[0], x0.shape[1], DIM)
        return out @ Wp.T + bp

    def _L0_ffn_ref(x, input_patterns, process_input_weights, process_values, output_input_weights, output_patterns):
        import jax, jax.numpy as jnp
        import numpy as np

        def gelu(x):
            return jax.nn.gelu(x, approximate=False)
        B, S, d_model = x.shape
        n_input = input_patterns.shape[0]
        n_process = process_input_weights.shape[0]
        n_output = output_input_weights.shape[0]
        k_input = max(n_input // 8, 64)
        k_process = max(n_process // 8, 32)
        k_output = max(n_output // 8, 64)
        input_acts = gelu(jnp.einsum('bsd,nd->bsn', x, input_patterns))
        input_acts_seq = input_acts.mean(axis=1)
        top_input_acts, top_input_idx = jax.lax.top_k(input_acts_seq, k_input)
        brow = jnp.arange(B)[:, None]
        input_repr = jnp.zeros((B, n_input), x.dtype).at[brow, top_input_idx].set(top_input_acts)
        process_acts = gelu(jnp.einsum('bn,pn->bp', input_repr, process_input_weights))
        top_process_acts, top_process_idx = jax.lax.top_k(process_acts, k_process)
        selected_process_values = process_values[top_process_idx]
        process_weights = jax.nn.softmax(top_process_acts, axis=-1)
        aggregated_value = jnp.einsum('bk,bkd->bd', process_weights, selected_process_values)
        output_acts_seq = gelu(jnp.einsum('bd,od->bo', aggregated_value, output_input_weights))
        top_output_acts, top_output_idx = jax.lax.top_k(output_acts_seq, k_output)
        selected_output_patterns = output_patterns[top_output_idx]
        out_per_seq = jnp.einsum('bk,bkm->bm', top_output_acts, selected_output_patterns)
        output = jnp.broadcast_to(out_per_seq[:, None, :], (B, S, d_model))
        return output

    def _L1_xattn_ref(q, k, v, Wq, bq, Wk, bk, Wv, bv, Wo, bo, mask):
        import jax, jax.numpy as jnp
        import numpy as np
        B, S, D, H = (2, 512, 256, 16)
        DH = D // H

        def _rope(x):
            s, dh = (x.shape[2], x.shape[3])
            inv = jnp.exp(jnp.arange(0, dh, 2, dtype=jnp.float32) * (-(4.0 * jnp.log(jnp.float32(10.0))) / dh))
            pos = jnp.arange(s, dtype=jnp.float32)[:, None]
            sin = jnp.sin(pos * inv)
            cos = jnp.cos(pos * inv)
            x1 = x[..., 0::2]
            x2 = x[..., 1::2]
            out = jnp.stack([x1 * sin - x2 * cos, -x1 * cos - x2 * sin], axis=-1)
            return out.reshape(x.shape)
        b, s, d = q.shape
        h, dh = (H, DH)

        def proj(x, W, bias):
            return (x @ W.T + bias).reshape(b, -1, h, dh).transpose(0, 2, 1, 3)
        Q = proj(q, Wq, bq)
        K = proj(k, Wk, bk)
        V = proj(v, Wv, bv)
        PQ = _rope(Q)
        PK = _rope(K)
        scores = jnp.einsum('bhqd,bhkd->bhqk', PQ, PK)
        neg = jnp.finfo(scores.dtype).min
        scores = jnp.where(mask, neg, scores)
        p = jax.nn.softmax(scores, axis=-1)
        p = jnp.where(mask, jnp.float32(0.0), p)
        out = jnp.einsum('bhqk,bhkd->bhqd', p, V)
        out = out.transpose(0, 2, 1, 3).reshape(b, s, d)
        return out @ Wo.T + bo

    def _L1_ffn_ref(hidden_states, gate_w, Wg, Wu, Wd, Ws_g, Ws_u, Ws_d):
        import jax, jax.numpy as jnp
        import numpy as np
        B, S, D = (4, 1024, 256)
        E, F_EXP = (16, 512)
        F_C = 2.0
        F_SH = 512
        b, s, d = hidden_states.shape
        e = gate_w.shape[0]
        cap = int(s * F_C / e)
        logits = jnp.einsum('bsd,ed->bse', hidden_states, gate_w)
        scores = jax.nn.softmax(logits, axis=-1).transpose(0, 2, 1)
        topk_w, topk_idx = jax.lax.top_k(scores, cap)
        x_tok = jnp.take_along_axis(hidden_states[:, None, :, :], topk_idx[..., None], axis=2)
        g = jnp.einsum('becd,efd->becf', x_tok, Wg)
        u = jnp.einsum('becd,efd->becf', x_tok, Wu)
        h = jax.nn.gelu(g, approximate=False) * u
        eo = jnp.einsum('becf,edf->becd', h, Wd) * topk_w[..., None]
        offs = (jnp.arange(b) * s)[:, None, None]
        flat_idx = (topk_idx + offs).reshape(-1)
        flat = jnp.zeros((b * s, d), hidden_states.dtype)
        flat = flat.at[flat_idx].add(eo.reshape(-1, d))
        out = flat.reshape(b, s, d)
        gs = jnp.einsum('bsd,fd->bsf', hidden_states, Ws_g)
        us = jnp.einsum('bsd,fd->bsf', hidden_states, Ws_u)
        shared = jnp.einsum('bsf,df->bsd', jax.nn.gelu(gs, approximate=False) * us, Ws_d)
        return out + shared
    x = x + jnp.tanh(g_xattn[0]) * _L0_xattn_ref(_layernorm(x, axis=-1), ctx_1024, ctx_1024, L0_xattn_Wq, L0_xattn_bq, L0_xattn_Wk, L0_xattn_bk, L0_xattn_Wv, L0_xattn_bv, L0_xattn_Wp, L0_xattn_bp)
    x = x + jnp.tanh(g_ffn[0]) * _L0_ffn_ref(_layernorm(x, axis=-1), L0_ffn_input_patterns, L0_ffn_process_input_weights, L0_ffn_process_values, L0_ffn_output_input_weights, L0_ffn_output_patterns)
    x = x + jnp.tanh(g_xattn[1]) * _L1_xattn_ref(_layernorm(x, axis=-1), ctx_1024, ctx_1024, L1_xattn_Wq, L1_xattn_bq, L1_xattn_Wk, L1_xattn_bk, L1_xattn_Wv, L1_xattn_bv, L1_xattn_Wo, L1_xattn_bo, mask_1x1xSxS2_bk1)
    x = x + jnp.tanh(g_ffn[1]) * _L1_ffn_ref(_layernorm(x, axis=-1), L1_ffn_gate_w, L1_ffn_Wg, L1_ffn_Wu, L1_ffn_Wd, L1_ffn_Ws_g, L1_ffn_Ws_u, L1_ffn_Ws_d)
    return x

_drawn_inputs = setup_inputs


def setup_inputs(seed=0):
    import zlib

    import numpy as np

    out = dict(_drawn_inputs(seed))
    spreads = {'g_ffn': (-1.0, 0.6)}
    factors = {'L0_xattn_Wq': 8.0,
     'L0_xattn_bq': 8.0,
     'L0_xattn_Wk': 8.0,
     'L0_xattn_bk': 8.0,
     'L0_xattn_bv': 8.0,
     'L0_xattn_bp': 3.948,
     'L0_ffn_input_patterns': 8.0,
     'L0_ffn_process_input_weights': 8.0,
     'L0_ffn_process_values': 8.0,
     'L0_ffn_output_input_weights': 8.0,
     'L0_ffn_output_patterns': 8.0,
     'L1_xattn_bk': 5.376,
     'L1_ffn_gate_w': 8.0,
     'L1_ffn_Wg': 8.0,
     'L1_ffn_Wu': 8.0,
     'L1_ffn_Wd': 8.0,
     'L1_ffn_Ws_g': 3.676,
     'L1_ffn_Ws_u': 3.583,
     'L1_ffn_Ws_d': 3.601}
    for name, (base, spread) in spreads.items():
        noise = np.random.default_rng([zlib.crc32(name.encode()), seed]).standard_normal(out[name].shape)
        drawn = base * np.exp(spread * noise) if base else spread * noise
        out[name] = jnp.asarray(drawn.astype(out[name].dtype))
    for name, factor in factors.items():
        out[name] = (out[name] * factor).astype(out[name].dtype)
    return out
```

```python
from contextlib import ExitStack

import concourse.bass as bass
from concourse import mybir
from concourse.alu_op_type import AluOpType as ALU

ACT = mybir.ActivationFunctionType
AX = mybir.AxisListType.X
F32 = mybir.dt.float32
BF16 = mybir.dt.bfloat16
U16 = mybir.dt.uint16
U8 = mybir.dt.uint8
U32 = mybir.dt.uint32

P = 128
B, S, D = 8, 256, 256
T = B * S
DC = D // P
H, HD, SK = 16, 16, 77
NG, GH = 3, 6
GR = GH * HD
KB = B * SK
NI, NP_, NO, DV = 2048, 1024, 2048, 128
TOP_I, TOP_P, TOP_O = NI // 8, NP_ // 8, NO // 8
E, F, CAP = 16, 512, 32
FC = F // P
EPS = 1e-5
MASKED = -float(2.0 ** 100)

C_ID, C_ONE, C_TRI, C_PAR, C_PW, C_SEL, C_IOTA, C_HM, C_PERM, C_GATE, C_END = (
    0, 128, 256, 384, 448, 464, 472, 504, 510, 606, 610)


def flamingo_kernel(nc, x_d, ctx_d, gates_d, mask_d, maskT_d, const_d, kone_d,
                    ropeA_d, ropeB_d, attn_d, pat_d, piw_d,
                    pv_d, oiw_d, op_d, gate_d, wg_d, wu_d, wd_d, sg_d, su_d, sd_d, out_d):
    with ExitStack() as ctx:
        def sem(name):
            return ctx.enter_context(nc.semaphore(name))

        def region(name, cols):
            whole = ctx.enter_context(nc.sbuf_tensor(name, [P, cols], F32))
            at = [0]

            def take(n, start=None):
                lo = at[0] if start is None else start
                at[0] = lo + n
                assert at[0] <= cols, (name, at[0], cols)
                return whole[:, lo:lo + n]
            return take

        keep = region("keep", 13700)
        x_sb = keep(T // P * D).rearrange("p (t d) -> p t d", d=D)
        xnT_s = keep(DC * T)
        xnT = xnT_s.rearrange("p (c t) -> p c t", c=DC)
        qT = xnT_s[:, 0:2 * NG * S].rearrange("p (s g q) -> p s g q", s=2, g=NG)
        qraw = xnT_s[:, 1536:2304].rearrange("p (g q) -> p g q", g=NG)
        qrot = xnT_s[:, 2304:3072].rearrange("p (g q) -> p g q", g=NG)
        pcp = xnT_s[:, 3072:3072 + NP_]
        xn_s = keep(2 * 2 * D)
        xn = xn_s.rearrange("p (s t d) -> p s t d", s=2, d=D)
        xnT_b = keep(DC * S).rearrange("p (c t) -> p c t", c=DC)
        cst = keep(C_END)
        ident, onesf = cst[:, C_ID:C_ONE], cst[:, C_ONE:C_TRI]
        par = cst[:, C_PAR:C_PW].rearrange("p (a m) -> p a m", a=2)
        pw, sel8, iota = cst[:, C_PW:C_SEL], cst[:, C_SEL:C_IOTA], cst[:, C_IOTA:C_HM]
        hmask, perm, gates = cst[:, C_HM:C_PERM], cst[:, C_PERM:C_GATE], cst[:, C_GATE:C_END]
        tg = keep(4)
        bn = keep(2 * 6).rearrange("p (t k) -> p t k", k=6)
        mv = keep(2 * 2).rearrange("p (t k) -> p t k", k=2)
        scrap, veps, rstd, mhalf, eps = keep(1), keep(2), keep(2), keep(2), keep(2)
        ones_b = keep(64).bitcast(BF16)
        tri_b = keep(64).bitcast(BF16)
        ident_b = keep(64).bitcast(BF16)
        bqs = keep(NG)
        acts = keep(128)
        tk = keep(8 * 128)
        key, khi, klo, neg, sgn, tmp, gtm, selm = (tk[:, 128 * j:128 * j + 128] for j in range(8))
        rden, ytmp = tk[:, 0:512], tk[:, 512:1024]
        cmpb, eqb = keep(64).bitcast(BF16), keep(64).bitcast(BF16)
        cntb = keep(4).bitcast(BF16)
        thr, ge, need, pmax, mx8, mxd, rs8, dsum = (keep(8) for _ in range(8))
        wpad_s = keep(512)
        wpad = wpad_s.rearrange("p (c m) -> p c m", m=32)
        outp = keep(D)
        aggT = keep(8)
        mask_w, maskT_w = keep(2 * 20).bitcast(U32), keep(64).bitcast(U32)
        mask_u, maskT_u = mask_w.bitcast(U8).rearrange("p (t k) -> p t k", t=2), maskT_w.bitcast(U8)
        maskb = keep(80).bitcast(BF16).rearrange("p (t k) -> p t k", t=2)
        maskTb = keep(128).bitcast(BF16)
        seen = keep(128).bitcast(BF16)
        anyv = keep(S)
        gate = keep(DC * E).rearrange("p (c e) -> p c e", c=DC)

        big = region("big", 19456)
        piw = big(16 * NP_).rearrange("p (c n) -> p c n", c=16)
        pvt = big(8 * DV).rearrange("p (c n) -> p c n", c=8)
        oiw = big(NO)
        opt = big(16 * D, 0).rearrange("p (c n) -> p c n", c=16)
        kraw = big(NG * KB, 0).rearrange("p (g n) -> p g n", g=NG)
        XT = big(E * DC * S, 2048).rearrange("p (e c t) -> p e c t", e=E, c=DC)
        EO = big(4 * B * D, 0).rearrange("p (g b d) -> p g b d", g=4, b=B)
        xn_all = big(T // P * D, 10240).rearrange("p (t d) -> p t d", d=D)
        sw = big(3072)
        hT = big(2 * FC * S).rearrange("p (s f n) -> p s f n", s=2, f=FC)

        vp = region("vp", 8192)
        V = vp(B * D).rearrange("p (b d) -> p b d", b=B)
        Vpad = vp(2 * H * 32).rearrange("p (s h m) -> p s h m", s=2, h=H)
        PT = vp(H * S).rearrange("p (h q) -> p h q", h=H)
        mpad_s = vp(2 * NG * P)
        mpad = mpad_s.rearrange("p (t g m) -> p t g m", t=2, g=NG)
        GWT = vp(B * 4 * S, 0).rearrange("p (b g t) -> p b g t", b=B, g=4)

        att = region("att", 10600)
        awt = att(2176 + 518)
        wq = awt[:, 0:576].rearrange("p (c g m) -> p c g m", c=DC, g=NG)
        wk = awt[:, 576:1152].rearrange("p (c g m) -> p c g m", c=DC, g=NG)
        wv = awt[:, 1152:1664].rearrange("p (c m) -> p c m", c=DC)
        wp = awt[:, 1664:2176].rearrange("p (c m) -> p c m", c=DC)
        bv, bp, bq, bk = awt[:, 2176:2432], awt[:, 2432:2688], awt[:, 2688:2691], awt[:, 2691:2694]
        ctxT = att(DC * KB).rearrange("p (c n) -> p c n", c=DC)
        kT = att(NG * KB).rearrange("p (g n) -> p g n", g=NG)
        kbd = att(2 * NG * GH * SK).rearrange("p (s h k) -> p s h k", s=2, k=SK)
        rope = att(2 * S)
        ropeA, ropeB = rope[:, 0:S], rope[:, S:2 * S]
        attnT = att(DC * S).rearrange("p (c q) -> p c q", c=DC)
        pat = att(1024).rearrange("p (s j c n) -> p s j c n", s=2, j=2, c=DC)
        ew = att(2 * 3072, 0)
        hgl = att(2 * 512).rearrange("p (f n) -> p f n", f=2)
        eo = att(2 * 2 * D).rearrange("p (s t d) -> p s t d", s=2, d=D)
        GW = att(1024).rearrange("p (t n) -> p t n", t=2)
        G = xn_s.rearrange("p (t n) -> p t n", t=2)
        probs, sc2_s, work, posm = (tk[:, 256 * j:256 * j + 256] for j in range(4))
        sc2 = sc2_s.rearrange("p (t m) -> p t m", t=2)
        posT = wpad_s[:, 0:256].rearrange("p (t m) -> p t m", t=2)
        cum = wpad_s[:, 256:512]

        ps = ctx.enter_context(nc.psum_tensor("ps", [P, 8, 512], F32))
        ps_all = ps[:, :, :]

        def weights(base):
            return (base[:, 0:1024].rearrange("p (c f) -> p c f", c=DC),
                    base[:, 1024:2048].rearrange("p (c f) -> p c f", c=DC),
                    base[:, 2048:3072].rearrange("p (f d) -> p f d", f=FC))

        expert_w = [weights(ew[:, 3072 * s:3072 * s + 3072]) for s in range(2)]
        shared_w = weights(sw)

        x_in, const_in, attn_in, mask_in = sem("x_in"), sem("const_in"), sem("attn_in"), sem("mask_in")
        kone_in, pat_in = sem("kone_in"), [sem("pat_in0"), sem("pat_in1")]
        piw_in, op_in, gate_in, sw_in = sem("piw_in"), sem("op_in"), sem("gate_in"), sem("sw_in")
        ew_in = [sem("ew_in0"), sem("ew_in1")]
        eo_moved = [sem("eo_moved0"), sem("eo_moved1")]
        out_done = sem("out_done")
        cleared, prepared, tanh_done, bqs_done = sem("cleared"), sem("prepared"), sem("tanh_done"), sem("bqs_done")
        stat_done, mv_done, veps_done, rstd_done = sem("stat_done"), sem("mv_done"), sem("veps_done"), sem("rstd_done")
        xn_done, xt_ps, xt_done = sem("xn_done"), sem("xt_ps"), sem("xt_done")
        k_ps, k_raw, k_perm, k_mulA, k_mulB, kT_done = (sem("k_ps"), sem("k_raw"), sem("k_perm"), sem("k_mulA"),
                                                        sem("k_mulB"), sem("kT_done"))
        v_ps, v_done = sem("v_ps"), sem("v_done")
        q_ps, q_raw, q_perm, q_mulA, q_mulB, q_done = (sem("q_ps"), sem("q_raw"), sem("q_perm"), sem("q_mulA"),
                                                       sem("q_mulB"), sem("q_done"))
        kbd_done, rowmax_ps, rowmax_done = sem("kbd_done"), sem("rowmax_ps"), sem("rowmax_done")
        mT_ps, mT_done, score_ps, exp_done, pv_ps = (sem("mT_ps"), sem("mT_done"), sem("score_ps"), sem("exp_done"),
                                                     sem("pv_ps"))
        rden_done, attn_done, proj_ps, bias_done, x_done = (sem("rden_done"), sem("attn_done"), sem("proj_ps"),
                                                            sem("bias_done"), sem("x_done"))
        any_ps, any_done = sem("any_ps"), sem("any_done")
        ia_ps, ia_done = sem("ia_ps"), [sem(f"ia_done{j}") for j in range(4)]
        tk_step, tk_cnt, tk_tot = sem("tk_step"), sem("tk_cnt"), sem("tk_tot")
        pr_ps, pr_copied, pr_cols, pa_done = sem("pr_ps"), sem("pr_copied"), sem("pr_cols"), sem("pa_done")
        sm_dve, sm_pe, sm_act = sem("sm_dve"), sem("sm_pe"), sem("sm_act")
        agg_ps, agg_done, oa_ps, oa_done = sem("agg_ps"), sem("agg_done"), sem("oa_ps"), sem("oa_done")
        op_ps, op_copied, op_rows, x2_done = sem("op_ps"), sem("op_copied"), sem("op_rows"), sem("x2_done")
        rt_dve, rt_pe, rt_act = sem("rt_dve"), sem("rt_pe"), sem("rt_act")
        g_done, gw_done, disp_ps, disp_done = sem("g_done"), sem("gw_done"), sem("disp_ps"), sem("disp_done")
        gwt_ps, gwt_done = sem("gwt_ps"), sem("gwt_done")
        gu_ps, gelu_done, h_done, down_ps, down_done = (sem("gu_ps"), sem("gelu_done"), sem("h_done"),
                                                        sem("down_ps"), sem("down_done"))
        comb_ps, y_done = sem("comb_ps"), sem("y_done")

        block = ctx.enter_context(nc.Block())

        def bslice(b):
            return bass.ds(b * S, S)

        def ktslice(b):
            return bass.ds(b * SK, SK)

        def tiles(b):
            return bass.ds(b * 2, 2)

        def steps(eng, layer, step):
            step(8 * layer, 0, 0, True, False)
            with eng.Fori(0, (B - 2) // 2) as t:
                for j in range(2):
                    b = t * 2 + (1 + j)
                    step(b + 8 * layer, b, (1 + j) % 2, False, False)
            step(8 * layer + B - 1, B - 1, (B - 1) % 2, False, True)

        @block.sync
        def _(sp):
            sp.dma_start(x_sb[:, 0:4, :], x_d.rearrange("(t p) d -> p t d", p=P)[:, 0:4, :]).then_inc(x_in, 16)
            sp.dma_start(cst[:, 0:C_GATE], const_d).then_inc(const_in, 16)
            sp.dma_start(gates, gates_d).then_inc(const_in, 16)
            sp.dma_start(awt, attn_d[0, :, 0:2694]).then_inc(attn_in, 16)
            sp.dma_start(ctxT, ctx_d).then_inc(attn_in, 16)
            for s in range(2):
                sp.dma_start(kbd[GR:P, s, :, :], kone_d).then_inc(kone_in, 16)
            sp.dma_start(x_sb[:, 4:16, :], x_d.rearrange("(t p) d -> p t d", p=P)[:, 4:16, :]).then_inc(x_in, 16)
            sp.dma_start(mask_w, mask_d.rearrange("p t k -> p (t k)")).then_inc(mask_in, 16)
            sp.dma_start(maskT_w, maskT_d).then_inc(mask_in, 16)
            sp.dma_start(ropeA[0:GR, :], ropeA_d).then_inc(mask_in, 16)
            sp.dma_start(ropeB[0:GR, :], ropeB_d).then_inc(mask_in, 16)
            for s in range(2):
                sp.dma_start(pat[:, s], pat_d[s]).then_inc(pat_in[s], 16)
            sp.dma_start(piw, piw_d).then_inc(piw_in, 16)
            sp.dma_start(pvt, pv_d).then_inc(piw_in, 16)
            sp.dma_start(oiw, oiw_d).then_inc(piw_in, 16)
            sp.wait_ge(proj_ps, B)
            sp.wait_ge(x_done, B)
            sp.dma_start(awt, attn_d[1, :, 0:2694]).then_inc(attn_in, 16)
            sp.dma_start(gate, gate_d).then_inc(gate_in, 16)
            with sp.Fori(1, 4) as t:
                for s in range(2):
                    sp.wait_ge(ia_ps, t * 16 + (8 * s - 8))
                    sp.dma_start(pat[:, s], pat_d[t * 2 + s]).then_inc(pat_in[s], 16)
            sp.wait_ge(pr_ps, 1)
            sp.dma_start(opt, op_d).then_inc(op_in, 16)
            sp.wait_ge(x_done, 2 * B)
            for w, d in zip(shared_w, (sg_d, su_d, sd_d)):
                sp.dma_start(w, d).then_inc(sw_in, 16)
            for e in range(2):
                for w, d in zip(expert_w[e], (wg_d, wu_d, wd_d)):
                    sp.dma_start(w, d[e]).then_inc(ew_in[e], 16)

            def expert_traffic(t, q, load):
                s = q % 2
                if load:
                    sp.wait_ge(down_ps, t * 4 + (B + q + 1))
                    for w, d in zip(expert_w[s], (wg_d, wu_d, wd_d)):
                        sp.dma_start(w, d[t * 4 + (q + 2)]).then_inc(ew_in[s], 16)
                sp.wait_ge(down_done, t * 4 + (B + q + 1))
                for g in range(4):
                    sp.dma_start(EO[32 * q:32 * q + 32, t, g::4, :], eo[32 * g:32 * g + 32, s, :, :]
                                 ).then_inc(eo_moved[s], 16)

            with sp.Fori(0, 3) as t:
                for q in range(4):
                    expert_traffic(t, q, True)
            for q in range(4):
                expert_traffic(3, q, q < 2)
            for b in range(B):
                sp.wait_ge(y_done, b + 1)
                sp.dma_start(out_d.rearrange("(t p) d -> p t d", p=P)[:, 2 * b:2 * b + 2, :],
                             x_sb[:, 2 * b:2 * b + 2, :]).then_inc(out_done, 16)
            sp.wait_ge(out_done, 16 * B)

        @block.gpsimd
        def _(pool):
            pool.memset(mhalf, -0.5).then_inc(cleared, 1)
            pool.memset(eps, EPS).then_inc(cleared, 1)
            pool.memset(mpad_s, 0.0).then_inc(cleared, 1)
            pool.memset(Vpad.rearrange("p s h m -> p (s h m)"), 0.0).then_inc(cleared, 1)
            pool.memset(PT.rearrange("p h q -> p (h q)"), 0.0).then_inc(cleared, 1)
            pool.memset(kbd[0:GR].rearrange("p s h k -> p (s h k)"), 0.0).then_inc(cleared, 1)
            pool.memset(wpad_s, 0.0).then_inc(cleared, 1)

            def inv_std(n):
                pool.wait_ge(mv_done, n * 2 + 2)
                pool.tensor_tensor(veps, mv[:, :, 1], eps, ALU.add).then_inc(veps_done, 1)
                pool.wait_ge(veps_done, n + 1)
                pool.tensor_tensor(rstd, veps, mhalf, ALU.pow).then_inc(rstd_done, 1)

            def block_keys(i, b, s, free):
                if not free:
                    pool.wait_ge(pv_ps, i - 1)
                for g in range(NG):
                    ins = pool.tensor_tensor(
                        kbd[0:GR, s, GH * g:GH * g + GH, :],
                        kT[0:GR, g, ktslice(b)].unsqueeze(1).to_broadcast([GR, GH, SK]),
                        hmask[0:GR, :].unsqueeze(2).to_broadcast([GR, GH, SK]), ALU.mult)
                for a in range(2):
                    ins = pool.tensor_copy(
                        Vpad[0:SK, s].rearrange("p (h a) m -> p h a m", a=2)[:, :, a, HD * a:HD * a + HD],
                        V[0:SK, bass.ds(b, 1), :].rearrange("p o (h a m) -> p (o h) a m", a=2, m=HD)[:, :, a, :])
                ins.then_inc(kbd_done, 1)

            def rotary_a(b):
                pool.wait_ge(q_raw, b + 1)
                pool.tensor_tensor(qrot[0:GR], qraw[0:GR], ropeA[0:GR].unsqueeze(1).to_broadcast([GR, NG, S]),
                                   ALU.mult).then_inc(q_mulA, 1)

            pool.wait_ge(cleared, 7)
            for layer in range(2):
                inv_std(16 * layer)
                if layer == 0:
                    pool.wait_ge(const_in, 32)
                if layer == 1:
                    for j in range(6):
                        g, nh = divmod(j, 2)
                        pool.wait_ge(k_raw, j + 1)
                        pool.tensor_tensor(
                            kT[0:GR, g, 308 * nh:308 * nh + 308].rearrange("p (b k) -> p b k", k=SK),
                            kraw[0:GR, g, 308 * nh:308 * nh + 308].rearrange("p (b k) -> p b k", k=SK),
                            ropeA[0:GR, 0:SK].unsqueeze(1).to_broadcast([GR, 4, SK]), ALU.mult).then_inc(k_mulA, 1)
                pool.wait_ge(kT_done, 6 * (layer + 1))
                pool.wait_ge(v_done, B * (layer + 1))
                block_keys(8 * layer, 0, 0, layer == 0)
                if layer == 1:
                    rotary_a(0)

                def step(i, b, s, first, last, layer=layer):
                    if last:
                        return
                    inv_std(i + (8 * layer + 1))
                    block_keys(i + 1, b + 1, 1 - s, first and layer == 0)
                    if layer == 1:
                        rotary_a(b + 1)
                steps(pool, layer, step)
                with pool.Fori(0, B) as b:
                    inv_std(b + (16 * layer + 8))

        @block.scalar
        def _(act):
            act.wait_ge(const_in, 32)
            act.activation(tg, gates, ACT.Tanh).then_inc(tanh_done, 1)

            def copy_xt(n, out, bank=2):
                act.wait_ge(xt_ps, n + 1)
                act.activation(out, ps[:, bank, :].rearrange("p (c t) -> p c t", c=DC), ACT.Copy
                               ).then_inc(xt_done, 1)

            def q_out(i, s, layer):
                act.wait_ge(q_ps, i + 1)
                if layer == 0:
                    act.wait_ge(bqs_done, 1)
                for g in range(NG):
                    src = ps[0:GR, 1 + g // 2, S * (g % 2):S * (g % 2) + S]
                    if layer == 0:
                        ins = act.activation(qT[0:GR, s, g, :], src, ACT.Identity, bias=bqs[0:GR, g:g + 1],
                                             scale=-0.25)
                    else:
                        ins = act.activation(qraw[0:GR, g, :], src, ACT.Identity, bias=bq[0:GR, g:g + 1], scale=1.0)
                ins.then_inc(q_done if layer == 0 else q_raw, 1)

            for layer in range(2):
                act.wait_ge(attn_in, 32 + 16 * layer)
                for j in range(6):
                    g, nh = divmod(j, 2)
                    act.wait_ge(k_ps, 6 * layer + j + 1)
                    dst = (kT if layer == 0 else kraw)[0:GR, g, 308 * nh:308 * nh + 308]
                    act.activation(dst, ps[0:GR, 1 + j, 0:308], ACT.Identity, bias=bk[0:GR, g:g + 1], scale=1.0
                                   ).then_inc(kT_done if layer == 0 else k_raw, 1)
                copy_xt(16 * layer, xnT_b)
                q_out(8 * layer, 0, layer)

                def step(i, b, s, first, last, layer=layer):
                    if not last:
                        copy_xt(i + (8 * layer + 1), xnT_b)
                    for t in range(2):
                        act.wait_ge(mT_ps, i * 2 + (t + 1))
                        act.activation(qT[GR:P, s, :, P * t:P * t + P],
                                       ps[GR:P, 3 + t, 0:NG * P].rearrange("p (g q) -> p g q", g=NG), ACT.Copy
                                       ).then_inc(mT_done, 1)
                    if not last:
                        q_out(i + 1, 1 - s, layer)
                    for k in range(4):
                        act.wait_ge(score_ps, i * 4 + (k + 1))
                        a = 3 + 2 * (k % 2)
                        act.activation(PT[0:SK, 4 * k:4 * k + 4, :],
                                       ps[0:SK, a:a + 2, :].rearrange("p a (h q) -> p (a h) q", h=2), ACT.Exp
                                       ).then_inc(exp_done, 1)
                steps(act, layer, step)

                if layer == 1:
                    break
                with act.Fori(0, B // 2) as t:
                    for j in range(2):
                        b = t * 2 + j
                        copy_xt(b + 8, xnT[:, :, bslice(b)], bank=1 + j)
                with act.Fori(0, 4) as t:
                    for u in range(4):
                        for g in range(4):
                            ch = t * 4 + u
                            act.wait_ge(ia_ps, t * 16 + (4 * u + g + 1))
                            for h in range(2):
                                part = ps[:, 3 + g, S * h:S * h + S]
                                ins = act.activation(part, part, ACT.Gelu,
                                                     accum_out=acts[:, bass.ds(ch * 8 + (2 * g + h), 1)])
                            ins.then_inc(ia_done[g], 1)
                act.wait_ge(pr_ps, 1)
                act.activation(pcp, ps[:, 2:4, :].rearrange("p a n -> p (a n)"), ACT.Copy).then_inc(pr_copied, 1)
                act.wait_ge(pr_cols, 1)
                act.activation(acts[:, 0:64], ps[:, 4, 0:64], ACT.Gelu).then_inc(pa_done, 1)
                act.wait_ge(sm_dve, 5)
                act.activation(gtm[:, 0:64], gtm[:, 0:64], ACT.Exp).then_inc(sm_act, 1)
                act.wait_ge(oa_ps, 1)
                act.activation(acts, ps[:, 4, 0:128], ACT.Gelu).then_inc(oa_done, 1)
                act.wait_ge(op_ps, 1)
                act.activation(outp, ps[:, 5, 0:D], ACT.Copy).then_inc(op_copied, 1)

            for b in range(B):
                copy_xt(24 + b, xnT[:, :, bslice(b)], bank=1 + b % 2)
            act.wait_ge(rt_dve, 2)
            act.activation(probs, probs, ACT.Exp).then_inc(rt_act, 1)
            for b in range(B):
                for c in range(DC):
                    act.wait_ge(disp_ps, DC * b + c + 1)
                    act.activation(XT[:, :, c, 32 * b:32 * b + 32],
                                   ps[:, c, :].rearrange("p (e s) -> p e s", e=E), ACT.Copy).then_inc(disp_done, 1)
                act.wait_ge(gwt_ps, b + 1)
                act.activation(GWT[:, b].rearrange("p g t -> p (g t)"),
                               ps[:, 2:4, :].rearrange("p a n -> p (a n)"), ACT.Copy
                               ).then_inc(gwt_done, 1)

            def gelus(u):
                for f in range(2):
                    act.wait_ge(gu_ps, u * 2 + (f + 1))
                    act.activation(hgl[:, f, :], ps[:, 2 * f, :], ACT.Gelu).then_inc(gelu_done, 1)

            def expert_out(u, s, reused):
                act.wait_ge(down_ps, u + 1)
                if reused is not None:
                    act.wait_ge(eo_moved[s], reused)
                act.activation(eo[:, s], ps[:, 4 + s, :].rearrange("p (t d) -> p t d", t=2), ACT.Copy
                               ).then_inc(down_done, 1)

            with act.Fori(0, B) as b:
                gelus(b)

            def four_experts(t, first):
                for q in range(4):
                    u = t * 4 + (B + q)
                    gelus(u)
                    if q > 0:
                        expert_out(u - 1, (q - 1) % 2, None if first and q < 3 else t * 128 + 64 * ((q - 1) // 2))
                expert_out(u, 1, t * 128 + 64)

            four_experts(0, True)
            with act.Fori(1, 4) as t:
                four_experts(t, False)

        @block.tensor
        def _(pe):
            def mm(out, lhsT, rhs, start=True, stop=True):
                return pe.matmul(out, lhsT, rhs, start=start, stop=stop, skip_group_check=True)

            def transpose_xn(n, src, bank=2):
                pe.wait_ge(xn_done, n * 2 + 2)
                for c in range(DC):
                    for t in range(2):
                        at = (c * 2 + t) * P
                        ins = pe.transpose(ps[:, bank, at:at + P], src[:, t, P * c:P * c + P], ident)
                ins.then_inc(xt_ps, 1)

            def project_q(i, n):
                pe.wait_ge(xt_done, n + 1)
                for g in range(NG):
                    out = ps[0:GR, 1 + g // 2, S * (g % 2):S * (g % 2) + S]
                    for c in range(DC):
                        ins = mm(out, wq[:, c, g, :], xnT_b[:, c, :], c == 0, c == DC - 1)
                ins.then_inc(q_ps, 1)

            def swap_pairs(b):
                pe.wait_ge(q_raw, b + 1)
                for g in range(NG):
                    ins = mm(ps[0:GR, 1 + g // 2, S * (g % 2):S * (g % 2) + S], perm[0:GR, :], qraw[0:GR, g, :])
                ins.then_inc(q_perm, 1)

            def project_out(i):
                pe.wait_ge(attn_done, i + 1)
                for t in range(2):
                    for c in range(DC):
                        ins = mm(ps[:, 1, D * t:D * t + D], attnT[:, c, P * t:P * t + P], wp[:, c, :],
                                 c == 0, c == DC - 1)
                ins.then_inc(proj_ps, 1)

            pe.wait_ge(const_in, 32)
            for layer in range(2):
                pe.wait_ge(attn_in, 32 + 16 * layer)
                if layer == 1:
                    pe.wait_ge(x2_done, B)
                for j in range(6):
                    g, nh = divmod(j, 2)
                    for c in range(DC):
                        ins = mm(ps[0:GR, 1 + j, 0:308], wk[:, c, g, :], ctxT[:, c, 308 * nh:308 * nh + 308],
                                 c == 0, c == DC - 1)
                    ins.then_inc(k_ps, 1)
                for b in range(B):
                    bank = 7 if b % 2 == 0 else 0
                    if b >= 2:
                        pe.wait_ge(v_done, 8 * layer + b - 1)
                    for c in range(DC):
                        ins = mm(ps[0:SK, bank, 0:D], ctxT[:, c, SK * b:SK * b + SK], wv[:, c, :],
                                 c == 0, c == DC - 1)
                    ins.then_inc(v_ps, 1)
                if layer == 1:
                    for j in range(6):
                        g, nh = divmod(j, 2)
                        pe.wait_ge(k_raw, j + 1)
                        mm(ps[0:GR, 1 + j, 0:308], perm[0:GR, :], kraw[0:GR, g, 308 * nh:308 * nh + 308]
                           ).then_inc(k_perm, 1)
                    pe.wait_ge(prepared, 6)
                    pe.wait_ge(v_done, 8 * layer + 7)
                    mm(ps[:, 7, 0:S], ones_b[0:SK, :], seen[0:SK, :]).then_inc(any_ps, 1)
                    pe.wait_ge(any_done, 1)
                pe.wait_ge(kT_done, 6 * (layer + 1))
                transpose_xn(16 * layer, xn[:, 0])
                project_q(8 * layer, 16 * layer)
                if layer == 1:
                    swap_pairs(0)
                pe.wait_ge(v_done, 8 * layer + 8)
                pe.wait_ge(prepared, 6)
                pe.wait_ge(kone_in, 32)
                pe.wait_ge(cleared, 7)

                def step(i, b, s, first, last, layer=layer):
                    n = i + 8 * layer

                    def row_scores(t):
                        for g in range(NG):
                            bank = (3, 4, 5)[g] if t == 0 else (6, 7, 0)[g]
                            out = ps[:, bank, 0:GH * SK]
                            ins = mm(out, qT[0:GR, s, g, P * t:P * t + P],
                                     kbd[0:GR, s, GH * g:GH * g + GH, :].rearrange("p h k -> p (h k)"),
                                     True, layer == 0)
                            if layer == 1:
                                ins = mm(out.rearrange("p (h k) -> p h k", k=SK), ident_b,
                                         maskb[:, t, 0:SK].unsqueeze(1).to_broadcast([P, GH, SK]), False, True)
                        ins.then_inc(rowmax_ps, 1)

                    pe.wait_ge(q_done, i + 1)
                    pe.wait_ge(kbd_done, i + 1)
                    row_scores(0)
                    if not first:
                        project_out(i - 1)
                    row_scores(1)
                    if not last:
                        transpose_xn(n + 1, xn[:, 1 - s])
                    for t in range(2):
                        pe.wait_ge(rowmax_done, i * 2 + (t + 1))
                        for g in range(NG):
                            ins = pe.transpose(ps[:, 3 + t, P * g:P * g + P], mpad[:, t, g, :], ident)
                        ins.then_inc(mT_ps, 1)
                    if not last:
                        if not first:
                            pe.wait_ge(x_done, i)
                        project_q(i + 1, n + 1)

                    def key_scores(k):
                        for m in range(4):
                            h = 4 * k + m
                            out = ps[0:SK, 3 + 2 * (k % 2) + m // 2, S * (m % 2):S * (m % 2) + S]
                            ins = mm(out, kbd[:, s, h, :], qT[:, s, h // GH, :], True, layer == 0)
                            if layer == 1:
                                ins = mm(out, ident_b[:, 0:SK], maskTb, False, True)
                        ins.then_inc(score_ps, 1)

                    pe.wait_ge(mT_done, i * 2 + 2)
                    key_scores(0)
                    key_scores(1)
                    pe.wait_ge(exp_done, i * 4 + 1)
                    key_scores(2)
                    if layer == 1 and not last:
                        swap_pairs(b + 1)
                    pe.wait_ge(exp_done, i * 4 + 2)
                    key_scores(3)
                    for c in range(DC):
                        pe.wait_ge(exp_done, i * 4 + (2 * c + 2))
                        for a in range(2):
                            for bank, den in ((7, False), (0, True)):
                                for j in range(4):
                                    h = 8 * c + 2 * j + a
                                    lhsT = par[:, a, :] if den else Vpad[:, s, h, :]
                                    ins = mm(ps[32 * j:32 * j + 32, bank, S * c:S * c + S], lhsT, PT[:, h, :],
                                             a == 0, a == 1)
                    ins.then_inc(pv_ps, 1)
                    if last:
                        project_out(i)
                steps(pe, layer, step)
                if layer == 1:
                    break

                with pe.Fori(0, B // 2) as t:
                    for j in range(2):
                        b = t * 2 + j
                        pe.wait_ge(xt_done, b + 7)
                        if j == 0:
                            pe.wait_ge(x_done, B)
                        transpose_xn(b + 8, xn[:, j], bank=1 + j)
                pe.wait_ge(xt_done, 2 * B)

                def four_chunks(t, first):
                    for u in range(4):
                        if u % 2 == 0:
                            pe.wait_ge(pat_in[u // 2], t * 16 + 16)
                        for g in range(4):
                            if not (first and u == 0):
                                pe.wait_ge(ia_done[g], t * 4 + u)
                            for c in range(DC):
                                ins = mm(ps[:, 3 + g, :], pat[:, u // 2, u % 2, c, :], xnT[:, c, 512 * g:512 * g + 512],
                                         c == 0, c == DC - 1)
                            ins.then_inc(ia_ps, 1)

                four_chunks(0, True)
                with pe.Fori(1, 4) as t:
                    four_chunks(t, False)

                def top_k(j, chunks):
                    base = (0, 36, 71)[j]
                    with pe.Fori(0, 16) as it:
                        pe.wait_ge(tk_cnt, it + (base + 1))
                        mm(ps[:, 7, 0:8], ones_b, cntb).then_inc(tk_tot, 1)
                    pe.wait_ge(tk_cnt, base + 17)
                    mm(ps[:, 7, 0:8], ones_b, cntb).then_inc(tk_tot, 1)
                    with pe.Fori(0, 16) as it:
                        pe.wait_ge(tk_cnt, it + (base + 18))
                        mm(ps[:, 7, 0:8], ones_b, cntb).then_inc(tk_tot, 1)
                    pe.wait_ge(tk_cnt, base + 34)
                    mm(ps[:, 7, 0:8], ones_b, cntb).then_inc(tk_tot, 1)
                    pe.wait_ge(tk_cnt, base + 35)
                    n = 8 * chunks
                    mm(ps[:, 7, 0:n], tri_b, eqb[:, 0:n], True, False)
                    for d in range(1, chunks):
                        ins = mm(ps[:, 7, 8 * d:n], ones_b, eqb[:, 0:n - 8 * d], False, d == chunks - 1)
                    ins.then_inc(tk_tot, 1)

                top_k(0, 16)
                pe.wait_ge(tk_cnt, 36)
                pe.wait_ge(piw_in, 48)
                for c in range(16):
                    g = c % 4
                    for a in range(2):
                        ins = mm(ps[32 * g:32 * g + 32, 2 + a, :], wpad[:, c, :], piw[:, c, 512 * a:512 * a + 512],
                                 c < 4, c >= 12)
                ins.then_inc(pr_ps, 1)
                pe.wait_ge(pr_copied, 1)
                for c in range(8):
                    ins = mm(ps[:, 4, 8 * c:8 * c + 8], pcp[:, P * c:P * c + P], sel8)
                ins.then_inc(pr_cols, 1)
                top_k(1, 8)
                pe.wait_ge(sm_dve, 1)
                pe.transpose(ps[0:8, 6, 0:P], pmax, ident).then_inc(sm_pe, 1)
                pe.wait_ge(sm_dve, 3)
                mm(ps[:, 6, 128:136], onesf[0:8, :], mxd[0:8, :]).then_inc(sm_pe, 1)
                pe.wait_ge(sm_dve, 7)
                mm(ps[:, 6, 136:144], onesf, dsum).then_inc(sm_pe, 1)
                pe.wait_ge(sm_dve, 9)
                for c in range(8):
                    ins = mm(ps[:, 5, 0:8], pvt[:, c, :], selm[:, 8 * c:8 * c + 8], c == 0, c == 7)
                ins.then_inc(agg_ps, 1)
                pe.wait_ge(agg_done, 1)
                for c in range(16):
                    ins = mm(ps[:, 4, 8 * c:8 * c + 8], oiw[:, P * c:P * c + P], aggT)
                ins.then_inc(oa_ps, 1)
                top_k(2, 16)
                pe.wait_ge(tk_cnt, 107)
                pe.wait_ge(op_in, 16)
                for c in range(16):
                    g = c % 4
                    ins = mm(ps[32 * g:32 * g + 32, 5, 0:D], wpad[:, c, :], opt[:, c, :], c < 4, c >= 12)
                ins.then_inc(op_ps, 1)
                pe.wait_ge(op_copied, 1)
                for b in range(B):
                    if b >= 2:
                        pe.wait_ge(x2_done, b - 1)
                    mm(ps[:, 1 + b % 2, 0:D], sel8[:, b:b + 1].to_broadcast([P, P]), outp).then_inc(op_rows, 1)

            pe.wait_ge(gate_in, 16)
            pe.wait_ge(x_done, 2 * B)
            for b in range(B):
                if b >= 2:
                    pe.wait_ge(xt_done, 24 + b - 1)
                transpose_xn(24 + b, xn_all[:, 2 * b:2 * b + 2, :], bank=1 + b % 2)
                pe.wait_ge(xt_done, 24 + b + 1)
                for t in range(2):
                    for c in range(DC):
                        ins = mm(ps[:, 6, E * (2 * b + t):E * (2 * b + t) + E],
                                 xnT[:, c, P * (2 * b + t):P * (2 * b + t) + P], gate[:, c, :], c == 0, c == DC - 1)
            ins.then_inc(rt_pe, 1)

            pe.wait_ge(rt_dve, 5)
            for t in range(2):
                ins = pe.transpose(ps[:, 7, P * t:P * t + P], sc2[:, t, :], ident)
            ins.then_inc(rt_pe, 1)
            pe.wait_ge(rt_dve, 18)
            for t in range(2):
                ins = pe.transpose(ps[:, 7, P * t:P * t + P], posm[:, P * t:P * t + P], ident)
            ins.then_inc(rt_pe, 1)

            for b in range(B):
                pe.wait_ge(g_done, 2 * b + 2)
                if b >= 1:
                    pe.wait_ge(disp_done, DC * b)
                for c in range(DC):
                    for t in range(2):
                        ins = mm(ps[:, c, :], xn_all[:, 2 * b + t, P * c:P * c + P], G[:, t, :], t == 0, t == 1)
                    ins.then_inc(disp_ps, 1)
                pe.wait_ge(gw_done, 2 * b + 2)
                if b >= 1:
                    pe.wait_ge(gwt_done, b)
                for g in range(4):
                    for t in range(2):
                        at = S * (g % 2) + P * t
                        ins = pe.transpose(ps[:, 2 + g // 2, at:at + P], GW[:, t, P * g:P * g + P], ident)
                ins.then_inc(gwt_ps, 1)
            pe.wait_ge(disp_done, DC * B)
            pe.wait_ge(gwt_done, B)

            def gate_up(u, f, w, rhs, first=False):
                if not first:
                    pe.wait_ge(h_done, u * 2 + (f - 1))
                for bank, m in ((2 * f, w[0]), (2 * f + 1, w[1])):
                    for a in range(2):
                        at = P * (2 * f + a)
                        for c in range(DC):
                            ins = mm(ps[:, bank, S * a:S * a + S], m[:, c, at:at + P], rhs(c), c == 0, c == DC - 1)
                ins.then_inc(gu_ps, 1)

            def down(u, s, w, first=False):
                pe.wait_ge(h_done, u * 2 + 2)
                if not first:
                    pe.wait_ge(down_done, u)
                for t in range(2):
                    for f in range(FC):
                        ins = mm(ps[:, 4 + s, D * t:D * t + D], hT[:, s, f, P * t:P * t + P], w[2][:, f, :],
                                 f == 0, f == FC - 1)
                ins.then_inc(down_ps, 1)

            pe.wait_ge(sw_in, 48)
            def shared_unit(u, s, first, second, last):
                def rhs(c):
                    return xnT[:, c, bslice(u)]
                gate_up(u, 0, shared_w, rhs, first)
                if not first:
                    down(u - 1, 1 - s, shared_w, second)
                gate_up(u, 1, shared_w, rhs, first)
                if last:
                    down(u, s, shared_w)

            shared_unit(0, 0, True, False, False)
            shared_unit(1, 1, False, True, False)
            with pe.Fori(1, B // 2 - 1) as t:
                for s in range(2):
                    shared_unit(t * 2 + s, s, False, False, False)
            shared_unit(B - 2, 0, False, False, False)
            shared_unit(B - 1, 1, False, False, True)
            with pe.Fori(0, 4) as t:
                for q in range(4):
                    s = q % 2
                    u = t * 4 + (B + q)
                    pe.wait_ge(ew_in[s], t * 96 + 48 * (q // 2 + 1))

                    def rhs(c, q=q):
                        return XT[:, t * 4 + q, c, :]
                    gate_up(u, 0, expert_w[s], rhs)
                    if q > 0:
                        down(u - 1, 1 - s, expert_w[1 - s])
                    gate_up(u, 1, expert_w[s], rhs)
                down(u, 1, expert_w[1])
            for s in range(2):
                pe.wait_ge(eo_moved[s], 64 * E // 2)
            pe.wait_ge(down_done, B + E)
            for b in range(B):
                if b >= 2:
                    pe.wait_ge(y_done, b - 1)
                for t in range(2):
                    for g in range(4):
                        ins = mm(ps[:, 6 + b % 2, D * t:D * t + D], GWT[:, b, g, P * t:P * t + P], EO[:, g, b, :],
                                 g == 0, g == 3)
                ins.then_inc(comb_ps, 1)

        @block.vector
        def _(dve):
            dve.wait_ge(const_in, 32)
            dve.tensor_copy(ones_b, onesf).then_inc(prepared, 1)
            dve.tensor_copy(tri_b, cst[:, C_TRI:C_PAR]).then_inc(prepared, 1)
            dve.tensor_copy(ident_b, ident).then_inc(prepared, 1)

            def stats(n, b):
                for t in range(2):
                    dve.bn_stats(bn[:, t, :], x_sb[:, b * 2 + t, :]).then_inc(stat_done, 1)
                dve.wait_ge(stat_done, n * 2 + 2)
                dve.memset(scrap, 0.0)
                for t in range(2):
                    dve.bn_aggr(mv[:, t, :], bn[:, t, :]).then_inc(mv_done, 1)

            def normalise(n, b, out):
                dve.wait_ge(rstd_done, n + 1)
                for t in range(2):
                    dve.tensor_scalar(out[:, t, :], x_sb[:, b * 2 + t, :], mv[:, t, 0:1], rstd[:, t:t + 1],
                                      ALU.subtract, ALU.mult).then_inc(xn_done, 1)

            def add_projection(i, b, layer):
                dve.wait_ge(proj_ps, i + 1)
                dve.tensor_tensor(ytmp.rearrange("p (t d) -> p t d", t=2),
                                  ps[:, 1, :].rearrange("p (t d) -> p t d", t=2),
                                  bp.unsqueeze(1).to_broadcast([P, 2, D]), ALU.add).then_inc(bias_done, 1)
                dve.wait_ge(bias_done, i + 1)
                xt = x_sb[:, tiles(b), :]
                dve.scalar_tensor_tensor(out=xt, in0=ytmp.rearrange("p (t d) -> p t d", t=2),
                                         scalar=tg[:, layer:layer + 1], in1=xt, op0=ALU.mult, op1=ALU.add
                                         ).then_inc(x_done, 1)

            def rotary_b(i, b, s):
                dve.wait_ge(q_perm, b + 1)
                dve.tensor_tensor(qT[0:GR, s], ps_all[0:GR, 1:3, :].rearrange("p a n -> p (a n)")[:, 0:NG * S]
                                  .rearrange("p (g q) -> p g q", g=NG),
                                  ropeB[0:GR].unsqueeze(1).to_broadcast([GR, NG, S]), ALU.mult).then_inc(q_mulB, 1)
                dve.wait_ge(q_mulA, b + 1)
                dve.wait_ge(q_mulB, b + 1)
                dve.tensor_tensor(qT[0:GR, s], qT[0:GR, s], qrot[0:GR], ALU.add).then_inc(q_done, 1)

            for layer in range(2):
                if layer == 0:
                    dve.wait_ge(x_in, 32)
                dve.wait_ge(attn_in, 32 + 16 * layer)
                if layer == 0:
                    dve.tensor_scalar(bqs[0:GR], bq[0:GR], -0.25, None, ALU.mult).then_inc(bqs_done, 1)
                else:
                    dve.wait_ge(x2_done, B)
                stats(16 * layer, 0)
                if layer == 0:
                    dve.wait_ge(cleared, 7)
                    dve.wait_ge(tanh_done, 1)
                for b in range(B):
                    dve.wait_ge(v_ps, 8 * layer + b + 1)
                    dve.tensor_tensor(V[0:SK, b, :], ps[0:SK, 7 if b % 2 == 0 else 0, 0:D], bv[0:SK], ALU.add
                                      ).then_inc(v_done, 1)
                normalise(16 * layer, 0, xn[:, 0])
                if layer == 0:
                    dve.wait_ge(mask_in, 64)
                    dve.tensor_scalar(maskb[:, :, 0:SK], mask_u[:, :, 0:SK], MASKED, None, ALU.mult).then_inc(prepared, 1)
                    dve.tensor_scalar(maskTb, maskT_u, MASKED, None, ALU.mult).then_inc(prepared, 1)
                    dve.tensor_scalar(seen, maskT_u, -1.0, 1.0, ALU.mult, ALU.add).then_inc(prepared, 1)
                else:
                    for j in range(6):
                        g, nh = divmod(j, 2)
                        dve.wait_ge(k_perm, j + 1)
                        buf = rden[0:GR, 0:308].rearrange("p (b k) -> p b k", k=SK)
                        dve.tensor_tensor(buf, ps[0:GR, 1 + j, 0:308].rearrange("p (b k) -> p b k", k=SK),
                                          ropeB[0:GR, 0:SK].unsqueeze(1).to_broadcast([GR, 4, SK]), ALU.mult
                                          ).then_inc(k_mulB, 1)
                        dve.wait_ge(k_mulA, j + 1)
                        dve.wait_ge(k_mulB, j + 1)
                        kt = kT[0:GR, g, 308 * nh:308 * nh + 308]
                        dve.tensor_tensor(kt, kt, rden[0:GR, 0:308], ALU.add).then_inc(kT_done, 1)
                        dve.wait_ge(kT_done, 6 + j + 1)
                    dve.wait_ge(any_ps, 1)
                    dve.tensor_scalar(anyv, ps[:, 7, 0:S], 1.0, None, ALU.min).then_inc(any_done, 1)
                    rotary_b(8, 0, 0)

                def step(i, b, s, first, last, layer=layer):
                    n = i + 8 * layer
                    if not last:
                        stats(n + 1, b + 1)
                    def row_max(t, banks):
                        lo, g0 = banks
                        k = len(range(g0, NG)) if t == 0 else (2 if g0 == 0 else 1)
                        src = ps[:, lo:lo + k, 0:GH * SK].rearrange("p g (h k) -> p g h k", k=SK)
                        return dve.tensor_reduce(mpad[:, t, g0:g0 + k, GR:GR + GH], src, AX, ALU.max, negate=True)
                    dve.wait_ge(rowmax_ps, i * 2 + 1)
                    row_max(0, (3, 0)).then_inc(rowmax_done, 1)
                    if not last:
                        normalise(n + 1, b + 1, xn[:, 1 - s])
                    if not first:
                        add_projection(i - 1, b - 1, layer)
                    dve.wait_ge(rowmax_ps, i * 2 + 2)
                    row_max(1, (6, 0))
                    row_max(1, (0, 2)).then_inc(rowmax_done, 1)
                    if layer == 1 and not last:
                        rotary_b(i + 1, b + 1, 1 - s)
                    dve.wait_ge(pv_ps, i + 1)
                    dve.reciprocal(rden, ps[:, 0, :]).then_inc(rden_done, 1)
                    if layer == 0:
                        dve.wait_ge(rden_done, i + 1)
                    else:
                        dve.wait_ge(rden_done, b * 2 + (B + 1))
                        rd = rden.rearrange("p (c q) -> p c q", c=DC)
                        dve.tensor_tensor(rd, rd, anyv.unsqueeze(1).to_broadcast([P, DC, S]), ALU.mult
                                          ).then_inc(rden_done, 1)
                        dve.wait_ge(rden_done, b * 2 + (B + 2))
                    dve.tensor_tensor(attnT.rearrange("p c q -> p (c q)"), ps[:, 7, :], rden, ALU.mult
                                      ).then_inc(attn_done, 1)
                    if last:
                        add_projection(i, b, layer)
                steps(dve, layer, step)
                dve.wait_ge(x_done, B * (layer + 1))
                if layer == 1:
                    break

                stats(8, 0)

                def next_norm(b, j, last=False):
                    dve.wait_ge(xt_ps, b + 7)
                    normalise(b + 8, b, xn[:, j])
                    if not last:
                        stats(b + 9, b + 1)

                with dve.Fori(0, B // 2 - 1) as t:
                    for j in range(2):
                        next_norm(t * 2 + j, j)
                next_norm(B - 2, 0)
                next_norm(B - 1, 1, True)

                count = [0]

                def link(ins):
                    count[0] += 1
                    ins.then_inc(tk_step, 1)
                    dve.wait_ge(tk_step, count[0])

                def top_k(j, data, chunks, k, out):
                    n, base = 8 * chunks, 35 * j
                    key_, hi_, lo_, neg_, sgn_, tmp_, sel_ = (a[:, 0:n] for a in (key, khi, klo, neg, sgn, tmp, out))

                    def per_batch(a):
                        return a.unsqueeze(1).to_broadcast([P, chunks, 8])

                    def chunked(a):
                        return a.rearrange("p (c b) -> p c b", b=8)

                    def count_up(src):
                        with nc.allow_low_precision(reason="counts up to 16 are exact in bfloat16"):
                            dve.tensor_reduce(cntb, src.rearrange("p (c b) -> p b c", b=8), AX, ALU.add
                                              ).then_inc(tk_cnt, 1)

                    link(dve.tensor_scalar(key_, data, 0.0, None, ALU.add))
                    halves = key_.bitcast(U16).rearrange("p (n two) -> p n two", two=2)
                    link(dve.tensor_copy(hi_, halves[:, :, 1]))
                    link(dve.tensor_copy(lo_, halves[:, :, 0]))
                    link(dve.tensor_scalar(neg_, hi_, 32768.0, None, ALU.is_ge))
                    link(dve.tensor_scalar(sgn_, neg_, -2.0, 1.0, ALU.mult, ALU.add))
                    link(dve.tensor_tensor(hi_, hi_, sgn_, ALU.mult))
                    link(dve.tensor_scalar(tmp_, neg_, 32767.0, 32768.0, ALU.mult, ALU.add))
                    link(dve.tensor_tensor(hi_, hi_, tmp_, ALU.add))
                    link(dve.tensor_tensor(lo_, lo_, sgn_, ALU.mult))
                    link(dve.tensor_scalar(tmp_, neg_, 65535.0, None, ALU.mult))
                    link(dve.tensor_tensor(lo_, lo_, tmp_, ALU.add))
                    link(dve.memset(need, float(k)))

                    def search(keys, tot0):
                        link(dve.memset(thr, 0.0))
                        c0 = count[0]
                        with dve.Fori(0, 16) as it:
                            p = pw[:, bass.ds(it, 1)]
                            dve.scalar_tensor_tensor(out=chunked(cmpb[:, 0:n]), in0=chunked(keys), scalar=p,
                                                     in1=per_batch(thr), op0=ALU.subtract, op1=ALU.is_ge
                                                     ).then_inc(tk_step, 1)
                            dve.wait_ge(tk_step, it * 3 + (c0 + 1))
                            count_up(cmpb[:, 0:n])
                            dve.wait_ge(tk_tot, it + (tot0 + 1))
                            dve.tensor_tensor(ge, ps[:, 7, 0:8], need, ALU.is_ge).then_inc(tk_step, 1)
                            dve.wait_ge(tk_step, it * 3 + (c0 + 2))
                            dve.scalar_tensor_tensor(out=thr, in0=ge, scalar=p, in1=thr, op0=ALU.mult, op1=ALU.add
                                                     ).then_inc(tk_step, 1)
                            dve.wait_ge(tk_step, it * 3 + (c0 + 3))
                        count[0] += 48

                    search(hi_, base)
                    link(dve.tensor_tensor(chunked(gtm[:, 0:n]), chunked(hi_), per_batch(thr), ALU.is_gt))
                    count_up(gtm[:, 0:n])
                    link(dve.tensor_tensor(chunked(tmp_), chunked(hi_), per_batch(thr), ALU.is_equal))
                    link(dve.scalar_tensor_tensor(out=lo_, in0=lo_, scalar=1.0, in1=tmp_, op0=ALU.add, op1=ALU.mult))
                    link(dve.tensor_scalar(lo_, lo_, -1.0, None, ALU.add))
                    dve.wait_ge(tk_tot, base + 17)
                    link(dve.tensor_tensor(need, need, ps[:, 7, 0:8], ALU.subtract))
                    search(lo_, base + 17)
                    link(dve.tensor_tensor(chunked(tmp_), chunked(lo_), per_batch(thr), ALU.is_gt))
                    count_up(tmp_)
                    link(dve.tensor_tensor(gtm[:, 0:n], gtm[:, 0:n], tmp_, ALU.add))
                    dve.wait_ge(tk_tot, base + 34)
                    link(dve.tensor_tensor(need, need, ps[:, 7, 0:8], ALU.subtract))
                    link(dve.tensor_tensor(chunked(tmp_), chunked(lo_), per_batch(thr), ALU.is_equal))
                    dve.tensor_copy(eqb[:, 0:n], tmp_).then_inc(tk_cnt, 1)
                    dve.wait_ge(tk_tot, base + 35)
                    link(dve.tensor_tensor(chunked(sel_), chunked(ps[:, 7, 0:n]), per_batch(need), ALU.is_le))
                    link(dve.tensor_tensor(sel_, sel_, tmp_, ALU.mult))
                    link(dve.tensor_tensor(sel_, sel_, gtm[:, 0:n], ALU.add))

                for g in range(4):
                    dve.wait_ge(ia_done[g], 16)
                link(dve.tensor_scalar(acts, acts, 1.0 / S, None, ALU.mult))
                top_k(0, acts, 16, TOP_I, selm)
                chunk8 = "p (c b) -> p c b"
                dve.tensor_tensor(wpad[:, :, 0:8], acts.rearrange(chunk8, b=8), selm.rearrange(chunk8, b=8),
                                  ALU.mult).then_inc(tk_cnt, 1)
                dve.wait_ge(pa_done, 1)
                top_k(1, acts[:, 0:64], 8, TOP_P, selm)
                dve.tensor_reduce(pmax, acts[:, 0:64].rearrange("p (c b) -> p b c", b=8), AX, ALU.max
                                  ).then_inc(sm_dve, 1)
                dve.wait_ge(sm_pe, 1)
                dve.tensor_reduce(mx8[0:8, 0:1], ps[0:8, 6, 0:P], AX, ALU.max).then_inc(sm_dve, 1)
                dve.wait_ge(sm_dve, 2)
                dve.tensor_scalar(mxd[0:8, :], ident[0:8, 0:8], mx8[0:8, 0:1], None, ALU.mult).then_inc(sm_dve, 1)
                dve.wait_ge(sm_pe, 2)
                g64, s64 = gtm[:, 0:64].rearrange(chunk8, b=8), selm[:, 0:64].rearrange(chunk8, b=8)
                dve.tensor_copy(rs8, ps[:, 6, 128:136]).then_inc(sm_dve, 1)
                dve.wait_ge(sm_dve, 4)
                dve.tensor_tensor(g64, acts[:, 0:64].rearrange(chunk8, b=8), rs8.unsqueeze(1).to_broadcast([P, 8, 8]),
                                  ALU.subtract).then_inc(sm_dve, 1)
                dve.wait_ge(sm_act, 1)
                dve.tensor_tensor(s64, g64, s64, ALU.mult).then_inc(sm_dve, 1)
                dve.wait_ge(sm_dve, 6)
                dve.tensor_reduce(dsum, selm[:, 0:64].rearrange("p (c b) -> p b c", b=8), AX, ALU.add
                                  ).then_inc(sm_dve, 1)
                dve.wait_ge(sm_pe, 3)
                dve.reciprocal(rs8, ps[:, 6, 136:144]).then_inc(sm_dve, 1)
                dve.wait_ge(sm_dve, 8)
                dve.tensor_tensor(s64, s64, rs8.unsqueeze(1).to_broadcast([P, 8, 8]), ALU.mult).then_inc(sm_dve, 1)
                dve.wait_ge(agg_ps, 1)
                dve.tensor_copy(aggT, ps[:, 5, 0:8]).then_inc(agg_done, 1)
                dve.wait_ge(oa_done, 1)
                top_k(2, acts, 16, TOP_O, selm)
                dve.tensor_tensor(wpad[:, :, 0:8], acts.rearrange(chunk8, b=8), selm.rearrange(chunk8, b=8),
                                  ALU.mult).then_inc(tk_cnt, 1)
                for b in range(B):
                    dve.wait_ge(op_rows, b + 1)
                    xt = x_sb[:, 2 * b:2 * b + 2, :]
                    dve.scalar_tensor_tensor(out=xt, in0=ps[:, 1 + b % 2, 0:D].unsqueeze(1).to_broadcast([P, 2, D]),
                                             scalar=tg[:, 2:3], in1=xt, op0=ALU.mult, op1=ALU.add
                                             ).then_inc(x2_done, 1)

            stats(24, 0)
            for b in range(B):
                normalise(24 + b, b, xn_all[:, 2 * b:2 * b + 2, :])
                if b < B - 1:
                    stats(25 + b, b + 1)
            count = [0]

            def route(ins):
                count[0] += 1
                ins.then_inc(rt_dve, 1)
                dve.wait_ge(rt_dve, count[0])

            logits = ps[:, 6, 0:256].rearrange("p (t e) -> p t e", e=E)
            pr3 = probs.rearrange("p (t e) -> p t e", e=E)
            cols = cum[:, 0:16]
            dve.wait_ge(rt_pe, 1)
            route(dve.tensor_reduce(cols, logits, AX, ALU.max))
            route(dve.tensor_tensor(pr3, logits, cols.unsqueeze(2).to_broadcast([P, 16, E]), ALU.subtract))
            dve.wait_ge(rt_act, 1)
            route(dve.tensor_reduce(cols, pr3, AX, ALU.add))
            route(dve.reciprocal(cum[:, 16:32], cols))
            route(dve.tensor_tensor(sc2.rearrange("p t (b e) -> p b t e", b=B),
                                    probs.rearrange("p (b t e) -> p b t e", b=B, t=2),
                                    cum[:, 16:32].rearrange("p (b t) -> p b t", t=2).unsqueeze(3)
                                    .to_broadcast([P, B, 2, E]), ALU.mult))
            dve.wait_ge(rt_pe, 2)
            route(dve.tensor_copy(work, ps[:, 7, 0:S]))
            for _ in range(CAP // 8):
                route(dve.max(mx8, work))
                route(dve.match_replace(work, mx8, work, -1.0))
            route(dve.tensor_scalar(work, work, 0.0, None, ALU.is_lt))
            route(dve.memset(probs, 1.0))
            route(dve.tensor_tensor_scan(cum, probs, work, 0.0, ALU.mult, ALU.add))
            route(dve.tensor_tensor(posm, cum, work, ALU.mult))
            dve.wait_ge(rt_pe, 3)
            route(dve.tensor_copy(posT, ps[:, 7, 0:S].rearrange("p (t m) -> p t m", t=2)))

            for b in range(B):
                for t in range(2):
                    if b >= 1:
                        dve.wait_ge(disp_ps, DC * b)
                        dve.wait_ge(gw_done, 2 * b)
                    dve.tensor_tensor(G[:, t].rearrange("p (e s) -> p e s", e=E),
                                      iota.unsqueeze(1).to_broadcast([P, E, 32]),
                                      posT[:, t, E * b:E * b + E].unsqueeze(2).to_broadcast([P, E, 32]), ALU.is_equal
                                      ).then_inc(g_done, 1)
                for t in range(2):
                    dve.wait_ge(g_done, 2 * b + t + 1)
                    if b >= 1:
                        dve.wait_ge(gwt_ps, b)
                    dve.tensor_tensor(GW[:, t].rearrange("p (e s) -> p e s", e=E),
                                      G[:, t].rearrange("p (e s) -> p e s", e=E),
                                      sc2[:, t, E * b:E * b + E].unsqueeze(2).to_broadcast([P, E, 32]), ALU.mult
                                      ).then_inc(gw_done, 1)

            def gated(u, s):
                for f in range(2):
                    dve.wait_ge(gelu_done, u * 2 + (f + 1))
                    dve.tensor_tensor(hT[:, s, 2 * f:2 * f + 2, :].rearrange("p f n -> p (f n)"), hgl[:, f, :],
                                      ps[:, 2 * f + 1, :], ALU.mult).then_inc(h_done, 1)

            with dve.Fori(0, B // 2) as t:
                for s in range(2):
                    u = t * 2 + s
                    gated(u, s)
                    dve.wait_ge(down_ps, u + 1)
                    xt = x_sb[:, tiles(u), :]
                    dve.scalar_tensor_tensor(out=xt, in0=ps[:, 4 + s, :].rearrange("p (t d) -> p t d", t=2),
                                             scalar=tg[:, 3:4], in1=xt, op0=ALU.mult, op1=ALU.add
                                             ).then_inc(down_done, 1)
            with dve.Fori(0, E // 2) as t:
                for s in range(2):
                    gated(t * 2 + (B + s), s)
            for b in range(B):
                dve.wait_ge(comb_ps, b + 1)
                xt = x_sb[:, 2 * b:2 * b + 2, :]
                dve.scalar_tensor_tensor(out=xt, in0=ps[:, 6 + b % 2, :].rearrange("p (t d) -> p t d", t=2),
                                         scalar=tg[:, 3:4], in1=xt, op0=ALU.mult, op1=ALU.add).then_inc(y_done, 1)


def kernel(**inputs):
    import numpy as np
    from concourse import bacc
    from concourse.bass_utils import run_bass_kernel_spmd

    a = {k: np.asarray(v) for k, v in inputs.items()}
    f32 = np.float32

    def halves(w):
        return np.ascontiguousarray(w.reshape(DC, P, -1).transpose(1, 0, 2))

    def grouped(w):
        return np.pad(w, ((0, 0), (0, NG * GR - D)))

    def attention(wq, bq, wk, bk, wv, bv, wo, bo):
        cols = [halves(grouped(wq.T)).reshape(P, -1), halves(grouped(wk.T)).reshape(P, -1),
                halves(wv.T).reshape(P, -1), halves(wo.T).reshape(P, -1),
                np.broadcast_to(bv, (P, D)), np.broadcast_to(bo, (P, D))]
        for b in (bq, bk):
            cols.append(np.pad(np.pad(b, (0, NG * GR - D)).reshape(NG, GR).T, ((0, P - GR), (0, 0))))
        return np.concatenate(cols, axis=1)

    const = np.zeros((P, C_END - 4), f32)
    const[:, C_ID:C_ONE] = np.eye(P)
    const[:, C_ONE:C_TRI] = 1.0
    const[:, C_TRI:C_PAR] = np.triu(np.ones((P, P)))
    const[:, C_PAR:C_PAR + 16] = 1.0
    const[:, C_PAR + 48:C_PAR + 64] = 1.0
    const[:, C_PW:C_SEL] = 2.0 ** np.arange(15, -1, -1)
    for b in range(B):
        const[b::32, C_SEL + b] = 1.0
    const[:, C_IOTA:C_HM] = np.arange(1, 33)
    for j in range(GH):
        const[HD * j:HD * j + HD, C_HM + j] = 1.0
    for r in range(GR):
        const[r ^ 1, C_PERM + r] = 1.0
    kone = np.zeros((P - GR, NG * GH, SK), f32)
    for h in range(NG * GH):
        kone[h % GH, h, :] = 1.0
    inv = np.exp(np.arange(0, HD, 2, dtype=f32) * f32(-(4.0 * np.log(f32(10.0))) / HD)).astype(f32)
    angle = np.arange(S, dtype=f32)[:, None] * inv
    sin, cos = np.sin(angle).T, np.cos(angle).T
    rope_a, rope_b = np.zeros((GR, S), f32), np.zeros((GR, S), f32)
    for r in range(GR):
        m = (r % HD) // 2
        rope_a[r] = sin[m] if r % 2 == 0 else -sin[m]
        rope_b[r] = -cos[m]

    mask = np.pad(a["mask_1x1xSxS2_bk1"].reshape(S, SK), ((0, 0), (0, 80 - SK)))
    maskT = np.pad(mask.T, ((0, P - 80), (0, 0)))
    arrays = {
        "x": a["x"].reshape(T, D),
        "ctx": halves(a["ctx_1024"].reshape(KB, D).T),
        "gates": np.broadcast_to(np.concatenate([a["g_xattn"], a["g_ffn"]]), (P, 4)),
        "mask": np.ascontiguousarray(mask.reshape(2, P, 80).transpose(1, 0, 2)).view(np.uint32),
        "maskT": np.ascontiguousarray(maskT).view(np.uint32),
        "const": const,
        "kone": kone,
        "ropeA": rope_a,
        "ropeB": rope_b,
        "attn": np.stack([
            attention(*(a["L0_xattn_" + n] for n in ("Wq", "bq", "Wk", "bk", "Wv", "bv", "Wp", "bp"))),
            attention(*(a["L1_xattn_" + n] for n in ("Wq", "bq", "Wk", "bk", "Wv", "bv", "Wo", "bo")))]),
        "pat": a["L0_ffn_input_patterns"].reshape(8, 2, P, DC, P).transpose(0, 4, 1, 3, 2),
        "piw": a["L0_ffn_process_input_weights"].T.reshape(16, P, NP_).transpose(1, 0, 2),
        "pv": a["L0_ffn_process_values"].reshape(8, P, DV).transpose(1, 0, 2),
        "oiw": a["L0_ffn_output_input_weights"].T,
        "op": a["L0_ffn_output_patterns"].reshape(16, P, D).transpose(1, 0, 2),
        "gate": halves(a["L1_ffn_gate_w"].T),
        "wg": a["L1_ffn_Wg"].transpose(0, 2, 1).reshape(E, DC, P, F).transpose(0, 2, 1, 3),
        "wu": a["L1_ffn_Wu"].transpose(0, 2, 1).reshape(E, DC, P, F).transpose(0, 2, 1, 3),
        "wd": a["L1_ffn_Wd"].transpose(0, 2, 1).reshape(E, FC, P, D).transpose(0, 2, 1, 3),
        "sg": halves(a["L1_ffn_Ws_g"].T),
        "su": halves(a["L1_ffn_Ws_u"].T),
        "sd": a["L1_ffn_Ws_d"].T.reshape(FC, P, D).transpose(1, 0, 2),
    }
    arrays = {f"in_{k}": np.ascontiguousarray(v) for k, v in arrays.items()}
    nc = bacc.Bacc("TRN2", target_bir_lowering=False, num_devices=1)
    args = [nc.dram_tensor(k, v.shape, mybir.dt.from_np(v.dtype), kind="ExternalInput").ap()
            for k, v in arrays.items()]
    out = nc.dram_tensor("out_x", [T, D], F32, kind="ExternalOutput").ap()
    flamingo_kernel(nc, *args, out)
    r = run_bass_kernel_spmd(nc, [arrays], core_ids=[0])
    return r.results[0]["out_x"].reshape(B, S, D)
```

```python
from contextlib import ExitStack

import concourse.bass as bass
from concourse import mybir
from concourse.alu_op_type import AluOpType as ALU

ACT = mybir.ActivationFunctionType
AX = mybir.AxisListType.X
F32 = mybir.dt.float32
BF16 = mybir.dt.bfloat16
F32R = mybir.dt.float32r
U16 = mybir.dt.uint16
U8 = mybir.dt.uint8
U32 = mybir.dt.uint32
I32 = mybir.dt.int32

P = 128
B, S, D = 8, 256, 256
T = B * S
DC = D // P
H, HD, SK = 16, 16, 77
NG, GH = 3, 6
GR = GH * HD
KB = B * SK
NI, NP_, NO, DV = 2048, 1024, 2048, 128
TOP_I, TOP_P, TOP_O = NI // 8, NP_ // 8, NO // 8
E, F, CAP = 16, 512, 32
FC = F // P
EPS = 1e-5
MASKED = -float(2.0 ** 100)

C_ID, C_ONE, C_TRI, C_PAR, C_PW, C_DIG, C_SEL, C_IOTA, C_HM, C_PERM, C_GATE, C_END = (
    0, 128, 256, 384, 448, 452, 468, 476, 508, 514, 610, 614)
RADIX, DIGITS = 16, 4


def flamingo_kernel(nc, x_d, ctx_d, gates_d, mask_d, maskT_d, const_d, kone_d,
                    ropeA_d, ropeB_d, attn_d, pat_d, piw_d,
                    pv_d, oiw_d, op_d, gate_d, wg_d, wu_d, wd_d, sg_d, su_d, sd_d, out_d):
    with ExitStack() as ctx:
        def sem(name):
            return ctx.enter_context(nc.semaphore(name))

        starts = {}

        def rounded(name, where, at, cols):
            t = nc.alloc_sbuf_tensor_at(name, [P, cols], F32R, offset=starts[where] + 4 * at)
            return t[:, :]

        def region(name, cols):
            whole = ctx.enter_context(nc.sbuf_tensor(name, [P, cols], F32))
            starts[name] = nc.sbuf_base - 4 * cols
            at = [0]

            def take(n, start=None):
                lo = at[0] if start is None else start
                at[0] = lo + n
                assert at[0] <= cols, (name, at[0], cols)
                return whole[:, lo:lo + n]
            return take

        keep = region("keep", 13900)
        x_sb = keep(T // P * D).rearrange("p (t d) -> p t d", d=D)
        xnT_s = keep(DC * T)
        xnT = xnT_s.rearrange("p (c t) -> p c t", c=DC)
        qT = xnT_s[:, 0:2 * NG * S].rearrange("p (s g q) -> p s g q", s=2, g=NG)
        qraw = xnT_s[:, 1536:2304].rearrange("p (g q) -> p g q", g=NG)
        qrot = xnT_s[:, 2304:3072].rearrange("p (g q) -> p g q", g=NG)
        pcp = xnT_s[:, 3072:3072 + NP_]
        qr = rounded("qr", "keep", T // P * D + 3072, NG * S).rearrange("p (g q) -> p g q", g=NG)
        xn_s = keep(2 * 2 * D)
        xn = xn_s.rearrange("p (s t d) -> p s t d", s=2, d=D)
        xnT_b = keep(DC * S).rearrange("p (c t) -> p c t", c=DC)
        cst = keep(C_END)
        ident, onesf = cst[:, C_ID:C_ONE], cst[:, C_ONE:C_TRI]
        par = cst[:, C_PAR:C_PW].rearrange("p (a m) -> p a m", a=2)
        pw, digit = cst[:, C_PW:C_DIG], cst[:, C_DIG:C_SEL]
        sel8, iota = cst[:, C_SEL:C_IOTA], cst[:, C_IOTA:C_HM]
        hmask, perm, gates = cst[:, C_HM:C_PERM], cst[:, C_PERM:C_GATE], cst[:, C_GATE:C_END]
        tg = keep(4)
        bn = keep(2 * 6).rearrange("p (t k) -> p t k", k=6)
        mv = keep(2 * 2).rearrange("p (t k) -> p t k", k=2)
        scrap, veps, rstd, mhalf, eps = keep(1), keep(2), keep(2), keep(2), keep(2)
        fbn = keep(2 * 6).rearrange("p (t k) -> p t k", k=6)
        fag = keep(2 * 2).rearrange("p (t k) -> p t k", k=2)
        fmv = keep(T // P * 2).rearrange("p (t k) -> p t k", k=2)
        fveps, frstd = keep(2), keep(T // P)
        ones_b = keep(64).bitcast(BF16)
        tri_b = keep(64).bitcast(BF16)
        ident_b = keep(64).bitcast(BF16)
        bqs = keep(NG)
        acts = keep(128)
        tk = keep(8 * 128)
        key, flip, met, gtm, selm = (tk[:, 128 * j:128 * j + 128] for j in range(5))
        khi, klo, level = (tk[:, 640 + 64 * j:704 + 64 * j].bitcast(U16) for j in range(3))
        rden, ytmp = tk[:, 0:512], tk[:, 512:1024]
        tied, above, above_lo, eqb = (keep(64).bitcast(BF16) for _ in range(4))
        reached = xnT_s[:, 0:1024].bitcast(BF16).rearrange("p (c n) -> p c n", c=16)
        cntb = keep(4).bitcast(BF16)
        thr, pmax, mx8, mxd, rs8, dsum = (keep(8) for _ in range(6))
        wpad_s = keep(512)
        wpad = wpad_s.rearrange("p (c m) -> p c m", m=32)
        outp = keep(D)
        aggT = keep(8)
        mask_w, maskT_w = keep(2 * 20).bitcast(U32), keep(64).bitcast(U32)
        mask_u, maskT_u = mask_w.bitcast(U8).rearrange("p (t k) -> p t k", t=2), maskT_w.bitcast(U8)
        maskb = keep(80).bitcast(BF16).rearrange("p (t k) -> p t k", t=2)
        maskTb = keep(128).bitcast(BF16)
        seen = keep(128).bitcast(BF16)
        anyv = keep(S)
        gate = keep(DC * E).rearrange("p (c e) -> p c e", c=DC)

        big = region("big", 19456)
        piw = big(16 * NP_).rearrange("p (c n) -> p c n", c=16)
        pvt = big(8 * DV).rearrange("p (c n) -> p c n", c=8)
        oiw = big(NO)
        opt = big(16 * D, 0).rearrange("p (c n) -> p c n", c=16)
        kraw = big(NG * KB, 0).rearrange("p (g n) -> p g n", g=NG)
        XT = big(E * DC * S, 2048).rearrange("p (e c t) -> p e c t", e=E, c=DC)
        EO = big(4 * B * D, 0).rearrange("p (g b d) -> p g b d", g=4, b=B)
        xn_all = big(T // P * D, 10240).rearrange("p (t d) -> p t d", d=D)
        sw = big(3072)
        hT = big(2 * FC * S).rearrange("p (s f n) -> p s f n", s=2, f=FC)

        vp = region("vp", 8192)
        V = vp(B * D).rearrange("p (b d) -> p b d", b=B)
        Vpad = vp(2 * H * 32).rearrange("p (s h m) -> p s h m", s=2, h=H)
        PT = vp(H * S).rearrange("p (h q) -> p h q", h=H)
        mpad_s = vp(2 * NG * P)
        mpad = mpad_s.rearrange("p (t g m) -> p t g m", t=2, g=NG)
        GWT = vp(B * 4 * S, 0).rearrange("p (b g t) -> p b g t", b=B, g=4)

        PAT_AT = 9576
        att = region("att", PAT_AT + 1392)
        awt = att(2176 + 518)
        wq = awt[:, 0:576].rearrange("p (c g m) -> p c g m", c=DC, g=NG)
        wk = awt[:, 576:1152].rearrange("p (c g m) -> p c g m", c=DC, g=NG)
        wv = awt[:, 1152:1664].rearrange("p (c m) -> p c m", c=DC)
        wp = awt[:, 1664:2176].rearrange("p (c m) -> p c m", c=DC)
        bv, bp, bq, bk = awt[:, 2176:2432], awt[:, 2432:2688], awt[:, 2688:2691], awt[:, 2691:2694]
        ctxT = att(DC * KB).rearrange("p (c n) -> p c n", c=DC)
        kT = att(NG * KB).rearrange("p (g n) -> p g n", g=NG)
        kbd = att(2 * NG * GH * SK).rearrange("p (s h k) -> p s h k", s=2, k=SK)
        rope = att(2 * S)
        ropeA, ropeB = rope[:, 0:S], rope[:, S:2 * S]
        attnT = att(DC * S).rearrange("p (c q) -> p c q", c=DC)
        kbr = rounded("kbr", "att", PAT_AT, NG * GH * SK).rearrange("p (h k) -> p h k", k=SK)
        pat_s = att(1024 + 368, PAT_AT)
        pat = pat_s[:, 0:1024].rearrange("p (s j c n) -> p s j c n", s=2, j=2, c=DC)
        ew = att(2 * 3072, 0)
        hgl = att(2 * 512).rearrange("p (f n) -> p f n", f=2)
        eo_s = att(2 * 2 * D)
        eo = eo_s.rearrange("p (s t d) -> p s t d", s=2, d=D)
        GW = [att(1024).rearrange("p (t n) -> p t n", t=2) for _ in range(2)]
        G = [a.rearrange("p (t n) -> p t n", t=2) for a in (xn_s, eo_s)]
        logT = anyv[0:E, :]
        probs, sc2_s, work, posm = (tk[:, 256 * j:256 * j + 256] for j in range(4))
        sc2 = sc2_s.rearrange("p (t m) -> p t m", t=2)
        posT = wpad_s[:, 0:256].rearrange("p (t m) -> p t m", t=2)
        cum = wpad_s[:, 256:512]

        ps = ctx.enter_context(nc.psum_tensor("ps", [P, 8, 512], F32))
        ps_all = ps[:, :, :]

        def weights(base):
            return (base[:, 0:1024].rearrange("p (c f) -> p c f", c=DC),
                    base[:, 1024:2048].rearrange("p (c f) -> p c f", c=DC),
                    base[:, 2048:3072].rearrange("p (f d) -> p f d", f=FC))

        expert_w = [weights(ew[:, 3072 * s:3072 * s + 3072]) for s in range(2)]
        shared_w = weights(sw)

        x_in, const_in, attn_in, mask_in = sem("x_in"), sem("const_in"), sem("attn_in"), sem("mask_in")
        kone_in, pat_in = sem("kone_in"), [sem("pat_in0"), sem("pat_in1")]
        piw_in, op_in, gate_in, sw_in = sem("piw_in"), sem("op_in"), sem("gate_in"), sem("sw_in")
        egu_in, ed_in = [sem("egu_in0"), sem("egu_in1")], [sem("ed_in0"), sem("ed_in1")]
        eo_moved = [sem("eo_moved0"), sem("eo_moved1")]
        out_done = sem("out_done")
        cleared, prepared, tanh_done, bqs_done = sem("cleared"), sem("prepared"), sem("tanh_done"), sem("bqs_done")
        fstat_done, faggr_done, fmv_done, fveps_done, frstd_done = (sem("fstat_done"), sem("faggr_done"), sem("fmv_done"), sem("fveps_done"),
                                                                    sem("frstd_done"))
        stat_done, mv_done, veps_done, rstd_done = sem("stat_done"), sem("mv_done"), sem("veps_done"), sem("rstd_done")
        xn_done, xt_ps, xt_done = sem("xn_done"), sem("xt_ps"), sem("xt_done")
        k_ps, k_raw, k_perm, k_mulA, k_mulB, kT_done = (sem("k_ps"), sem("k_raw"), sem("k_perm"), sem("k_mulA"),
                                                        sem("k_mulB"), sem("kT_done"))
        v_ps, v_done = sem("v_ps"), sem("v_done")
        q_ps, q_raw, q_perm, q_mulA, q_mulB, q_done = (sem("q_ps"), sem("q_raw"), sem("q_perm"), sem("q_mulA"),
                                                       sem("q_mulB"), sem("q_done"))
        qr_done = sem("qr_done")
        kbd_done, rowmax_ps, rowmax_done = sem("kbd_done"), sem("rowmax_ps"), sem("rowmax_done")
        mT_ps, mT_done, score_ps, exp_done, pv_ps = (sem("mT_ps"), sem("mT_done"), sem("score_ps"), sem("exp_done"),
                                                     sem("pv_ps"))
        rden_done, attn_done, proj_ps, bias_done, x_done = (sem("rden_done"), sem("attn_done"), sem("proj_ps"),
                                                            sem("bias_done"), sem("x_done"))
        any_ps, any_done = sem("any_ps"), sem("any_done")
        ia_ps, ia_done = sem("ia_ps"), [sem(f"ia_done{j}") for j in range(4)]
        tk_step, tk_cnt, tk_tot = sem("tk_step"), sem("tk_cnt"), sem("tk_tot")
        pr_ps, pr_copied, pr_cols, pa_done = sem("pr_ps"), sem("pr_copied"), sem("pr_cols"), sem("pa_done")
        sm_dve, sm_pe, sm_act = sem("sm_dve"), sem("sm_pe"), sem("sm_act")
        agg_ps, agg_done, oa_ps, oa_done = sem("agg_ps"), sem("agg_done"), sem("oa_ps"), sem("oa_done")
        op_ps, op_copied, op_rows, x2_done = sem("op_ps"), sem("op_copied"), sem("op_rows"), sem("x2_done")
        logT_ps, logT_done = sem("logT_ps"), sem("logT_done")
        rt_dve, rt_pe, rt_act = sem("rt_dve"), sem("rt_pe"), sem("rt_act")
        g_done, gw_done, disp_ps, disp_done = sem("g_done"), sem("gw_done"), sem("disp_ps"), sem("disp_done")
        gwt_ps, gwt_done = sem("gwt_ps"), sem("gwt_done")
        gu_ps, gelu_done, h_done, down_ps, down_done = (sem("gu_ps"), sem("gelu_done"), sem("h_done"),
                                                        sem("down_ps"), sem("down_done"))
        comb_ps, y_done = sem("comb_ps"), sem("y_done")

        block = ctx.enter_context(nc.Block())

        def bslice(b):
            return bass.ds(b * S, S)

        def ktslice(b):
            return bass.ds(b * SK, SK)

        def tiles(b):
            return bass.ds(b * 2, 2)

        def q_bank(g):
            return ps[0:GR, (5, 5, 2)[g], S * (g % 2):S * (g % 2) + S]

        def steps(eng, layer, step):
            for b in range(2):
                step(8 * layer + b, b, b, b == 0, False, True)
            with eng.Fori(1, B // 2 - 1) as t:
                for j in range(2):
                    b = t * 2 + j
                    step(b + 8 * layer, b, j, False, False, True)
            for b in range(B - 2, B):
                step(8 * layer + b, b, b % 2, False, b == B - 1, False)

        @block.sync
        def _(sp):
            sp.dma_start(x_sb[:, 0:4, :], x_d.rearrange("(t p) d -> p t d", p=P)[:, 0:4, :]).then_inc(x_in, 16)
            sp.dma_start(cst[:, 0:C_GATE], const_d).then_inc(const_in, 16)
            sp.dma_start(gates, gates_d).then_inc(const_in, 16)
            sp.dma_start(awt, attn_d[0, :, 0:2694]).then_inc(attn_in, 16)
            sp.dma_start(ctxT, ctx_d).then_inc(attn_in, 16)
            for s in range(2):
                sp.dma_start(kbd[GR:P, s, :, :], kone_d).then_inc(kone_in, 16)
            sp.dma_start(x_sb[:, 4:16, :], x_d.rearrange("(t p) d -> p t d", p=P)[:, 4:16, :]).then_inc(x_in, 16)
            sp.dma_start(mask_w, mask_d.rearrange("p t k -> p (t k)")).then_inc(mask_in, 16)
            sp.dma_start(maskT_w, maskT_d).then_inc(mask_in, 16)
            sp.dma_start(ropeA[0:GR, :], ropeA_d).then_inc(mask_in, 16)
            sp.dma_start(ropeB[0:GR, :], ropeB_d).then_inc(mask_in, 16)
            sp.dma_start(piw, piw_d).then_inc(piw_in, 16)
            sp.dma_start(pvt, pv_d).then_inc(piw_in, 16)
            sp.dma_start(oiw, oiw_d).then_inc(piw_in, 16)
            sp.wait_ge(proj_ps, B)
            sp.wait_ge(x_done, B)
            for s in range(2):
                sp.dma_start(pat[:, s], pat_d[s]).then_inc(pat_in[s], 16)
            sp.dma_start(awt, attn_d[1, :, 0:2694]).then_inc(attn_in, 16)
            sp.dma_start(gate, gate_d).then_inc(gate_in, 16)
            with sp.Fori(1, 4) as t:
                for s in range(2):
                    sp.wait_ge(ia_ps, t * 16 + (8 * s - 8))
                    sp.dma_start(pat[:, s], pat_d[t * 2 + s]).then_inc(pat_in[s], 16)
            sp.wait_ge(pr_ps, 1)
            sp.dma_start(opt, op_d).then_inc(op_in, 16)
            sp.wait_ge(oa_ps, 1)
            for w, d in zip(shared_w, (sg_d, su_d, sd_d)):
                sp.dma_start(w, d).then_inc(sw_in, 16)
            sp.wait_ge(x_done, 2 * B)
            for e in range(2):
                for w, d, arrived in zip(expert_w[e], (wg_d, wu_d, wd_d), (egu_in, egu_in, ed_in)):
                    sp.dma_start(w, d[e]).then_inc(arrived[e], 16)

            def expert_traffic(t, q, load):
                s = q % 2
                if load:
                    sp.wait_ge(gu_ps, t * 8 + 2 * (B + q + 1))
                    for w, d in zip(expert_w[s][0:2], (wg_d, wu_d)):
                        sp.dma_start(w, d[t * 4 + (q + 2)]).then_inc(egu_in[s], 16)
                    sp.wait_ge(down_ps, t * 4 + (B + q + 1))
                    sp.dma_start(expert_w[s][2], wd_d[t * 4 + (q + 2)]).then_inc(ed_in[s], 16)
                sp.wait_ge(down_done, t * 4 + (B + q + 1))
                for g in range(4):
                    sp.dma_start(EO[32 * q:32 * q + 32, t, g::4, :], eo[32 * g:32 * g + 32, s, :, :]
                                 ).then_inc(eo_moved[s], 16)

            with sp.Fori(0, 3) as t:
                for q in range(4):
                    expert_traffic(t, q, True)
            for q in range(4):
                expert_traffic(3, q, q < 2)
            for b in range(B):
                sp.wait_ge(y_done, b + 1)
                sp.dma_start(out_d.rearrange("(t p) d -> p t d", p=P)[:, 2 * b:2 * b + 2, :],
                             x_sb[:, 2 * b:2 * b + 2, :]).then_inc(out_done, 16)
            sp.wait_ge(out_done, 16 * B)

        @block.gpsimd
        def _(pool):
            pool.memset(mhalf, -0.5).then_inc(cleared, 1)
            pool.memset(eps, EPS).then_inc(cleared, 1)
            pool.memset(mpad_s, 0.0).then_inc(cleared, 1)
            pool.memset(Vpad.rearrange("p s h m -> p (s h m)"), 0.0).then_inc(cleared, 1)
            pool.memset(PT.rearrange("p h q -> p (h q)"), 0.0).then_inc(cleared, 1)
            pool.memset(kbd[0:GR].rearrange("p s h k -> p (s h k)"), 0.0).then_inc(cleared, 1)
            pool.memset(wpad_s, 0.0).then_inc(cleared, 1)

            def inv_std(n):
                pool.wait_ge(mv_done, n * 2 + 2)
                pool.tensor_tensor(veps, mv[:, :, 1], eps, ALU.add).then_inc(veps_done, 1)
                pool.wait_ge(veps_done, n + 1)
                pool.tensor_tensor(rstd, veps, mhalf, ALU.pow).then_inc(rstd_done, 1)

            def inv_std_second(i, b):
                pool.wait_ge(fmv_done, i + 1)
                if not (isinstance(i, int) and i == 0):
                    pool.wait_ge(frstd_done, i)
                pool.tensor_tensor(fveps, fmv[:, tiles(b), 1], eps, ALU.add).then_inc(fveps_done, 1)
                pool.wait_ge(fveps_done, i + 1)
                pool.tensor_tensor(frstd[:, tiles(b)], fveps, mhalf, ALU.pow).then_inc(frstd_done, 1)

            def block_keys(b, s):
                for g in range(NG):
                    keys = kT[0:GR, g, ktslice(b)].unsqueeze(1).to_broadcast([GR, GH, SK])
                    own = hmask[0:GR, :].unsqueeze(2).to_broadcast([GR, GH, SK])
                    pool.tensor_tensor(kbd[0:GR, s, GH * g:GH * g + GH, :], keys, own, ALU.mult)
                    pool.tensor_tensor(kbr[0:GR, GH * g:GH * g + GH, :], keys, own, ALU.mult)
                for a in range(2):
                    ins = pool.tensor_copy(
                        Vpad[0:SK, s].rearrange("p (h a) m -> p h a m", a=2)[:, :, a, HD * a:HD * a + HD],
                        V[0:SK, bass.ds(b, 1), :].rearrange("p o (h a m) -> p (o h) a m", a=2, m=HD)[:, :, a, :])
                ins.then_inc(kbd_done, 1)

            def rotary_a(b):
                pool.wait_ge(q_raw, b + 1)
                pool.tensor_tensor(qrot[0:GR], qraw[0:GR], ropeA[0:GR].unsqueeze(1).to_broadcast([GR, NG, S]),
                                   ALU.mult).then_inc(q_mulA, 1)

            pool.wait_ge(cleared, 7)
            for layer in range(2):
                inv_std(8 * layer)
                inv_std(8 * layer + 1)
                if layer == 0:
                    pool.wait_ge(const_in, 32)
                if layer == 1:
                    for j in range(6):
                        g, nh = divmod(j, 2)
                        pool.wait_ge(k_raw, j + 1)
                        pool.tensor_tensor(
                            kT[0:GR, g, 308 * nh:308 * nh + 308].rearrange("p (b k) -> p b k", k=SK),
                            kraw[0:GR, g, 308 * nh:308 * nh + 308].rearrange("p (b k) -> p b k", k=SK),
                            ropeA[0:GR, 0:SK].unsqueeze(1).to_broadcast([GR, 4, SK]), ALU.mult).then_inc(k_mulA, 1)
                pool.wait_ge(kT_done, 6 * (layer + 1))
                pool.wait_ge(v_done, B * (layer + 1))
                block_keys(0, 0)
                if layer == 1:
                    rotary_a(0)

                def step(i, b, s, first, last, ahead, layer=layer):
                    if last:
                        return
                    pool.wait_ge(rowmax_ps, i * 2 + 2)
                    block_keys(b + 1, 1 - s)
                    if ahead:
                        inv_std(i + 2)
                    if layer == 1:
                        rotary_a(b + 1)
                    if not first:
                        inv_std_second(i - 1, b - 1)
                steps(pool, layer, step)
                for b in range(B - 2, B):
                    inv_std_second(8 * layer + b, b)

        @block.scalar
        def _(act):
            act.wait_ge(const_in, 32)
            act.activation(tg, gates, ACT.Tanh).then_inc(tanh_done, 1)

            def copy_xt(n, out, bank=2):
                act.wait_ge(xt_ps, n + 1)
                act.activation(out, ps[:, bank, :].rearrange("p (c t) -> p c t", c=DC), ACT.Copy
                               ).then_inc(xt_done, 1)

            def q_out(i, s, layer):
                act.wait_ge(q_ps, i + 1)
                if layer == 0:
                    act.wait_ge(bqs_done, 1)
                for g in range(NG):
                    src = q_bank(g)
                    if layer == 0:
                        ins = act.activation(qT[0:GR, s, g, :], src, ACT.Identity, bias=bqs[0:GR, g:g + 1],
                                             scale=-0.25)
                    else:
                        ins = act.activation(qraw[0:GR, g, :], src, ACT.Identity, bias=bq[0:GR, g:g + 1], scale=1.0)
                ins.then_inc(q_done if layer == 0 else q_raw, 1)

            def round_q(i, s):
                act.wait_ge(q_done, i + 1)
                act.activation(qr[0:GR], qT[0:GR, s], ACT.Copy).then_inc(qr_done, 1)

            for layer in range(2):
                act.wait_ge(attn_in, 32 + 16 * layer)
                for j in range(6):
                    g, nh = divmod(j, 2)
                    act.wait_ge(k_ps, 6 * layer + j + 1)
                    dst = (kT if layer == 0 else kraw)[0:GR, g, 308 * nh:308 * nh + 308]
                    act.activation(dst, ps[0:GR, 1 + j, 0:308], ACT.Identity, bias=bk[0:GR, g:g + 1], scale=1.0
                                   ).then_inc(kT_done if layer == 0 else k_raw, 1)
                copy_xt(16 * layer, xnT_b)
                q_out(8 * layer, 0, layer)
                round_q(8 * layer, 0)

                def step(i, b, s, first, last, ahead, layer=layer):
                    if not last:
                        copy_xt(i + (8 * layer + 1), xnT_b)
                    for t in range(2):
                        act.wait_ge(mT_ps, i * 2 + (t + 1))
                        act.activation(qT[GR:P, s, :, P * t:P * t + P],
                                       ps[GR:P, 3 + t, 0:NG * P].rearrange("p (g q) -> p g q", g=NG), ACT.Copy
                                       ).then_inc(mT_done, 1)
                    if not last:
                        q_out(i + 1, 1 - s, layer)
                    for k in range(4):
                        act.wait_ge(score_ps, i * 4 + (k + 1))
                        a = 3 + 2 * (k % 2)
                        act.activation(PT[0:SK, 4 * k:4 * k + 4, :],
                                       ps[0:SK, a:a + 2, :].rearrange("p a (h q) -> p (a h) q", h=2), ACT.Exp
                                       ).then_inc(exp_done, 1)
                    if not last:
                        round_q(i + 1, 1 - s)
                steps(act, layer, step)

                if layer == 1:
                    break
                with act.Fori(0, B // 2) as t:
                    for j in range(2):
                        b = t * 2 + j
                        copy_xt(b + 8, xnT[:, :, bslice(b)], bank=1 + j)
                with act.Fori(0, 4) as t:
                    for u in range(4):
                        for g in range(4):
                            ch = t * 4 + u
                            act.wait_ge(ia_ps, t * 16 + (4 * u + g + 1))
                            for h in range(2):
                                part = ps[:, 3 + g, S * h:S * h + S]
                                ins = act.activation(part, part, ACT.Gelu,
                                                     accum_out=acts[:, bass.ds(ch * 8 + (2 * g + h), 1)])
                            ins.then_inc(ia_done[g], 1)
                act.wait_ge(pr_ps, 1)
                act.activation(pcp, ps[:, 2:4, :].rearrange("p a n -> p (a n)"), ACT.Copy).then_inc(pr_copied, 1)
                act.wait_ge(pr_cols, 1)
                act.activation(acts[:, 0:64], ps[:, 4, 0:64], ACT.Gelu).then_inc(pa_done, 1)
                act.wait_ge(sm_dve, 5)
                act.activation(gtm[:, 0:64], gtm[:, 0:64], ACT.Exp).then_inc(sm_act, 1)
                act.wait_ge(oa_ps, 1)
                act.activation(acts, ps[:, 4, 0:128], ACT.Gelu).then_inc(oa_done, 1)
                act.wait_ge(op_ps, 1)
                act.activation(outp, ps[:, 5, 0:D], ACT.Copy).then_inc(op_copied, 1)

            def gelu_half(u, f):
                act.wait_ge(gu_ps, u * 2 + (f + 1))
                act.activation(hgl[:, f, :], ps[:, 2 * f, :], ACT.Gelu).then_inc(gelu_done, 1)

            for b in range(B):
                copy_xt(24 + b, xnT[:, :, bslice(b)], bank=6)
                if b > 0:
                    gelu_half((b - 1) // 2, (b - 1) % 2)
                act.wait_ge(logT_ps, b + 1)
                act.activation(logT, ps[0:E, 7, 0:S], ACT.Copy).then_inc(logT_done, 1)
            gelu_half(3, 1)
            act.wait_ge(rt_dve, 2)
            act.activation(probs, probs, ACT.Exp).then_inc(rt_act, 1)
            for h in range(8, 16):
                gelu_half(h // 2, h % 2)
            for b in range(B):
                lo = 4 * (b % 2)
                for c in range(DC):
                    act.wait_ge(disp_ps, DC * b + c + 1)
                    act.activation(XT[:, :, c, 32 * b:32 * b + 32],
                                   ps[:, lo + c, :].rearrange("p (e s) -> p e s", e=E), ACT.Copy).then_inc(disp_done, 1)
                act.wait_ge(gwt_ps, b + 1)
                act.activation(GWT[:, b].rearrange("p g t -> p (g t)"),
                               ps[:, lo + 2:lo + 4, :].rearrange("p a n -> p (a n)"), ACT.Copy
                               ).then_inc(gwt_done, 1)

            def expert_out(u, s, reused):
                act.wait_ge(down_ps, u + 1)
                if reused is not None:
                    act.wait_ge(eo_moved[s], reused)
                act.activation(eo[:, s], ps[:, 4 + s, :].rearrange("p (t d) -> p t d", t=2), ACT.Copy
                               ).then_inc(down_done, 1)

            def four_experts(t, first):
                for q in range(4):
                    u = t * 4 + (B + q)
                    gelu_half(u, 0)
                    gelu_half(u, 1)
                    if not (first and q == 0):
                        expert_out(u - 1, (q - 1) % 2, None if first and q < 3 else t * 128 + 64 * ((q - 1) // 2))

            four_experts(0, True)
            with act.Fori(1, E // 4) as t:
                four_experts(t, False)
            expert_out(B + E - 1, 1, 64 * (E // 2 - 1))

        @block.tensor
        def _(pe):
            def mm(out, lhsT, rhs, start=True, stop=True):
                return pe.matmul(out, lhsT, rhs, start=start, stop=stop, skip_group_check=True)

            def transpose_xn(n, src, bank=2):
                pe.wait_ge(xn_done, n * 2 + 2)
                for c in range(DC):
                    for t in range(2):
                        at = (c * 2 + t) * P
                        ins = pe.transpose(ps[:, bank, at:at + P], src[:, t, P * c:P * c + P], ident)
                ins.then_inc(xt_ps, 1)

            def project_q(g):
                for c in range(DC):
                    ins = mm(q_bank(g), wq[:, c, g, :], xnT_b[:, c, :], c == 0, c == DC - 1)
                if g == NG - 1:
                    ins.then_inc(q_ps, 1)

            def swap_pairs(b):
                pe.wait_ge(q_raw, b + 1)
                for g in range(NG):
                    ins = mm(ps[0:GR, 1 + g // 2, S * (g % 2):S * (g % 2) + S], perm[0:GR, :], qraw[0:GR, g, :])
                ins.then_inc(q_perm, 1)

            def project_out(i):
                pe.wait_ge(attn_done, i * 2 + 2)
                for t in range(2):
                    for c in range(DC):
                        ins = mm(ps[:, 1, D * t:D * t + D], attnT[:, c, P * t:P * t + P], wp[:, c, :],
                                 c == 0, c == DC - 1)
                ins.then_inc(proj_ps, 1)

            pe.wait_ge(const_in, 32)
            for layer in range(2):
                pe.wait_ge(attn_in, 32 + 16 * layer)
                if layer == 1:
                    pe.wait_ge(x2_done, B)
                for j in range(6):
                    g, nh = divmod(j, 2)
                    for c in range(DC):
                        ins = mm(ps[0:GR, 1 + j, 0:308], wk[:, c, g, :], ctxT[:, c, 308 * nh:308 * nh + 308],
                                 c == 0, c == DC - 1)
                    ins.then_inc(k_ps, 1)
                for b in range(B):
                    bank = 7 if b % 2 == 0 else 0
                    if b >= 2:
                        pe.wait_ge(v_done, 8 * layer + b - 1)
                    for c in range(DC):
                        ins = mm(ps[0:SK, bank, 0:D], ctxT[:, c, SK * b:SK * b + SK], wv[:, c, :],
                                 c == 0, c == DC - 1)
                    ins.then_inc(v_ps, 1)
                if layer == 1:
                    for j in range(6):
                        g, nh = divmod(j, 2)
                        pe.wait_ge(k_raw, j + 1)
                        mm(ps[0:GR, 1 + j, 0:308], perm[0:GR, :], kraw[0:GR, g, 308 * nh:308 * nh + 308]
                           ).then_inc(k_perm, 1)
                    pe.wait_ge(prepared, 6)
                    pe.wait_ge(v_done, 8 * layer + 7)
                    mm(ps[:, 7, 0:S], ones_b[0:SK, :], seen[0:SK, :]).then_inc(any_ps, 1)
                    pe.wait_ge(any_done, 1)
                pe.wait_ge(kT_done, 6 * (layer + 1))
                transpose_xn(16 * layer, xn[:, 0])
                pe.wait_ge(xt_done, 16 * layer + 1)
                for g in range(NG):
                    project_q(g)
                if layer == 1:
                    swap_pairs(0)
                pe.wait_ge(v_done, 8 * layer + 8)
                pe.wait_ge(prepared, 6)
                pe.wait_ge(kone_in, 32)
                pe.wait_ge(cleared, 7)

                def step(i, b, s, first, last, ahead, layer=layer):
                    n = i + 8 * layer

                    def row_scores(t):
                        for g in range(NG):
                            bank = (3, 4, 5)[g] if t == 0 else (6, 7, 0)[g]
                            out = ps[:, bank, 0:GH * SK]
                            ins = mm(out, qr[0:GR, g, P * t:P * t + P],
                                     kbr[0:GR, GH * g:GH * g + GH, :].rearrange("p h k -> p (h k)"),
                                     True, layer == 0)
                            if layer == 1:
                                ins = mm(out.rearrange("p (h k) -> p h k", k=SK), ident_b,
                                         maskb[:, t, 0:SK].unsqueeze(1).to_broadcast([P, GH, SK]), False, True)
                        ins.then_inc(rowmax_ps, 1)

                    pe.wait_ge(q_done, i + 1)
                    if not last:
                        transpose_xn(n + 1, xn[:, 1 - s])
                    pe.wait_ge(qr_done, i + 1)
                    pe.wait_ge(kbd_done, i + 1)
                    row_scores(0)
                    if not first:
                        pe.wait_ge(attn_done, i * 2)
                    row_scores(1)
                    if not first:
                        project_out(i - 1)
                    for t in range(2):
                        pe.wait_ge(rowmax_done, i * 2 + (t + 1))
                        for g in range(NG):
                            ins = pe.transpose(ps[:, 3 + t, P * g:P * g + P], mpad[:, t, g, :], ident)
                        ins.then_inc(mT_ps, 1)
                        if not last:
                            if t == 0:
                                pe.wait_ge(xt_done, n + 2)
                                project_q(0)
                                project_q(1)
                            else:
                                project_q(2)

                    def key_scores(k):
                        for m in range(4):
                            h = 4 * k + m
                            out = ps[0:SK, 3 + 2 * (k % 2) + m // 2, S * (m % 2):S * (m % 2) + S]
                            ins = mm(out, kbd[:, s, h, :], qT[:, s, h // GH, :], True, layer == 0)
                            if layer == 1:
                                ins = mm(out, ident_b[:, 0:SK], maskTb, False, True)
                        ins.then_inc(score_ps, 1)

                    def weigh_values(c):
                        bank = 7 if c == 0 else 0
                        for den in range(2):
                            for a in range(2):
                                for j in range(4):
                                    h = 8 * c + 2 * j + a
                                    lhsT = par[:, a, :] if den else Vpad[:, s, h, :]
                                    ins = mm(ps[32 * j:32 * j + 32, bank, S * den:S * den + S], lhsT, PT[:, h, :],
                                             a == 0, a == 1)
                        ins.then_inc(pv_ps, 1)

                    pe.wait_ge(mT_done, i * 2 + 2)
                    key_scores(0)
                    if not last:
                        pe.wait_ge(q_done if layer == 0 else q_raw, (i if layer == 0 else b) + 2)
                    key_scores(1)
                    pe.wait_ge(exp_done, i * 4 + 1)
                    key_scores(2)
                    if layer == 1 and not last:
                        if not first:
                            pe.wait_ge(bias_done, i)
                        swap_pairs(b + 1)
                    pe.wait_ge(exp_done, i * 4 + 2)
                    weigh_values(0)
                    key_scores(3)
                    pe.wait_ge(exp_done, i * 4 + 4)
                    weigh_values(1)
                    if last:
                        project_out(i)
                steps(pe, layer, step)
                if layer == 1:
                    break

                with pe.Fori(0, B // 2) as t:
                    for j in range(2):
                        b = t * 2 + j
                        pe.wait_ge(xt_done, b + 7)
                        if j == 0:
                            pe.wait_ge(x_done, B)
                        transpose_xn(b + 8, xn[:, j], bank=1 + j)
                pe.wait_ge(xt_done, 2 * B)

                def four_chunks(t, first):
                    for u in range(4):
                        if u % 2 == 0:
                            pe.wait_ge(pat_in[u // 2], t * 16 + 16)
                        for g in range(4):
                            if not (first and u == 0):
                                pe.wait_ge(ia_done[g], t * 4 + u)
                            for c in range(DC):
                                ins = mm(ps[:, 3 + g, :], pat[:, u // 2, u % 2, c, :], xnT[:, c, 512 * g:512 * g + 512],
                                         c == 0, c == DC - 1)
                            ins.then_inc(ia_ps, 1)

                four_chunks(0, True)
                with pe.Fori(1, 4) as t:
                    four_chunks(t, False)

                def top_k(j, chunks):
                    n, base = 8 * chunks, (0, 20, 39)[j]

                    def count(first, more):
                        for half in range(2):
                            pe.wait_ge(tk_cnt, first + half)
                            if more and half == 0:
                                mm(ps[:, 7, 0:P], ones_b, cntb.unsqueeze(1).to_broadcast([P, RADIX, 8]), True, False)
                            for c in range(half * chunks // 2, (half + 1) * chunks // 2):
                                ins = mm(ps[:, 7, 0:P], ones_b, reached[:, c, :], c == 0 and not more, c == chunks - 1)
                        ins.then_inc(tk_tot, 1)

                    with pe.Fori(0, DIGITS) as it:
                        count(it * 2 + (base + 1), False)
                    with pe.Fori(0, DIGITS) as it:
                        count(it * 2 + (base + 10), True)
                    pe.wait_ge(tk_cnt, base + 18)
                    mm(ps[:, 7, 0:n], ones_b, cntb.unsqueeze(1).to_broadcast([P, chunks, 8]), True, False)
                    pe.wait_ge(tk_cnt, base + 19)
                    mm(ps[:, 7, 0:n], tri_b, eqb[:, 0:n], False, False)
                    for d in range(1, chunks):
                        ins = mm(ps[:, 7, 8 * d:n], ones_b, eqb[:, 0:n - 8 * d], False, d == chunks - 1)
                    ins.then_inc(tk_tot, 1)

                top_k(0, 16)
                pe.wait_ge(tk_cnt, 20)
                pe.wait_ge(piw_in, 48)
                for c in range(16):
                    g = c % 4
                    for a in range(2):
                        ins = mm(ps[32 * g:32 * g + 32, 2 + a, :], wpad[:, c, :], piw[:, c, 512 * a:512 * a + 512],
                                 c < 4, c >= 12)
                ins.then_inc(pr_ps, 1)
                pe.wait_ge(pr_copied, 1)
                for c in range(8):
                    ins = mm(ps[:, 4, 8 * c:8 * c + 8], pcp[:, P * c:P * c + P], sel8)
                ins.then_inc(pr_cols, 1)
                top_k(1, 8)
                pe.wait_ge(sm_dve, 1)
                pe.transpose(ps[0:8, 6, 0:P], pmax, ident).then_inc(sm_pe, 1)
                pe.wait_ge(sm_dve, 3)
                mm(ps[:, 6, 128:136], onesf[0:8, :], mxd[0:8, :]).then_inc(sm_pe, 1)
                pe.wait_ge(sm_dve, 7)
                mm(ps[:, 6, 136:144], onesf, dsum).then_inc(sm_pe, 1)
                pe.wait_ge(sm_dve, 9)
                for c in range(8):
                    ins = mm(ps[:, 5, 0:8], pvt[:, c, :], selm[:, 8 * c:8 * c + 8], c == 0, c == 7)
                ins.then_inc(agg_ps, 1)
                pe.wait_ge(agg_done, 1)
                for c in range(16):
                    ins = mm(ps[:, 4, 8 * c:8 * c + 8], oiw[:, P * c:P * c + P], aggT)
                ins.then_inc(oa_ps, 1)
                top_k(2, 16)
                pe.wait_ge(tk_cnt, 59)
                pe.wait_ge(op_in, 16)
                for c in range(16):
                    g = c % 4
                    ins = mm(ps[32 * g:32 * g + 32, 5, 0:D], wpad[:, c, :], opt[:, c, :], c < 4, c >= 12)
                ins.then_inc(op_ps, 1)
                pe.wait_ge(op_copied, 1)
                for b in range(B):
                    if b >= 2:
                        pe.wait_ge(x2_done, b - 1)
                    mm(ps[:, 1 + b % 2, 0:D], sel8[:, b:b + 1].to_broadcast([P, P]), outp).then_inc(op_rows, 1)

            def gate_up(u, f, w, rhs, first=False):
                if not first:
                    pe.wait_ge(h_done, u * 2 + (f - 1))
                for bank, m in ((2 * f, w[0]), (2 * f + 1, w[1])):
                    for a in range(2):
                        at = P * (2 * f + a)
                        for c in range(DC):
                            ins = mm(ps[:, bank, S * a:S * a + S], m[:, c, at:at + P], rhs(c), c == 0, c == DC - 1)
                ins.then_inc(gu_ps, 1)

            def down(u, s, w, first=False):
                pe.wait_ge(h_done, u * 2 + 2)
                if not first:
                    pe.wait_ge(down_done, u)
                for t in range(2):
                    for f in range(FC):
                        ins = mm(ps[:, 4 + s, D * t:D * t + D], hT[:, s, f, P * t:P * t + P], w[2][:, f, :],
                                 f == 0, f == FC - 1)
                ins.then_inc(down_ps, 1)

            def shared_half(h):
                u, f = h // 2, h % 2
                gate_up(u, f, shared_w, lambda c: xnT[:, c, S * u:S * u + S], u == 0)
                if f == 0 and u > 0:
                    down(u - 1, (u - 1) % 2, shared_w, u == 1)

            def logits_to_rows(b):
                pe.wait_ge(logT_done, b + 1)
                for t in range(2):
                    at = 256 + E * (2 * b + t)
                    ins = pe.transpose(ps[:, 7, at:at + E], logT[:, P * t:P * t + P], ident[0:E, 0:E])
                return ins

            pe.wait_ge(gate_in, 16)
            pe.wait_ge(x_done, 2 * B)
            for b in range(B):
                transpose_xn(24 + b, xn_all[:, 2 * b:2 * b + 2, :], bank=6)
                if b == 1:
                    pe.wait_ge(sw_in, 48)
                if b > 0:
                    shared_half(b - 1)
                    logits_to_rows(b - 1)
                pe.wait_ge(xt_done, 24 + b + 1)
                for c in range(DC):
                    ins = mm(ps[0:E, 7, 0:S], gate[:, c, :], xnT[:, c, S * b:S * b + S], c == 0, c == DC - 1)
                ins.then_inc(logT_ps, 1)
            shared_half(7)
            logits_to_rows(B - 1).then_inc(rt_pe, 1)

            shared_half(8)
            shared_half(9)
            pe.wait_ge(rt_dve, 5)
            for t in range(2):
                ins = pe.transpose(ps[:, 7, P * t:P * t + P], sc2[:, t, :], ident)
            ins.then_inc(rt_pe, 1)
            for h in range(10, 13):
                shared_half(h)
            pe.wait_ge(rt_dve, 18)
            for t in range(2):
                ins = pe.transpose(ps[:, 7, P * t:P * t + P], posm[:, P * t:P * t + P], ident)
            ins.then_inc(rt_pe, 1)
            for h in range(13, 16):
                shared_half(h)
            down(B - 1, 1, shared_w)

            for b in range(B):
                lo = 4 * (b % 2)
                pe.wait_ge(g_done, 2 * b + 2)
                if b == 0:
                    pe.wait_ge(h_done, 2 * B)
                elif b == 1:
                    pe.wait_ge(down_done, B)
                else:
                    pe.wait_ge(disp_done, DC * (b - 1))
                for c in range(DC):
                    for t in range(2):
                        ins = mm(ps[:, lo + c, :], xn_all[:, 2 * b + t, P * c:P * c + P], G[b % 2][:, t, :],
                                 t == 0, t == 1)
                    ins.then_inc(disp_ps, 1)
                pe.wait_ge(gw_done, 2 * b + 2)
                if b >= 2:
                    pe.wait_ge(gwt_done, b - 1)
                for g in range(4):
                    for t in range(2):
                        at = S * (g % 2) + P * t
                        ins = pe.transpose(ps[:, lo + 2 + g // 2, at:at + P], GW[b % 2][:, t, P * g:P * g + P], ident)
                ins.then_inc(gwt_ps, 1)
            pe.wait_ge(disp_done, DC * B)
            pe.wait_ge(gwt_done, B)

            def four_experts(t, first):
                for q in range(4):
                    s = q % 2
                    u = t * 4 + (B + q)
                    pe.wait_ge(egu_in[s], t * 64 + 32 * (q // 2 + 1))

                    def rhs(c, q=q):
                        return XT[:, t * 4 + q, c, :]
                    gate_up(u, 0, expert_w[s], rhs)
                    if not (first and q == 0):
                        pe.wait_ge(ed_in[1 - s], t * 32 + 16 * ((q - 1) // 2 + 1))
                        down(u - 1, 1 - s, expert_w[1 - s])
                    gate_up(u, 1, expert_w[s], rhs)

            four_experts(0, True)
            with pe.Fori(1, E // 4) as t:
                four_experts(t, False)
            pe.wait_ge(ed_in[1], 16 * E // 2)
            down(B + E - 1, 1, expert_w[1])
            for s in range(2):
                pe.wait_ge(eo_moved[s], 64 * E // 2)
            pe.wait_ge(down_done, B + E)
            for b in range(B):
                if b >= 2:
                    pe.wait_ge(y_done, b - 1)
                for t in range(2):
                    for g in range(4):
                        ins = mm(ps[:, 6 + b % 2, D * t:D * t + D], GWT[:, b, g, P * t:P * t + P], EO[:, g, b, :],
                                 g == 0, g == 3)
                ins.then_inc(comb_ps, 1)

        @block.vector
        def _(dve):
            dve.wait_ge(const_in, 32)
            dve.tensor_copy(ones_b, onesf).then_inc(prepared, 1)
            dve.tensor_copy(tri_b, cst[:, C_TRI:C_PAR]).then_inc(prepared, 1)
            dve.tensor_copy(ident_b, ident).then_inc(prepared, 1)

            def stats(n, b):
                for t in range(2):
                    dve.bn_stats(bn[:, t, :], x_sb[:, b * 2 + t, :]).then_inc(stat_done, 1)
                dve.wait_ge(stat_done, n * 2 + 2)
                dve.memset(scrap, 0.0)
                for t in range(2):
                    dve.bn_aggr(mv[:, t, :], bn[:, t, :]).then_inc(mv_done, 1)

            def normalise(i, b, out):
                dve.wait_ge(rstd_done, i + 1)
                for t in range(2):
                    dve.tensor_scalar(out[:, t, :], x_sb[:, b * 2 + t, :], mv[:, t, 0:1], rstd[:, t:t + 1],
                                      ALU.subtract, ALU.mult).then_inc(xn_done, 1)

            def stats_second(i, b):
                dve.wait_ge(x_done, i + 1)
                dve.memset(scrap, 0.0)
                for t in range(2):
                    dve.bn_stats(fbn[:, t, :], x_sb[:, b * 2 + t, :]).then_inc(fstat_done, 1)
                dve.wait_ge(fstat_done, i * 2 + 2)
                dve.memset(scrap, 0.0)
                for t in range(2):
                    dve.bn_aggr(fag[:, t, :], fbn[:, t, :]).then_inc(faggr_done, 1)
                dve.wait_ge(faggr_done, i * 2 + 2)
                dve.tensor_copy(fmv[:, tiles(b), :], fag).then_inc(fmv_done, 1)

            def normalise_second(i, b, out):
                dve.wait_ge(frstd_done, i + 1)
                for t in range(2):
                    dve.tensor_scalar(out[:, t, :], x_sb[:, 2 * b + t, :], fmv[:, 2 * b + t, 0:1],
                                      frstd[:, 2 * b + t:2 * b + t + 1], ALU.subtract, ALU.mult).then_inc(xn_done, 1)

            def add_projection(i, b, layer):
                dve.wait_ge(proj_ps, i + 1)
                dve.tensor_tensor(ytmp.rearrange("p (t d) -> p t d", t=2),
                                  ps[:, 1, :].rearrange("p (t d) -> p t d", t=2),
                                  bp.unsqueeze(1).to_broadcast([P, 2, D]), ALU.add).then_inc(bias_done, 1)
                dve.wait_ge(bias_done, i + 1)
                xt = x_sb[:, tiles(b), :]
                dve.scalar_tensor_tensor(out=xt, in0=ytmp.rearrange("p (t d) -> p t d", t=2),
                                         scalar=tg[:, layer:layer + 1], in1=xt, op0=ALU.mult, op1=ALU.add
                                         ).then_inc(x_done, 1)

            def rotary_b(i, b, s):
                dve.wait_ge(q_perm, b + 1)
                dve.tensor_tensor(qT[0:GR, s], ps_all[0:GR, 1:3, :].rearrange("p a n -> p (a n)")[:, 0:NG * S]
                                  .rearrange("p (g q) -> p g q", g=NG),
                                  ropeB[0:GR].unsqueeze(1).to_broadcast([GR, NG, S]), ALU.mult).then_inc(q_mulB, 1)
                dve.wait_ge(q_mulA, b + 1)
                dve.wait_ge(q_mulB, b + 1)
                dve.tensor_tensor(qT[0:GR, s], qT[0:GR, s], qrot[0:GR], ALU.add).then_inc(q_done, 1)

            for layer in range(2):
                if layer == 0:
                    dve.wait_ge(x_in, 32)
                dve.wait_ge(attn_in, 32 + 16 * layer)
                if layer == 0:
                    dve.tensor_scalar(bqs[0:GR], bq[0:GR], -0.25, None, ALU.mult).then_inc(bqs_done, 1)
                else:
                    dve.wait_ge(x2_done, B)
                for b in range(2):
                    stats(8 * layer + b, b)
                    normalise(8 * layer + b, b, xn[:, b])
                if layer == 0:
                    dve.wait_ge(cleared, 7)
                    dve.wait_ge(tanh_done, 1)
                for b in range(B):
                    dve.wait_ge(v_ps, 8 * layer + b + 1)
                    dve.tensor_tensor(V[0:SK, b, :], ps[0:SK, 7 if b % 2 == 0 else 0, 0:D], bv[0:SK], ALU.add
                                      ).then_inc(v_done, 1)
                if layer == 0:
                    dve.wait_ge(mask_in, 64)
                    dve.tensor_scalar(maskb[:, :, 0:SK], mask_u[:, :, 0:SK], MASKED, None, ALU.mult).then_inc(prepared, 1)
                    dve.tensor_scalar(maskTb, maskT_u, MASKED, None, ALU.mult).then_inc(prepared, 1)
                    dve.tensor_scalar(seen, maskT_u, -1.0, 1.0, ALU.mult, ALU.add).then_inc(prepared, 1)
                else:
                    for j in range(6):
                        g, nh = divmod(j, 2)
                        dve.wait_ge(k_perm, j + 1)
                        buf = rden[0:GR, 0:308].rearrange("p (b k) -> p b k", k=SK)
                        dve.tensor_tensor(buf, ps[0:GR, 1 + j, 0:308].rearrange("p (b k) -> p b k", k=SK),
                                          ropeB[0:GR, 0:SK].unsqueeze(1).to_broadcast([GR, 4, SK]), ALU.mult
                                          ).then_inc(k_mulB, 1)
                        dve.wait_ge(k_mulA, j + 1)
                        dve.wait_ge(k_mulB, j + 1)
                        kt = kT[0:GR, g, 308 * nh:308 * nh + 308]
                        dve.tensor_tensor(kt, kt, rden[0:GR, 0:308], ALU.add).then_inc(kT_done, 1)
                        dve.wait_ge(kT_done, 6 + j + 1)
                    dve.wait_ge(any_ps, 1)
                    dve.tensor_scalar(anyv, ps[:, 7, 0:S], 1.0, None, ALU.min).then_inc(any_done, 1)
                    rotary_b(8, 0, 0)

                def step(i, b, s, first, last, ahead, layer=layer):
                    n = i + 8 * layer

                    def row_max(t, banks):
                        lo, g0 = banks
                        k = len(range(g0, NG)) if t == 0 else (2 if g0 == 0 else 1)
                        src = ps[:, lo:lo + k, 0:GH * SK].rearrange("p g (h k) -> p g h k", k=SK)
                        return dve.tensor_reduce(mpad[:, t, g0:g0 + k, GR:GR + GH], src, AX, ALU.max, negate=True)

                    dve.wait_ge(rowmax_ps, i * 2 + 1)
                    row_max(0, (3, 0)).then_inc(rowmax_done, 1)
                    dve.wait_ge(rowmax_ps, i * 2 + 2)
                    row_max(1, (6, 0))
                    row_max(1, (0, 2)).then_inc(rowmax_done, 1)
                    if not first:
                        add_projection(i - 1, b - 1, layer)
                    if ahead:
                        stats(i + 2, b + 2)
                        dve.wait_ge(xt_ps, n + 1)
                        normalise(i + 2, b + 2, xn[:, s])
                    if not first:
                        stats_second(i - 1, b - 1)
                    if layer == 1 and not last:
                        rotary_b(i + 1, b + 1, 1 - s)
                    for c in range(DC):
                        bank = 7 if c == 0 else 0
                        rd = rden[:, S * c:S * c + S]
                        dve.wait_ge(pv_ps, i * 2 + (c + 1))
                        dve.reciprocal(rd, ps[:, bank, S:2 * S]).then_inc(rden_done, 1)
                        if layer == 0:
                            dve.wait_ge(rden_done, i * 2 + (c + 1))
                        else:
                            dve.wait_ge(rden_done, b * 4 + (2 * B + 2 * c + 1))
                            dve.tensor_tensor(rd, rd, anyv, ALU.mult).then_inc(rden_done, 1)
                            dve.wait_ge(rden_done, b * 4 + (2 * B + 2 * c + 2))
                        dve.tensor_tensor(attnT[:, c, :], ps[:, bank, 0:S], rd, ALU.mult).then_inc(attn_done, 1)
                    if last:
                        add_projection(i, b, layer)
                steps(dve, layer, step)
                dve.wait_ge(x_done, B * (layer + 1))
                stats_second(8 * layer + B - 1, B - 1)
                if layer == 1:
                    break

                for b in range(B):
                    dve.wait_ge(xt_ps, b + 7)
                    normalise_second(b, b, xn[:, b % 2])

                count = [0]

                def link(ins):
                    count[0] += 1
                    ins.then_inc(tk_step, 1)
                    dve.wait_ge(tk_step, count[0])

                def top_k(j, data, chunks, k, out):
                    n, tot = 8 * chunks, 9 * j
                    key_, flip_, hi_, lo_, tied_, above_, lower_, eq_, out_ = (
                        a[:, 0:n] for a in (key, flip, khi, klo, tied, above, above_lo, eqb, out))

                    def per_batch(a):
                        return a.unsqueeze(1).to_broadcast([P, chunks, 8])

                    def chunked(a):
                        return a.rearrange("p (c b) -> p c b", b=8)

                    def sum_chunks(src):
                        with nc.allow_low_precision(reason="counts up to 16 are exact in bfloat16"):
                            dve.tensor_reduce(cntb, src.rearrange("p (c b) -> p b c", b=8), AX, ALU.add
                                              ).then_inc(tk_cnt, 1)

                    link(dve.tensor_scalar(key_, data, 0.0, None, ALU.add))
                    link(dve.tensor_scalar(flip_.bitcast(I32), key_.bitcast(I32), 31, -2 ** 31,
                                           ALU.arith_shift_right, ALU.bitwise_or))
                    link(dve.tensor_tensor(key_.bitcast(I32), key_.bitcast(I32), flip_.bitcast(I32), ALU.bitwise_xor))
                    halves = key_.bitcast(U16).rearrange("p (n two) -> p n two", two=2)
                    link(dve.tensor_copy(hi_, halves[:, :, 1]))
                    link(dve.tensor_copy(lo_, halves[:, :, 0]))

                    def search(keys, tot0):
                        link(dve.memset(thr, 0.0))
                        c0 = count[0]
                        half = chunks // 2
                        for it in range(DIGITS):
                            dve.scalar_tensor_tensor(out=chunked(level), in0=digit.unsqueeze(2).to_broadcast([P, RADIX, 8]),
                                                     scalar=float(RADIX ** (DIGITS - 1 - it)),
                                                     in1=thr.unsqueeze(1).to_broadcast([P, RADIX, 8]),
                                                     op0=ALU.mult, op1=ALU.add).then_inc(tk_step, 1)
                            dve.wait_ge(tk_step, it * 3 + (c0 + 1))
                            for h in range(2):
                                dve.tensor_tensor(reached[:, half * h:half * h + half, :].rearrange("p c (j b) -> p c j b", b=8),
                                                  chunked(keys)[:, half * h:half * h + half, :].unsqueeze(2)
                                                  .to_broadcast([P, half, RADIX, 8]),
                                                  chunked(level).unsqueeze(1).to_broadcast([P, half, RADIX, 8]),
                                                  ALU.is_ge).then_inc(tk_cnt, 1)
                            dve.wait_ge(tk_tot, it + (tot0 + 1))
                            dve.scalar_tensor_tensor(out=met, in0=ps[:, 7, 0:P], scalar=float(k), in1=level,
                                                     op0=ALU.is_ge, op1=ALU.mult).then_inc(tk_step, 1)
                            dve.wait_ge(tk_step, it * 3 + (c0 + 2))
                            dve.tensor_reduce(thr, met.rearrange("p (j b) -> p b j", b=8), AX, ALU.max
                                              ).then_inc(tk_step, 1)
                            dve.wait_ge(tk_step, it * 3 + (c0 + 3))
                        count[0] += 3 * DIGITS

                    search(hi_, tot)
                    link(dve.tensor_tensor(chunked(above_), chunked(hi_), per_batch(thr), ALU.is_gt))
                    sum_chunks(above_)
                    link(dve.tensor_tensor(chunked(tied_), chunked(hi_), per_batch(thr), ALU.is_equal))
                    link(dve.tensor_tensor(lo_, lo_, tied_, ALU.mult))
                    search(lo_, tot + 4)
                    link(dve.tensor_tensor(chunked(lower_), chunked(lo_), per_batch(thr), ALU.is_gt))
                    link(dve.tensor_tensor(above_, above_, lower_, ALU.add))
                    sum_chunks(above_)
                    link(dve.tensor_tensor(chunked(eq_), chunked(lo_), per_batch(thr), ALU.is_equal))
                    dve.tensor_tensor(eq_, eq_, tied_, ALU.mult).then_inc(tk_cnt, 1)
                    dve.wait_ge(tk_tot, tot + 9)
                    link(dve.scalar_tensor_tensor(out=out_, in0=ps[:, 7, 0:n], scalar=float(k), in1=eq_,
                                                  op0=ALU.is_le, op1=ALU.mult))
                    link(dve.tensor_tensor(out_, out_, above_, ALU.add))

                for g in range(4):
                    dve.wait_ge(ia_done[g], 16)
                link(dve.tensor_scalar(acts, acts, 1.0 / S, None, ALU.mult))
                top_k(0, acts, 16, TOP_I, selm)
                chunk8 = "p (c b) -> p c b"
                dve.tensor_tensor(wpad[:, :, 0:8], acts.rearrange(chunk8, b=8), selm.rearrange(chunk8, b=8),
                                  ALU.mult).then_inc(tk_cnt, 1)
                dve.wait_ge(pa_done, 1)
                top_k(1, acts[:, 0:64], 8, TOP_P, selm)
                dve.tensor_reduce(pmax, acts[:, 0:64].rearrange("p (c b) -> p b c", b=8), AX, ALU.max
                                  ).then_inc(sm_dve, 1)
                dve.wait_ge(sm_pe, 1)
                dve.tensor_reduce(mx8[0:8, 0:1], ps[0:8, 6, 0:P], AX, ALU.max).then_inc(sm_dve, 1)
                dve.wait_ge(sm_dve, 2)
                dve.tensor_scalar(mxd[0:8, :], ident[0:8, 0:8], mx8[0:8, 0:1], None, ALU.mult).then_inc(sm_dve, 1)
                dve.wait_ge(sm_pe, 2)
                g64, s64 = gtm[:, 0:64].rearrange(chunk8, b=8), selm[:, 0:64].rearrange(chunk8, b=8)
                dve.tensor_copy(rs8, ps[:, 6, 128:136]).then_inc(sm_dve, 1)
                dve.wait_ge(sm_dve, 4)
                dve.tensor_tensor(g64, acts[:, 0:64].rearrange(chunk8, b=8), rs8.unsqueeze(1).to_broadcast([P, 8, 8]),
                                  ALU.subtract).then_inc(sm_dve, 1)
                dve.wait_ge(sm_act, 1)
                dve.tensor_tensor(s64, g64, s64, ALU.mult).then_inc(sm_dve, 1)
                dve.wait_ge(sm_dve, 6)
                dve.tensor_reduce(dsum, selm[:, 0:64].rearrange("p (c b) -> p b c", b=8), AX, ALU.add
                                  ).then_inc(sm_dve, 1)
                dve.wait_ge(sm_pe, 3)
                dve.reciprocal(rs8, ps[:, 6, 136:144]).then_inc(sm_dve, 1)
                dve.wait_ge(sm_dve, 8)
                dve.tensor_tensor(s64, s64, rs8.unsqueeze(1).to_broadcast([P, 8, 8]), ALU.mult).then_inc(sm_dve, 1)
                dve.wait_ge(agg_ps, 1)
                dve.tensor_copy(aggT, ps[:, 5, 0:8]).then_inc(agg_done, 1)
                dve.wait_ge(oa_done, 1)
                top_k(2, acts, 16, TOP_O, selm)
                dve.tensor_tensor(wpad[:, :, 0:8], acts.rearrange(chunk8, b=8), selm.rearrange(chunk8, b=8),
                                  ALU.mult).then_inc(tk_cnt, 1)
                for b in range(B):
                    dve.wait_ge(op_rows, b + 1)
                    xt = x_sb[:, 2 * b:2 * b + 2, :]
                    dve.scalar_tensor_tensor(out=xt, in0=ps[:, 1 + b % 2, 0:D].unsqueeze(1).to_broadcast([P, 2, D]),
                                             scalar=tg[:, 2:3], in1=xt, op0=ALU.mult, op1=ALU.add
                                             ).then_inc(x2_done, 1)

            for b in range(B):
                normalise_second(8 + b, b, xn_all[:, 2 * b:2 * b + 2, :])

            def gated(u, s, f):
                dve.wait_ge(gelu_done, u * 2 + (f + 1))
                dve.tensor_tensor(hT[:, s, 2 * f:2 * f + 2, :].rearrange("p f n -> p (f n)"), hgl[:, f, :],
                                  ps[:, 2 * f + 1, :], ALU.mult).then_inc(h_done, 1)

            def add_shared(u):
                dve.wait_ge(down_ps, u + 1)
                xt = x_sb[:, 2 * u:2 * u + 2, :]
                dve.scalar_tensor_tensor(out=xt, in0=ps[:, 4 + u % 2, :].rearrange("p (t d) -> p t d", t=2),
                                         scalar=tg[:, 3:4], in1=xt, op0=ALU.mult, op1=ALU.add
                                         ).then_inc(down_done, 1)

            def shared_half(h):
                gated(h // 2, h // 2 % 2, h % 2)
                if h % 2 == 0 and h > 0:
                    add_shared(h // 2 - 1)

            for h in range(8):
                shared_half(h)
            count = [0]

            def route(ins):
                count[0] += 1
                ins.then_inc(rt_dve, 1)
                dve.wait_ge(rt_dve, count[0])

            logits = ps[:, 7, 256:512].rearrange("p (t e) -> p t e", e=E)
            pr3 = probs.rearrange("p (t e) -> p t e", e=E)
            cols = cum[:, 0:16]
            dve.wait_ge(rt_pe, 1)
            route(dve.tensor_reduce(cols, logits, AX, ALU.max))
            route(dve.tensor_tensor(pr3, logits, cols.unsqueeze(2).to_broadcast([P, 16, E]), ALU.subtract))
            dve.wait_ge(rt_act, 1)
            route(dve.tensor_reduce(cols, pr3, AX, ALU.add))
            route(dve.reciprocal(cum[:, 16:32], cols))
            route(dve.tensor_tensor(sc2.rearrange("p t (b e) -> p b t e", b=B),
                                    probs.rearrange("p (b t e) -> p b t e", b=B, t=2),
                                    cum[:, 16:32].rearrange("p (b t) -> p b t", t=2).unsqueeze(3)
                                    .to_broadcast([P, B, 2, E]), ALU.mult))
            shared_half(8)
            shared_half(9)
            dve.wait_ge(rt_pe, 2)
            route(dve.tensor_copy(work, ps[:, 7, 0:S]))
            for j in range(CAP // 8):
                route(dve.max(mx8, work))
                route(dve.match_replace(work, mx8, work, -1.0))
                if j == 1:
                    shared_half(10)
            shared_half(11)
            route(dve.tensor_scalar(work, work, 0.0, None, ALU.is_lt))
            route(dve.memset(probs, 1.0))
            route(dve.tensor_tensor_scan(cum, probs, work, 0.0, ALU.mult, ALU.add))
            route(dve.tensor_tensor(posm, cum, work, ALU.mult))
            shared_half(12)
            dve.wait_ge(rt_pe, 3)
            route(dve.tensor_copy(posT, ps[:, 7, 0:S].rearrange("p (t m) -> p t m", t=2)))

            for h in range(13, 16):
                shared_half(h)
            add_shared(B - 1)

            for b in range(B):
                s = b % 2
                for t in range(2):
                    if b >= 2:
                        dve.wait_ge(disp_ps, DC * (b - 1))
                        dve.wait_ge(gw_done, 2 * (b - 1))
                    dve.tensor_tensor(G[s][:, t].rearrange("p (e s) -> p e s", e=E),
                                      iota.unsqueeze(1).to_broadcast([P, E, 32]),
                                      posT[:, t, E * b:E * b + E].unsqueeze(2).to_broadcast([P, E, 32]), ALU.is_equal
                                      ).then_inc(g_done, 1)
                for t in range(2):
                    dve.wait_ge(g_done, 2 * b + t + 1)
                    if b >= 2:
                        dve.wait_ge(gwt_ps, b - 1)
                    dve.tensor_tensor(GW[s][:, t].rearrange("p (e s) -> p e s", e=E),
                                      G[s][:, t].rearrange("p (e s) -> p e s", e=E),
                                      sc2[:, t, E * b:E * b + E].unsqueeze(2).to_broadcast([P, E, 32]), ALU.mult
                                      ).then_inc(gw_done, 1)

            with dve.Fori(0, E // 2) as t:
                for s in range(2):
                    for f in range(2):
                        gated(t * 2 + (B + s), s, f)
            for b in range(B):
                dve.wait_ge(comb_ps, b + 1)
                xt = x_sb[:, 2 * b:2 * b + 2, :]
                dve.scalar_tensor_tensor(out=xt, in0=ps[:, 6 + b % 2, :].rearrange("p (t d) -> p t d", t=2),
                                         scalar=tg[:, 3:4], in1=xt, op0=ALU.mult, op1=ALU.add).then_inc(y_done, 1)


def kernel(**inputs):
    import numpy as np
    from concourse import bacc
    from concourse.bass_utils import run_bass_kernel_spmd

    a = {k: np.asarray(v) for k, v in inputs.items()}
    f32 = np.float32

    def halves(w):
        return np.ascontiguousarray(w.reshape(DC, P, -1).transpose(1, 0, 2))

    def grouped(w):
        return np.pad(w, ((0, 0), (0, NG * GR - D)))

    def attention(wq, bq, wk, bk, wv, bv, wo, bo):
        cols = [halves(grouped(wq.T)).reshape(P, -1), halves(grouped(wk.T)).reshape(P, -1),
                halves(wv.T).reshape(P, -1), halves(wo.T).reshape(P, -1),
                np.broadcast_to(bv, (P, D)), np.broadcast_to(bo, (P, D))]
        for b in (bq, bk):
            cols.append(np.pad(np.pad(b, (0, NG * GR - D)).reshape(NG, GR).T, ((0, P - GR), (0, 0))))
        return np.concatenate(cols, axis=1)

    const = np.zeros((P, C_END - 4), f32)
    const[:, C_ID:C_ONE] = np.eye(P)
    const[:, C_ONE:C_TRI] = 1.0
    const[:, C_TRI:C_PAR] = np.triu(np.ones((P, P)))
    const[:, C_PAR:C_PAR + 16] = 1.0
    const[:, C_PAR + 48:C_PAR + 64] = 1.0
    const[:, C_PW:C_DIG] = float(RADIX) ** np.arange(DIGITS - 1, -1, -1)
    const[:, C_DIG:C_SEL] = np.arange(RADIX)
    for b in range(B):
        const[b::32, C_SEL + b] = 1.0
    const[:, C_IOTA:C_HM] = np.arange(1, 33)
    for j in range(GH):
        const[HD * j:HD * j + HD, C_HM + j] = 1.0
    for r in range(GR):
        const[r ^ 1, C_PERM + r] = 1.0
    kone = np.zeros((P - GR, NG * GH, SK), f32)
    for h in range(NG * GH):
        kone[h % GH, h, :] = 1.0
    inv = np.exp(np.arange(0, HD, 2, dtype=f32) * f32(-(4.0 * np.log(f32(10.0))) / HD)).astype(f32)
    angle = np.arange(S, dtype=f32)[:, None] * inv
    sin, cos = np.sin(angle).T, np.cos(angle).T
    rope_a, rope_b = np.zeros((GR, S), f32), np.zeros((GR, S), f32)
    for r in range(GR):
        m = (r % HD) // 2
        rope_a[r] = sin[m] if r % 2 == 0 else -sin[m]
        rope_b[r] = -cos[m]

    mask = np.pad(a["mask_1x1xSxS2_bk1"].reshape(S, SK), ((0, 0), (0, 80 - SK)))
    maskT = np.pad(mask.T, ((0, P - 80), (0, 0)))
    arrays = {
        "x": a["x"].reshape(T, D),
        "ctx": halves(a["ctx_1024"].reshape(KB, D).T),
        "gates": np.broadcast_to(np.concatenate([a["g_xattn"], a["g_ffn"]]), (P, 4)),
        "mask": np.ascontiguousarray(mask.reshape(2, P, 80).transpose(1, 0, 2)).view(np.uint32),
        "maskT": np.ascontiguousarray(maskT).view(np.uint32),
        "const": const,
        "kone": kone,
        "ropeA": rope_a,
        "ropeB": rope_b,
        "attn": np.stack([
            attention(*(a["L0_xattn_" + n] for n in ("Wq", "bq", "Wk", "bk", "Wv", "bv", "Wp", "bp"))),
            attention(*(a["L1_xattn_" + n] for n in ("Wq", "bq", "Wk", "bk", "Wv", "bv", "Wo", "bo")))]),
        "pat": a["L0_ffn_input_patterns"].reshape(8, 2, P, DC, P).transpose(0, 4, 1, 3, 2),
        "piw": a["L0_ffn_process_input_weights"].T.reshape(16, P, NP_).transpose(1, 0, 2),
        "pv": a["L0_ffn_process_values"].reshape(8, P, DV).transpose(1, 0, 2),
        "oiw": a["L0_ffn_output_input_weights"].T,
        "op": a["L0_ffn_output_patterns"].reshape(16, P, D).transpose(1, 0, 2),
        "gate": halves(a["L1_ffn_gate_w"].T),
        "wg": a["L1_ffn_Wg"].transpose(0, 2, 1).reshape(E, DC, P, F).transpose(0, 2, 1, 3),
        "wu": a["L1_ffn_Wu"].transpose(0, 2, 1).reshape(E, DC, P, F).transpose(0, 2, 1, 3),
        "wd": a["L1_ffn_Wd"].transpose(0, 2, 1).reshape(E, FC, P, D).transpose(0, 2, 1, 3),
        "sg": halves(a["L1_ffn_Ws_g"].T),
        "su": halves(a["L1_ffn_Ws_u"].T),
        "sd": a["L1_ffn_Ws_d"].T.reshape(FC, P, D).transpose(1, 0, 2),
    }
    arrays = {f"in_{k}": np.ascontiguousarray(v) for k, v in arrays.items()}
    nc = bacc.Bacc("TRN2", target_bir_lowering=False, num_devices=1)
    args = [nc.dram_tensor(k, v.shape, mybir.dt.from_np(v.dtype), kind="ExternalInput").ap()
            for k, v in arrays.items()]
    out = nc.dram_tensor("out_x", [T, D], F32, kind="ExternalOutput").ap()
    flamingo_kernel(nc, *args, out)
    r = run_bass_kernel_spmd(nc, [arrays], core_ids=[0])
    return r.results[0]["out_x"].reshape(B, S, D)
```

```python
from contextlib import ExitStack

import concourse.bass as bass
from concourse import mybir
from concourse.alu_op_type import AluOpType as ALU

ACT = mybir.ActivationFunctionType
AX = mybir.AxisListType.X
F32 = mybir.dt.float32
BF16 = mybir.dt.bfloat16
F32R = mybir.dt.float32r
U16 = mybir.dt.uint16
U8 = mybir.dt.uint8
U32 = mybir.dt.uint32
I32 = mybir.dt.int32

P = 128
B, S, D = 8, 256, 256
T = B * S
DC = D // P
H, HD, SK = 16, 16, 77
NG, GH = 3, 6
GR = GH * HD
KB = B * SK
NI, NP_, NO, DV = 2048, 1024, 2048, 128
TOP_I, TOP_P, TOP_O = NI // 8, NP_ // 8, NO // 8
E, F, CAP = 16, 512, 32
FC = F // P
EPS = 1e-5
MASKED = -float(2.0 ** 100)

C_ID, C_ONE, C_TRI, C_PAR, C_PW, C_DIG, C_SEL, C_IOTA, C_HM, C_PERM, C_GATE, C_END = (
    0, 128, 256, 384, 448, 452, 468, 476, 508, 514, 610, 614)
RADIX, DIGITS = 16, 4


def flamingo_kernel(nc, x_d, ctx_d, gates_d, mask_d, maskT_d, const_d, kone_d,
                    ropeA_d, ropeB_d, attn_d, pat_d, piw_d,
                    pv_d, oiw_d, op_d, gate_d, wg_d, wu_d, wd_d, sg_d, su_d, sd_d, out_d):
    with ExitStack() as ctx:
        def sem(name):
            return ctx.enter_context(nc.semaphore(name))

        starts = {}

        def rounded(name, where, at, cols):
            t = nc.alloc_sbuf_tensor_at(name, [P, cols], F32R, offset=starts[where] + 4 * at)
            return t[:, :]

        def region(name, cols):
            whole = ctx.enter_context(nc.sbuf_tensor(name, [P, cols], F32))
            starts[name] = nc.sbuf_base - 4 * cols
            at = [0]

            def take(n, start=None):
                lo = at[0] if start is None else start
                at[0] = lo + n
                assert at[0] <= cols, (name, at[0], cols)
                return whole[:, lo:lo + n]

            def used(multiple):
                at[0] = -(-at[0] // multiple) * multiple
                return at[0]
            return take, used

        keep, keep_used = region("keep", 13904)
        x_sb = keep(T // P * D).rearrange("p (t d) -> p t d", d=D)
        xnT_s = keep(DC * T)
        qT = xnT_s[:, 0:2 * NG * S].rearrange("p (s g q) -> p s g q", s=2, g=NG)
        qraw = xnT_s[:, 1536:2304].rearrange("p (g q) -> p g q", g=NG)
        qrot = xnT_s[:, 2304:3072].rearrange("p (g q) -> p g q", g=NG)
        kraw = xnT_s[:, 1024:1024 + NG * KB].rearrange("p (g n) -> p g n", g=NG)
        pcp = xnT_s[:, 3072:3072 + NP_]
        qr = rounded("qr", "keep", T // P * D + 3072, NG * S).rearrange("p (g q) -> p g q", g=NG)
        xn_s = keep(2 * 2 * D)
        xn = xn_s.rearrange("p (s t d) -> p s t d", s=2, d=D)
        xnT_b_s = keep(DC * S)
        xnT_b = xnT_b_s.rearrange("p (c t) -> p c t", c=DC)
        cst = keep(C_END)
        ident, onesf = cst[:, C_ID:C_ONE], cst[:, C_ONE:C_TRI]
        par = cst[:, C_PAR:C_PW].rearrange("p (a m) -> p a m", a=2)
        pw, digit = cst[:, C_PW:C_DIG], cst[:, C_DIG:C_SEL]
        sel8, iota = cst[:, C_SEL:C_IOTA], cst[:, C_IOTA:C_HM]
        hmask, perm, gates = cst[:, C_HM:C_PERM], cst[:, C_PERM:C_GATE], cst[:, C_GATE:C_END]
        tg = keep(4)
        bn = keep(2 * 6).rearrange("p (t k) -> p t k", k=6)
        mv = keep(2 * 2).rearrange("p (t k) -> p t k", k=2)
        scrap, veps, rstd, mhalf, eps = keep(1), keep(2), keep(2), keep(2), keep(2)
        fbn = keep(2 * 6).rearrange("p (t k) -> p t k", k=6)
        fag = keep(2 * 2).rearrange("p (t k) -> p t k", k=2)
        fmv = keep(T // P * 2).rearrange("p (t k) -> p t k", k=2)
        fveps, frstd = keep(2), keep(T // P)
        ones_b = keep(64).bitcast(BF16)
        tri_b = keep(64).bitcast(BF16)
        ident_b = keep(64).bitcast(BF16)
        bqs = keep(NG)
        acts = keep(128)
        TK_AT = keep_used(8)
        tk = keep(8 * 128)
        key, flip, met, gtm, selm = (tk[:, 128 * j:128 * j + 128] for j in range(5))
        khi, klo, level = (tk[:, 640 + 64 * j:704 + 64 * j].bitcast(U16) for j in range(3))
        rden, ytmp = tk[:, 0:512], tk[:, 512:1024]
        tied, above, above_lo, eqb = (keep(64).bitcast(BF16) for _ in range(4))
        reached = xnT_s[:, 0:1024].bitcast(BF16).rearrange("p (c n) -> p c n", c=16)
        cntb = keep(4).bitcast(BF16)
        thr, pmax, mx8, mxd, rs8, dsum = (keep(8) for _ in range(6))
        wpad_s = keep(512)
        wpad = wpad_s.rearrange("p (c m) -> p c m", m=32)
        outp = keep(D)
        aggT = keep(8)
        mask_w, maskT_w = keep(2 * 20).bitcast(U32), keep(64).bitcast(U32)
        mask_u, maskT_u = mask_w.bitcast(U8).rearrange("p (t k) -> p t k", t=2), maskT_w.bitcast(U8)
        maskb = keep(80).bitcast(BF16).rearrange("p (t k) -> p t k", t=2)
        maskTb = keep(128).bitcast(BF16)
        seen = keep(128).bitcast(BF16)
        anyv = keep(S)
        gate = keep(DC * E).rearrange("p (c e) -> p c e", c=DC)

        big, _ = region("big", 19456)
        piw = big(16 * NP_).rearrange("p (c n) -> p c n", c=16)
        pvt = big(8 * DV).rearrange("p (c n) -> p c n", c=8)
        oiw = big(NO)
        opt = big(16 * D, 0).rearrange("p (c n) -> p c n", c=16)
        XT = big(E * DC * S, 2048).rearrange("p (e c t) -> p e c t", e=E, c=DC)
        EO = big(4 * B * D, 0).rearrange("p (g b d) -> p g b d", g=4, b=B)
        xn_all = big(T // P * D, 10240).rearrange("p (t d) -> p t d", d=D)

        vp, _ = region("vp", 8192)
        V = vp(B * D).rearrange("p (b d) -> p b d", b=B)
        Vpad = vp(2 * H * 32).rearrange("p (s h m) -> p s h m", s=2, h=H)
        PT_AT = B * D + 2 * H * 32
        PT = vp(H * S, PT_AT).rearrange("p (h q) -> p h q", h=H)
        mpad_s = vp(2 * NG * P)
        mpad = mpad_s.rearrange("p (t g m) -> p t g m", t=2, g=NG)
        GWT = vp(B * 4 * S, 0).rearrange("p (b g t) -> p b g t", b=B, g=4)

        PAT_AT = 9576
        att, _ = region("att", PAT_AT + 1392)
        awt = att(2176 + 518)
        wq = awt[:, 0:576].rearrange("p (c g m) -> p c g m", c=DC, g=NG)
        wk = awt[:, 576:1152].rearrange("p (c g m) -> p c g m", c=DC, g=NG)
        wv = awt[:, 1152:1664].rearrange("p (c m) -> p c m", c=DC)
        wp = awt[:, 1664:2176].rearrange("p (c m) -> p c m", c=DC)
        bv, bp, bq, bk = awt[:, 2176:2432], awt[:, 2432:2688], awt[:, 2688:2691], awt[:, 2691:2694]
        ctxT = att(DC * KB).rearrange("p (c n) -> p c n", c=DC)
        kT = att(NG * KB).rearrange("p (g n) -> p g n", g=NG)
        kbd = att(2 * NG * GH * SK).rearrange("p (s h k) -> p s h k", s=2, k=SK)
        rope = att(2 * S)
        ropeA, ropeB = rope[:, 0:S], rope[:, S:2 * S]
        attnT = att(DC * S).rearrange("p (c q) -> p c q", c=DC)
        kbr = rounded("kbr", "att", PAT_AT, NG * GH * SK).rearrange("p (h k) -> p h k", k=SK)
        pat_s = att(1024 + 368, PAT_AT)
        pat = pat_s[:, 0:1024].rearrange("p (s n) -> p s n", s=2)
        xhi = rounded("xhi", "keep", T // P * D, DC * T).rearrange("p (c t) -> p c t", c=DC)
        xlo = rounded("xlo", "vp", PT_AT, DC * T).rearrange("p (c t) -> p c t", c=DC)
        phi = rounded("phi", "att", 3928, 1024).rearrange("p (s n) -> p s n", s=2)
        plo = rounded("plo", "keep", T // P * D + DC * T, 1024).rearrange("p (s n) -> p s n", s=2)

        WCOLS = 2 * DC * F + FC * D
        raw = [att(WCOLS, 2 * WCOLS), big(WCOLS, 16384)]
        hgl = att(1024).rearrange("p (f n) -> p f n", f=2)
        hval = att(512)
        whi = [rounded("whi0", "att", 0, WCOLS), rounded("whi1", "big", 10240, WCOLS),
               rounded("swhi", "big", 0, WCOLS)]
        wlo = [rounded("wlo0", "att", WCOLS, WCOLS), rounded("wlo1", "big", 10240 + WCOLS, WCOLS),
               rounded("swlo", "big", WCOLS, WCOLS)]
        SHARED = 2
        KEEP_X, KEEP_XN = T // P * D, T // P * D + DC * T
        hhi_s, hlo_s = rounded("hhi_s", "big", 6144, 2048), rounded("hlo_s", "big", 8192, 2048)
        hhi_e, hlo_e = rounded("hhi_e", "keep", KEEP_X, 2048), rounded("hlo_e", "keep", KEEP_X + 2048, 2048)
        thi = [rounded("thi0", "keep", KEEP_XN, 512), rounded("thi1", "keep", TK_AT, 512)]
        tlo = [rounded("tlo0", "keep", KEEP_XN + 512, 512), rounded("tlo1", "keep", TK_AT + 512, 512)]
        ghi = ctx.enter_context(nc.sbuf_tensor("ghi", [P, DC * E], F32R))[:, :]
        glo = ctx.enter_context(nc.sbuf_tensor("glo", [P, DC * E], F32R))[:, :]
        eo = [a.rearrange("p (t d) -> p t d", t=2) for a in (xnT_b_s, wpad_s)]
        G = [rounded(f"G{j}", "keep", at, 1024).rearrange("p (t n) -> p t n", t=2)
             for j, at in enumerate((KEEP_XN, KEEP_X))]
        nhi = [rounded(f"nhi{j}", "big", 14336 + 1024 * j, 512).rearrange("p (t d) -> p t d", t=2) for j in range(2)]
        nlo = [rounded(f"nlo{j}", "big", 14848 + 1024 * j, 512).rearrange("p (t d) -> p t d", t=2) for j in range(2)]
        GW = [xnT_s[:, 1024 * j:1024 * j + 1024].rearrange("p (t n) -> p t n", t=2) for j in (1, 2)]
        logT = anyv[0:E, :]
        probs, sc2_s, work, posm = (tk[:, 256 * j:256 * j + 256] for j in range(4))
        sc2 = sc2_s.rearrange("p (t m) -> p t m", t=2)
        posT = wpad_s[:, 0:256].rearrange("p (t m) -> p t m", t=2)
        cum = wpad_s[:, 256:512]

        ps = ctx.enter_context(nc.psum_tensor("ps", [P, 8, 512], F32))
        ps_all = ps[:, :, :]

        PIECES = [bass.ds(1024 * j, 1024) for j in range(3)]

        x_rest_in = sem("x_rest_in")
        x_in, const_in, attn_in, mask_in = sem("x_in"), sem("const_in"), sem("attn_in"), sem("mask_in")
        kone_in, pat_in = sem("kone_in"), [sem("pat_in0"), sem("pat_in1")]
        piw_in, op_in, gate_in, sw_in = sem("piw_in"), sem("op_in"), sem("gate_in"), sem("sw_in")
        ew_in = [sem("ew_in0"), sem("ew_in1")]
        gu_hi, d_hi, t_hi = sem("gu_hi"), sem("d_hi"), sem("t_hi")
        gu_split, d_split, t_split = sem("gu_split"), sem("d_split"), sem("t_split")
        sw_hi, sw_split, gate_hi, gate_split = sem("sw_hi"), sem("sw_split"), sem("gate_hi"), sem("gate_split")
        hval_done, hhi_done = sem("hval_done"), sem("hhi_done")
        eo_moved = [sem("eo_moved0"), sem("eo_moved1")]
        out_done = sem("out_done")
        cleared, prepared, tanh_done, bqs_done = sem("cleared"), sem("prepared"), sem("tanh_done"), sem("bqs_done")
        fstat_done, faggr_done, fmv_done = sem("fstat_done"), sem("faggr_done"), sem("fmv_done")
        fveps_done, frstd_done = sem("fveps_done"), sem("frstd_done")
        stat_done, mv_done, veps_done, rstd_done = sem("stat_done"), sem("mv_done"), sem("veps_done"), sem("rstd_done")
        xn_done, xt_ps, xt_done = sem("xn_done"), sem("xt_ps"), sem("xt_done")
        k_ps, k_raw, k_perm, k_mulA, k_mulB, kT_done = (sem("k_ps"), sem("k_raw"), sem("k_perm"), sem("k_mulA"),
                                                        sem("k_mulB"), sem("kT_done"))
        k_swap, v_raw = sem("k_swap"), sem("v_raw")
        v_ps, v_done = sem("v_ps"), sem("v_done")
        q_ps, q_out_done, q_perm, q_mulA, q_mulB, q_done = (sem("q_ps"), sem("q_out_done"), sem("q_perm"), sem("q_mulA"),
                                                       sem("q_mulB"), sem("q_done"))
        qr_done = sem("qr_done")
        kbd_done, rowmax_ps, rowmax_done = sem("kbd_done"), sem("rowmax_ps"), sem("rowmax_done")
        mT_ps, mT_done, score_ps, exp_done, pv_ps = (sem("mT_ps"), sem("mT_done"), sem("score_ps"), sem("exp_done"),
                                                     sem("pv_ps"))
        rden_done, attn_done, proj_ps, bias_done, x_done = (sem("rden_done"), sem("attn_done"), sem("proj_ps"),
                                                            sem("bias_done"), sem("x_done"))
        any_ps, any_done = sem("any_ps"), sem("any_done")
        xlo_done, pat_split = sem("xlo_done"), sem("pat_split")
        phi_done = sem("phi_done")
        ia_ps, ia_done = sem("ia_ps"), [sem(f"ia_done{j}") for j in range(4)]
        tk_step, tk_cnt, tk_tot = sem("tk_step"), sem("tk_cnt"), sem("tk_tot")
        pr_ps, pr_copied, pr_cols, pa_done = sem("pr_ps"), sem("pr_copied"), sem("pr_cols"), sem("pa_done")
        sm_dve, sm_pe, sm_act = sem("sm_dve"), sem("sm_pe"), sem("sm_act")
        agg_ps, agg_done, oa_ps, oa_done = sem("agg_ps"), sem("agg_done"), sem("oa_ps"), sem("oa_done")
        op_ps, op_copied, op_rows, x2_done = sem("op_ps"), sem("op_copied"), sem("op_rows"), sem("x2_done")
        nhi_done, nlo_done = sem("nhi_done"), sem("nlo_done")
        logT_ps, logT_done = sem("logT_ps"), sem("logT_done")
        rt_dve, rt_pe, rt_act = sem("rt_dve"), sem("rt_pe"), sem("rt_act")
        g_done, gw_done, disp_ps, disp_done = sem("g_done"), sem("gw_done"), sem("disp_ps"), sem("disp_done")
        gwt_ps, gwt_done = sem("gwt_ps"), sem("gwt_done")
        gu_ps, gelu_done, h_done, down_ps, down_done = (sem("gu_ps"), sem("gelu_done"), sem("h_done"),
                                                        sem("down_ps"), sem("down_done"))
        comb_ps, y_done = sem("comb_ps"), sem("y_done")

        block = ctx.enter_context(nc.Block())

        def bslice(b):
            return bass.ds(b * S, S)

        def ktslice(b):
            return bass.ds(b * SK, SK)

        def tiles(b):
            return bass.ds(b * 2, 2)

        def q_bank(g):
            return ps[0:GR, (5, 5, 2)[g], S * (g % 2):S * (g % 2) + S]

        DISPATCH_AT, COMBINE_AT = (6, 4), (0, 2)
        EARLY = 4

        def steps(eng, layer, step):
            for b in range(2):
                step(8 * layer + b, b, b, b == 0, False, True)
            with eng.Fori(1, B // 2 - 1) as t:
                for j in range(2):
                    b = t * 2 + j
                    step(b + 8 * layer, b, j, False, False, True)
            for b in range(B - 2, B):
                step(8 * layer + b, b, b % 2, False, b == B - 1, False)

        @block.sync
        def _(sp):
            x_t = x_d.rearrange("(t p) d -> p t d", p=P)
            sp.dma_start(cst[:, 0:C_GATE], const_d).then_inc(const_in, 16)
            sp.dma_start(gates, gates_d).then_inc(const_in, 16)
            sp.dma_start(awt, attn_d[0, :, 0:2694]).then_inc(attn_in, 16)
            sp.dma_start(ctxT, ctx_d).then_inc(attn_in, 16)
            sp.dma_start(x_sb[:, 0:4, :], x_t[:, 0:4, :]).then_inc(x_in, 16)
            for s in range(2):
                sp.dma_start(kbd[GR:P, s, :, :], kone_d).then_inc(kone_in, 16)
            sp.dma_start(x_sb[:, 4:16, :], x_t[:, 4:16, :]).then_inc(x_rest_in, 16)
            sp.dma_start(mask_w, mask_d.rearrange("p t k -> p (t k)")).then_inc(mask_in, 16)
            sp.dma_start(maskT_w, maskT_d).then_inc(mask_in, 16)
            sp.dma_start(ropeA[0:GR, :], ropeA_d).then_inc(mask_in, 16)
            sp.dma_start(ropeB[0:GR, :], ropeB_d).then_inc(mask_in, 16)
            sp.dma_start(piw, piw_d).then_inc(piw_in, 16)
            sp.dma_start(pvt, pv_d).then_inc(piw_in, 16)
            sp.dma_start(oiw, oiw_d).then_inc(piw_in, 16)
            sp.wait_ge(proj_ps, B)
            sp.wait_ge(x_done, B)
            for s in range(2):
                sp.dma_start(pat[:, s], pat_d[s]).then_inc(pat_in[s], 16)
            sp.dma_start(awt, attn_d[1, :, 0:2694]).then_inc(attn_in, 16)
            sp.dma_start(gate, gate_d).then_inc(gate_in, 16)
            with sp.Fori(1, 4) as t:
                for s in range(2):
                    sp.wait_ge(pat_split, t * 2 + (s - 1))
                    sp.dma_start(pat[:, s], pat_d[t * 2 + s]).then_inc(pat_in[s], 16)
            sp.wait_ge(pr_ps, 1)
            sp.dma_start(opt, op_d).then_inc(op_in, 16)
            sp.wait_ge(oa_ps, 1)
            for piece, d in zip(PIECES, (sg_d, su_d, sd_d)):
                sp.dma_start(raw[1][:, piece], d).then_inc(sw_in, 16)

            def load_expert(x, slot):
                for piece, d in zip(PIECES, (wg_d, wu_d, wd_d)):
                    sp.dma_start(raw[slot][:, piece], d[x]).then_inc(ew_in[slot], 16)

            sp.wait_ge(x_done, 2 * B)
            load_expert(0, 0)
            sp.wait_ge(sw_split, 3)
            load_expert(1, 1)
            sp.wait_ge(gu_split, 2)
            sp.wait_ge(d_split, 1)
            load_expert(2, 0)

            def expert_traffic(t, q, load):
                if load:
                    sp.wait_ge(gu_split, t * 8 + (2 * q + 4))
                    sp.wait_ge(d_split, t * 4 + (q + 2))
                    load_expert(t * 4 + (q + 3), (q + 1) % 2)
                sp.wait_ge(down_done, t * 4 + (B + q + 1))
                for g in range(4):
                    sp.dma_start(EO[32 * q:32 * q + 32, t, g::4, :], eo[q % 2][32 * g:32 * g + 32]
                                 ).then_inc(eo_moved[q % 2], 16)

            with sp.Fori(0, 3) as t:
                for q in range(4):
                    expert_traffic(t, q, True)
            for q in range(4):
                expert_traffic(3, q, q == 0)
            for b in range(B):
                sp.wait_ge(y_done, b + 1)
                sp.dma_start(out_d.rearrange("(t p) d -> p t d", p=P)[:, 2 * b:2 * b + 2, :],
                             x_sb[:, 2 * b:2 * b + 2, :]).then_inc(out_done, 16)
            sp.wait_ge(out_done, 16 * B)

        @block.gpsimd
        def _(pool):
            pool.memset(mhalf, -0.5).then_inc(cleared, 1)
            pool.memset(eps, EPS).then_inc(cleared, 1)
            pool.memset(mpad_s, 0.0).then_inc(cleared, 1)
            pool.memset(Vpad.rearrange("p s h m -> p (s h m)"), 0.0).then_inc(cleared, 1)
            pool.memset(PT.rearrange("p h q -> p (h q)"), 0.0).then_inc(cleared, 1)
            pool.memset(kbd[0:GR].rearrange("p s h k -> p (s h k)"), 0.0).then_inc(cleared, 1)
            pool.memset(wpad_s, 0.0).then_inc(cleared, 1)

            def inv_std(n):
                pool.wait_ge(mv_done, n * 2 + 2)
                pool.tensor_tensor(veps, mv[:, :, 1], eps, ALU.add).then_inc(veps_done, 1)
                pool.wait_ge(veps_done, n + 1)
                pool.tensor_tensor(rstd, veps, mhalf, ALU.pow).then_inc(rstd_done, 1)

            def inv_std_second(i, b):
                pool.wait_ge(fmv_done, i + 1)
                if not isinstance(i, int) or i > 0:
                    pool.wait_ge(frstd_done, i)
                pool.tensor_tensor(fveps, fmv[:, tiles(b), 1], eps, ALU.add).then_inc(fveps_done, 1)
                pool.wait_ge(fveps_done, i + 1)
                pool.tensor_tensor(frstd[:, tiles(b)], fveps, mhalf, ALU.pow).then_inc(frstd_done, 1)

            def block_keys(b, s, values=None):
                for g in range(NG):
                    keys = kT[0:GR, g, ktslice(b)].unsqueeze(1).to_broadcast([GR, GH, SK])
                    own = hmask[0:GR, :].unsqueeze(2).to_broadcast([GR, GH, SK])
                    pool.tensor_tensor(kbd[0:GR, s, GH * g:GH * g + GH, :], keys, own, ALU.mult)
                    pool.tensor_tensor(kbr[0:GR, GH * g:GH * g + GH, :], keys, own, ALU.mult)
                if values is not None:
                    pool.wait_ge(v_done, values)
                for a in range(2):
                    ins = pool.tensor_copy(
                        Vpad[0:SK, s].rearrange("p (h a) m -> p h a m", a=2)[:, :, a, HD * a:HD * a + HD],
                        V[0:SK, bass.ds(b, 1), :].rearrange("p o (h a m) -> p (o h) a m", a=2, m=HD)[:, :, a, :])
                ins.then_inc(kbd_done, 1)

            def rotary_a(b):
                pool.wait_ge(q_out_done, b * NG + NG * (B + 1))
                pool.tensor_tensor(qrot[0:GR], qraw[0:GR], ropeA[0:GR].unsqueeze(1).to_broadcast([GR, NG, S]),
                                   ALU.mult).then_inc(q_mulA, 1)

            pool.wait_ge(cleared, 7)
            for layer in range(2):
                if layer == 0:
                    for b in range(2):
                        inv_std(b)
                    pool.wait_ge(const_in, 32)
                    pool.wait_ge(kT_done, 6)
                    block_keys(0, 0, B)
                else:
                    pool.wait_ge(mask_in, 64)
                    for j in range(6):
                        g, nh = divmod(j, 2)
                        pool.wait_ge(k_swap, j + 1)
                        straight, swapped = (a[0:GR, g, 308 * nh:308 * nh + 308].rearrange("p (b k) -> p b k", k=SK)
                                             for a in (kraw, kT))
                        pool.tensor_tensor(straight, straight, ropeA[0:GR, 0:SK].unsqueeze(1).to_broadcast([GR, 4, SK]),
                                           ALU.mult).then_inc(k_mulA, 1)
                        pool.tensor_tensor(swapped, swapped, ropeB[0:GR, 0:SK].unsqueeze(1).to_broadcast([GR, 4, SK]),
                                           ALU.mult).then_inc(k_mulB, 1)
                        pool.wait_ge(k_mulA, j + 1)
                        pool.wait_ge(k_mulB, j + 1)
                        pool.tensor_tensor(swapped, swapped, straight, ALU.add).then_inc(kT_done, 1)
                    for j in range(B // 2):
                        pool.wait_ge(v_raw, j + 1)
                        v2 = V[0:SK, 2 * j:2 * j + 2, :]
                        pool.tensor_tensor(v2, v2, bv[0:SK].unsqueeze(1).to_broadcast([SK, 2, D]), ALU.add
                                           ).then_inc(v_done, 1)
                    pool.wait_ge(kT_done, 12)
                    block_keys(0, 0, B + B // 2)
                    for b in range(2):
                        inv_std(8 + b)
                    rotary_a(0)

                def step(i, b, s, first, last, ahead, layer=layer):
                    if last:
                        return
                    pool.wait_ge(rowmax_ps, i * 2 + 2)
                    block_keys(b + 1, 1 - s)
                    if ahead:
                        inv_std(i + 2)
                    if layer == 1:
                        rotary_a(b + 1)
                    if not first:
                        inv_std_second(i - 1, b - 1)
                steps(pool, layer, step)
                for b in range(B - 2, B):
                    inv_std_second(8 * layer + b, b)
                if layer == 0:
                    pool.wait_ge(ia_ps, 64)
                    pool.memset(PT[64:P].rearrange("p h q -> p (h q)"), 0.0).then_inc(cleared, 1)
                    pool.wait_ge(cleared, 8)

            for b in range(B):
                pool.wait_ge(nhi_done, b + 1)
                pool.tensor_tensor(nlo[b % 2], xn_all[:, 2 * b:2 * b + 2, :], nhi[b % 2], ALU.subtract
                                   ).then_inc(nlo_done, 1)

            def low_parts(t, q):
                x, slot = t * 4 + q, q % 2
                pool.wait_ge(t_hi, x + 1)
                pool.tensor_tensor(tlo[slot], XT[:, bass.ds(x, 1), :, :].rearrange("p o c t -> p (o c t)"),
                                   thi[slot], ALU.subtract).then_inc(t_split, 1)
                pool.wait_ge(d_hi, x + 1)
                pool.tensor_tensor(wlo[slot][:, PIECES[2]], raw[slot][:, PIECES[2]], whi[slot][:, PIECES[2]],
                                   ALU.subtract).then_inc(d_split, 1)

            with pool.Fori(0, E // 4) as t:
                for q in range(4):
                    low_parts(t, q)

        @block.scalar
        def _(act):
            act.wait_ge(const_in, 32)
            act.activation(tg, gates, ACT.Tanh).then_inc(tanh_done, 1)

            def copy_xt(n, out, bank=2):
                act.wait_ge(xt_ps, n + 1)
                act.activation(out, ps[:, bank, :].rearrange("p (c t) -> p c t", c=DC), ACT.Copy
                               ).then_inc(xt_done, 1)

            def q_out(i, s, layer, groups):
                if layer == 0:
                    act.wait_ge(bqs_done, 1)
                for g in groups:
                    act.wait_ge(q_ps, i * NG + (1 if g == 2 else NG))
                    if layer == 0:
                        ins = act.activation(qT[0:GR, s, g, :], q_bank(g), ACT.Identity, bias=bqs[0:GR, g:g + 1],
                                             scale=-0.25)
                    else:
                        ins = act.activation(qraw[0:GR, g, :], q_bank(g), ACT.Identity, bias=bq[0:GR, g:g + 1],
                                             scale=1.0)
                    ins.then_inc(q_out_done, 1)

            def round_q(i, s, layer):
                if layer == 0:
                    act.wait_ge(q_out_done, i * NG + NG)
                else:
                    act.wait_ge(q_done, i - (B - 1))
                act.activation(qr[0:GR], qT[0:GR, s], ACT.Copy).then_inc(qr_done, 1)

            def keys_out(layer, to, done):
                for j in range(6):
                    g, nh = divmod(j, 2)
                    act.wait_ge(k_ps, 6 * layer + j + 1)
                    act.activation(to[0:GR, g, 308 * nh:308 * nh + 308], ps[0:GR, 1 + j, 0:308], ACT.Identity,
                                   bias=bk[0:GR, g:g + 1], scale=1.0).then_inc(done, 1)

            def values_out(j):
                act.wait_ge(v_ps, B + j + 1)
                act.activation(V[0:SK, 2 * j:2 * j + 2, :], ps[0:SK, 0, :].rearrange("p (b d) -> p b d", b=2),
                               ACT.Copy).then_inc(v_raw, 1)

            for layer in range(2):
                if layer == 0:
                    act.wait_ge(attn_in, 32)
                    keys_out(0, kT, kT_done)
                copy_xt(16 * layer, xnT_b)
                q_out(8 * layer, 0, layer, (2, 0, 1))
                round_q(8 * layer, 0, layer)

                def step(i, b, s, first, last, ahead, layer=layer):
                    if not last:
                        copy_xt(i + (8 * layer + 1), xnT_b)
                        q_out(i + 1, 1 - s, layer, (2,))
                    for t in range(2):
                        act.wait_ge(mT_ps, i * 2 + (t + 1))
                        act.activation(qT[GR:P, s, :, P * t:P * t + P],
                                       ps[GR:P, 3 + t, 0:NG * P].rearrange("p (g q) -> p g q", g=NG), ACT.Copy
                                       ).then_inc(mT_done, 1)
                    if not last:
                        q_out(i + 1, 1 - s, layer, (0, 1))
                    for k in range(4):
                        act.wait_ge(score_ps, i * 4 + (k + 1))
                        a = 3 + 2 * (k % 2)
                        act.activation(PT[0:SK, 4 * k:4 * k + 4, :],
                                       ps[0:SK, a:a + 2, :].rearrange("p a (h q) -> p (a h) q", h=2), ACT.Exp
                                       ).then_inc(exp_done, 1)
                        if last and layer == 1 and k < 3:
                            act.wait_ge(sw_in, 48)
                            act.activation(whi[SHARED][:, PIECES[k]], raw[1][:, PIECES[k]], ACT.Copy
                                           ).then_inc(sw_hi, 1)
                    if not last:
                        round_q(i + 1, 1 - s, layer)
                    elif layer == 1:
                        act.wait_ge(gate_in, 16)
                        act.activation(ghi, gate.rearrange("p c e -> p (c e)"), ACT.Copy).then_inc(gate_hi, 1)
                steps(act, layer, step)

                if layer == 1:
                    break
                with act.Fori(0, B // 2) as t:
                    for j in range(2):
                        b = t * 2 + j
                        copy_xt(b + 8, xhi[:, :, bslice(b)], bank=1 + j)
                with act.Fori(0, 4) as t:
                    for u in range(4):
                        for g in range(4):
                            ch = t * 4 + u
                            act.wait_ge(ia_ps, t * 16 + (4 * u + g + 1))
                            for h in range(2):
                                part = ps[:, 3 + g, S * h:S * h + S]
                                ins = act.activation(part, part, ACT.Gelu,
                                                     accum_out=acts[:, bass.ds(ch * 8 + (2 * g + h), 1)])
                            ins.then_inc(ia_done[g], 1)
                act.wait_ge(attn_in, 48)
                keys_out(1, kraw, k_raw)
                for j in range(2):
                    values_out(j)
                act.wait_ge(pr_ps, 1)
                act.activation(pcp, ps[:, 2:4, :].rearrange("p a n -> p (a n)"), ACT.Copy).then_inc(pr_copied, 1)
                act.wait_ge(pr_cols, 1)
                act.activation(acts[:, 0:64], ps[:, 4, 0:64], ACT.Gelu).then_inc(pa_done, 1)
                for j in range(6):
                    g, nh = divmod(j, 2)
                    act.wait_ge(k_perm, j + 1)
                    act.activation(kT[0:GR, g, 308 * nh:308 * nh + 308], ps[0:GR, 1 + j, 0:308], ACT.Copy
                                   ).then_inc(k_swap, 1)
                for j in range(2, 4):
                    values_out(j)
                act.wait_ge(sm_dve, 5)
                act.activation(gtm[:, 0:64], gtm[:, 0:64], ACT.Exp).then_inc(sm_act, 1)
                act.wait_ge(oa_ps, 1)
                act.activation(acts, ps[:, 4, 0:128], ACT.Gelu).then_inc(oa_done, 1)
                act.wait_ge(op_ps, 1)
                act.activation(outp, ps[:, 5, 0:D], ACT.Copy).then_inc(op_copied, 1)

            def gelu_half(u, f):
                act.wait_ge(gu_ps, u * 2 + (f + 1))
                act.activation(hgl[:, f, :], ps[:, 2 * f, :], ACT.Gelu).then_inc(gelu_done, 1)

            for b in range(B):
                copy_xt(24 + b, xhi[:, :, bslice(b)], bank=6)
                if b > 0:
                    gelu_half((b - 1) // 2, (b - 1) % 2)
                act.wait_ge(logT_ps, b + 1)
                act.activation(logT, ps[0:E, 7, 0:S], ACT.Copy).then_inc(logT_done, 1)
            gelu_half(3, 1)
            act.wait_ge(rt_dve, 2)
            act.activation(probs, probs, ACT.Exp).then_inc(rt_act, 1)

            def round_weights(slot, piece):
                act.activation(whi[slot][:, PIECES[piece]], raw[slot][:, PIECES[piece]], ACT.Copy
                               ).then_inc(d_hi if piece == 2 else gu_hi, 1)

            def round_tokens(x, slot):
                act.activation(thi[slot], XT[:, bass.ds(x, 1), :, :].rearrange("p o c t -> p (o c t)"), ACT.Copy
                               ).then_inc(t_hi, 1)

            def round_norms(b):
                if b >= 2:
                    act.wait_ge(disp_ps, DC * (b - 1))
                act.activation(nhi[b % 2], xn_all[:, 2 * b:2 * b + 2, :], ACT.Copy).then_inc(nhi_done, 1)

            for h in range(8, 16):
                gelu_half(h // 2, h % 2)
                if h in (11, 13):
                    round_norms((h - 11) // 2)
                if h == 10:
                    act.wait_ge(ew_in[0], 48)
                if h in (10, 12, 14):
                    round_weights(0, (h - 10) // 2)
            for b in range(B):
                d_at, c_at = DISPATCH_AT[b % 2], COMBINE_AT[b % 2]
                if b == 0:
                    act.wait_ge(down_ps, B)
                for c in range(DC):
                    act.wait_ge(disp_ps, DC * b + c + 1)
                    act.activation(XT[:, :, c, 32 * b:32 * b + 32],
                                   ps[:, d_at + c, :].rearrange("p (e s) -> p e s", e=E), ACT.Copy).then_inc(disp_done, 1)
                if b == B - 1:
                    act.wait_ge(disp_done, DC * B)
                    round_tokens(0, 0)
                act.wait_ge(gwt_ps, b + 1)
                act.activation(GWT[:, b].rearrange("p g t -> p (g t)"),
                               ps[:, c_at:c_at + 2, :].rearrange("p a n -> p (a n)"), ACT.Copy
                               ).then_inc(gwt_done, 1)
                if b + 2 < B:
                    round_norms(b + 2)

            def expert_out(u, s, reused):
                act.wait_ge(down_ps, u + 1)
                if reused is not None:
                    act.wait_ge(eo_moved[s], reused)
                act.activation(eo[s], ps[:, 4 + s, :].rearrange("p (t d) -> p t d", t=2), ACT.Copy
                               ).then_inc(down_done, 1)

            def four_experts(t, first, last):
                for q in range(4):
                    u = t * 4 + (B + q)
                    slot = (q + 1) % 2
                    more = not (last and q == 3)
                    if more:
                        round_tokens(t * 4 + (q + 1), slot)
                        act.wait_ge(ew_in[slot], t * 96 + 48 * ((q + 1) // 2 + 1))
                        round_weights(slot, 0)
                    gelu_half(u, 0)
                    if more:
                        round_weights(slot, 1)
                    if not (first and q == 0):
                        expert_out(u - 1, (q - 1) % 2, None if first and q < 3 else t * 128 + 64 * ((q - 1) // 2))
                    if more:
                        round_weights(slot, 2)
                    gelu_half(u, 1)

            four_experts(0, True, False)
            with act.Fori(1, E // 4 - 1) as t:
                four_experts(t, False, False)
            four_experts(E // 4 - 1, False, True)
            expert_out(B + E - 1, 1, 64 * (E // 2 - 1))

        @block.tensor
        def _(pe):
            def mm(out, lhsT, rhs, start=True, stop=True):
                return pe.matmul(out, lhsT, rhs, start=start, stop=stop, skip_group_check=True)

            def transpose_xn(n, src, bank=2):
                pe.wait_ge(xn_done, n * 2 + 2)
                for c in range(DC):
                    for t in range(2):
                        at = (c * 2 + t) * P
                        ins = pe.transpose(ps[:, bank, at:at + P], src[:, t, P * c:P * c + P], ident)
                ins.then_inc(xt_ps, 1)

            def project_q(g):
                for c in range(DC):
                    ins = mm(q_bank(g), wq[:, c, g, :], xnT_b[:, c, :], c == 0, c == DC - 1)
                ins.then_inc(q_ps, 1)

            def swap_pairs(b):
                pe.wait_ge(q_out_done, b * NG + NG * (B + 1))
                for g in range(NG):
                    ins = mm(ps[0:GR, 1 + g // 2, S * (g % 2):S * (g % 2) + S], perm[0:GR, :], qraw[0:GR, g, :])
                ins.then_inc(q_perm, 1)

            def project_out(i):
                pe.wait_ge(attn_done, i * 2 + 2)
                for t in range(2):
                    for c in range(DC):
                        ins = mm(ps[:, 0, D * t:D * t + D], attnT[:, c, P * t:P * t + P], wp[:, c, :],
                                 c == 0, c == DC - 1)
                ins.then_inc(proj_ps, 1)

            def project_keys(layer, j):
                g, nh = divmod(j, 2)
                for c in range(DC):
                    ins = mm(ps[0:GR, 1 + j, 0:308], wk[:, c, g, :], ctxT[:, c, 308 * nh:308 * nh + 308],
                             c == 0, c == DC - 1)
                ins.then_inc(k_ps, 1)

            pe.wait_ge(const_in, 32)
            for layer in range(2):
                pe.wait_ge(attn_in, 32 + 16 * layer)
                if layer == 0:
                    for j in range(6):
                        project_keys(0, j)

                def project_values():
                    for b in range(B):
                        bank = 7 if b % 2 == 0 else 0
                        if b >= 2:
                            pe.wait_ge(v_done, 8 * layer + b - 1)
                        for c in range(DC):
                            ins = mm(ps[0:SK, bank, 0:D], ctxT[:, c, SK * b:SK * b + SK], wv[:, c, :],
                                     c == 0, c == DC - 1)
                        ins.then_inc(v_ps, 1)

                if layer == 1:
                    pe.wait_ge(cleared, 8)
                    pe.wait_ge(any_done, 1)
                    pe.wait_ge(x2_done, B)
                pe.wait_ge(kT_done, 6 * (layer + 1))
                transpose_xn(16 * layer, xn[:, 0])
                pe.wait_ge(xt_done, 16 * layer + 1)
                for g in (2, 0, 1):
                    project_q(g)
                if layer == 0:
                    project_values()
                if layer == 1:
                    swap_pairs(0)
                pe.wait_ge(v_done, B if layer == 0 else B + B // 2)
                pe.wait_ge(prepared, 6)
                pe.wait_ge(kone_in, 32)
                pe.wait_ge(cleared, 7)

                def step(i, b, s, first, last, ahead, layer=layer):
                    n = i + 8 * layer

                    def row_scores(t):
                        for g in range(NG):
                            bank = (3, 4, 5)[g] if t == 0 else (6, 7, 1)[g]
                            out = ps[:, bank, 0:GH * SK]
                            ins = mm(out, qr[0:GR, g, P * t:P * t + P],
                                     kbr[0:GR, GH * g:GH * g + GH, :].rearrange("p h k -> p (h k)"),
                                     True, layer == 0)
                            if layer == 1:
                                ins = mm(out.rearrange("p (h k) -> p h k", k=SK), ident_b,
                                         maskb[:, t, 0:SK].unsqueeze(1).to_broadcast([P, GH, SK]), False, True)
                        ins.then_inc(rowmax_ps, 1)

                    if layer == 0:
                        pe.wait_ge(q_out_done, i * NG + NG)
                    else:
                        pe.wait_ge(q_done, b + 1)
                    if not last:
                        transpose_xn(n + 1, xn[:, 1 - s])
                    pe.wait_ge(qr_done, i + 1)
                    pe.wait_ge(kbd_done, i + 1)
                    row_scores(0)
                    if not first:
                        pe.wait_ge(attn_done, i * 2 - 1)
                    row_scores(1)
                    if not last:
                        pe.wait_ge(xt_done, n + 2)
                        project_q(2)
                    if not first:
                        project_out(i - 1)
                    for t in range(2):
                        pe.wait_ge(rowmax_done, i * 2 + (t + 1))
                        for g in range(NG):
                            ins = pe.transpose(ps[:, 3 + t, P * g:P * g + P], mpad[:, t, g, :], ident)
                        ins.then_inc(mT_ps, 1)
                        if not last and t == 0:
                            project_q(0)
                            project_q(1)

                    def key_scores(k):
                        for m in range(4):
                            h = 4 * k + m
                            out = ps[0:SK, 3 + 2 * (k % 2) + m // 2, S * (m % 2):S * (m % 2) + S]
                            ins = mm(out, kbd[:, s, h, :], qT[:, s, h // GH, :], True, layer == 0)
                            if layer == 1:
                                ins = mm(out, ident_b[:, 0:SK], maskTb, False, True)
                        ins.then_inc(score_ps, 1)

                    def weigh_values(c):
                        bank = 7 if c == 0 else 0
                        for den in range(2):
                            for a in range(2):
                                for j in range(4):
                                    h = 8 * c + 2 * j + a
                                    lhsT = par[:, a, :] if den else Vpad[:, s, h, :]
                                    ins = mm(ps[32 * j:32 * j + 32, bank, S * den:S * den + S], lhsT, PT[:, h, :],
                                             a == 0, a == 1)
                        ins.then_inc(pv_ps, 1)

                    pe.wait_ge(mT_done, i * 2 + 2)
                    key_scores(0)
                    if not last:
                        pe.wait_ge(q_out_done, i * NG + 2 * NG)
                    key_scores(1)
                    pe.wait_ge(exp_done, i * 4 + 1)
                    key_scores(2)
                    if layer == 1 and not last:
                        swap_pairs(b + 1)
                    pe.wait_ge(exp_done, i * 4 + 2)
                    key_scores(3)
                    weigh_values(0)
                    pe.wait_ge(exp_done, i * 4 + 4)
                    if not first:
                        pe.wait_ge(bias_done, i)
                    weigh_values(1)
                    if last:
                        if layer == 0:
                            for j in range(2):
                                transpose_xn(B + j, xn[:, j], bank=1 + j)
                        else:
                            transpose_xn(24, xn_all[:, 0:2, :], bank=6)
                        project_out(i)
                steps(pe, layer, step)
                if layer == 1:
                    break

                pe.wait_ge(x_done, B)
                for b in range(2, B):
                    pe.wait_ge(xt_done, b + 7)
                    pe.wait_ge(xlo_done, b - 1)
                    transpose_xn(b + 8, xn[:, b % 2], bank=1 + b % 2)
                pe.wait_ge(xt_done, 2 * B)
                pe.wait_ge(xlo_done, B)

                def four_chunks(t, first):
                    for u in range(4):
                        if u % 2 == 0:
                            pe.wait_ge(pat_split, t * 2 + (u // 2 + 1))
                        at = 256 * (u % 2)
                        for g in range(4):
                            if not (first and u == 0):
                                pe.wait_ge(ia_done[g], t * 4 + u)
                            for c in range(DC):
                                for pp, xx in ((phi, xhi), (phi, xlo), (plo, xhi)):
                                    ins = mm(ps[:, 3 + g, :], pp[:, u // 2, at + P * c:at + P * c + P],
                                             xx[:, c, 512 * g:512 * g + 512],
                                             c == 0 and xx is xhi and pp is phi, c == DC - 1 and pp is plo)
                            ins.then_inc(ia_ps, 1)

                four_chunks(0, True)
                with pe.Fori(1, 4) as t:
                    four_chunks(t, False)

                def keys(j):
                    if j == 0:
                        pe.wait_ge(attn_in, 48)
                    project_keys(1, j)

                def swapped_keys(j):
                    g, nh = divmod(j, 2)
                    pe.wait_ge(k_raw, j + 1)
                    mm(ps[0:GR, 1 + j, 0:308], perm[0:GR, :], kraw[0:GR, g, 308 * nh:308 * nh + 308]
                       ).then_inc(k_perm, 1)

                def values(j):
                    if j > 0:
                        pe.wait_ge(v_raw, j)
                    for h in range(2):
                        for c in range(DC):
                            at = SK * (2 * j + h)
                            ins = mm(ps[0:SK, 0, D * h:D * h + D], ctxT[:, c, at:at + SK], wv[:, c, :],
                                     c == 0, c == DC - 1)
                    ins.then_inc(v_ps, 1)

                def seen_keys(_):
                    pe.wait_ge(prepared, 6)
                    pe.wait_ge(v_raw, 4)
                    mm(ps[:, 0, 0:S], ones_b[0:SK, :], seen[0:SK, :]).then_inc(any_ps, 1)

                def top_k(j, chunks, between):
                    n, base = 8 * chunks, (0, 36, 71)[j]

                    def count(first, more):
                        for quarter in range(4):
                            pe.wait_ge(tk_cnt, first + quarter)
                            if more and quarter == 0:
                                mm(ps[:, 7, 0:P], ones_b, cntb.unsqueeze(1).to_broadcast([P, RADIX, 8]), True, False)
                            for c in range(quarter * chunks // 4, (quarter + 1) * chunks // 4):
                                ins = mm(ps[:, 7, 0:P], ones_b, reached[:, c, :], c == 0 and not more, c == chunks - 1)
                        ins.then_inc(tk_tot, 1)

                    for it in range(2 * DIGITS):
                        count(it * 4 + (base + (1 if it < DIGITS else 2)), it >= DIGITS)
                        if it < len(between):
                            work, arg = between[it]
                            work(arg)
                    pe.wait_ge(tk_cnt, base + 34)
                    mm(ps[:, 7, 0:n], ones_b, cntb.unsqueeze(1).to_broadcast([P, chunks, 8]), True, False)
                    pe.wait_ge(tk_cnt, base + 35)
                    mm(ps[:, 7, 0:n], tri_b, eqb[:, 0:n], False, False)
                    for d in range(1, chunks):
                        ins = mm(ps[:, 7, 8 * d:n], ones_b, eqb[:, 0:n - 8 * d], False, d == chunks - 1)
                    ins.then_inc(tk_tot, 1)

                top_k(0, 16, [(keys, j) for j in range(6)] + [(values, j) for j in range(2)])
                pe.wait_ge(tk_cnt, 36)
                pe.wait_ge(piw_in, 48)
                pe.wait_ge(k_raw, 6)
                for c in range(16):
                    g = c % 4
                    for a in range(2):
                        ins = mm(ps[32 * g:32 * g + 32, 2 + a, :], wpad[:, c, :], piw[:, c, 512 * a:512 * a + 512],
                                 c < 4, c >= 12)
                ins.then_inc(pr_ps, 1)
                pe.wait_ge(pr_copied, 1)
                for c in range(8):
                    ins = mm(ps[:, 4, 8 * c:8 * c + 8], pcp[:, P * c:P * c + P], sel8)
                ins.then_inc(pr_cols, 1)
                top_k(1, 8, [(swapped_keys, j) for j in range(6)] + [(values, j) for j in range(2, 4)])
                pe.wait_ge(k_swap, 6)
                pe.wait_ge(sm_dve, 1)
                pe.transpose(ps[0:8, 6, 0:P], pmax, ident).then_inc(sm_pe, 1)
                pe.wait_ge(sm_dve, 3)
                mm(ps[:, 6, 128:136], onesf[0:8, :], mxd[0:8, :]).then_inc(sm_pe, 1)
                pe.wait_ge(sm_dve, 7)
                mm(ps[:, 6, 136:144], onesf, dsum).then_inc(sm_pe, 1)
                pe.wait_ge(sm_dve, 9)
                for c in range(8):
                    ins = mm(ps[:, 5, 0:8], pvt[:, c, :], selm[:, 8 * c:8 * c + 8], c == 0, c == 7)
                ins.then_inc(agg_ps, 1)
                pe.wait_ge(agg_done, 1)
                for c in range(16):
                    ins = mm(ps[:, 4, 8 * c:8 * c + 8], oiw[:, P * c:P * c + P], aggT)
                ins.then_inc(oa_ps, 1)
                top_k(2, 16, [(seen_keys, 0)])
                pe.wait_ge(tk_cnt, 107)
                pe.wait_ge(op_in, 16)
                for c in range(16):
                    g = c % 4
                    ins = mm(ps[32 * g:32 * g + 32, 5, 0:D], wpad[:, c, :], opt[:, c, :], c < 4, c >= 12)
                ins.then_inc(op_ps, 1)
                pe.wait_ge(op_copied, 1)
                for b in range(B):
                    if b >= 2:
                        pe.wait_ge(x2_done, b - 1)
                    mm(ps[:, 1 + b % 2, 0:D], sel8[:, b:b + 1].to_broadcast([P, P]), outp).then_inc(op_rows, 1)

            def split_products(out, w, x, first, last):
                for j, (lhsT, rhs) in enumerate(((w[0], x[0]), (w[0], x[1]), (w[1], x[0]))):
                    ins = mm(out, lhsT, rhs, first and j == 0, last and j == 2)
                return ins

            def gate_up(u, f, slot, tokens, first=False):
                if not first:
                    pe.wait_ge(h_done, u * 2 + (f - 1))
                for m in range(2):
                    for a in range(2):
                        for c in range(DC):
                            at = 1024 * m + F * c + P * (2 * f + a)
                            ins = split_products(ps[:, 2 * f + m, S * a:S * a + S],
                                                 (whi[slot][:, at:at + P], wlo[slot][:, at:at + P]), tokens(c),
                                                 c == 0, c == DC - 1)
                ins.then_inc(gu_ps, 1)

            def down(u, s, slot, h, first=False):
                pe.wait_ge(h_done, u * 2 + 2)
                if not first:
                    pe.wait_ge(down_done, u)
                for t in range(2):
                    for f in range(FC):
                        at, row = 2048 + D * f, 1024 * s + S * f + P * t
                        ins = split_products(ps[:, 4 + s, D * t:D * t + D],
                                             (h[0][:, row:row + P], h[1][:, row:row + P]),
                                             (whi[slot][:, at:at + D], wlo[slot][:, at:at + D]), f == 0, f == FC - 1)
                ins.then_inc(down_ps, 1)

            def shared_half(h):
                u, f = h // 2, h % 2
                gate_up(u, f, SHARED, lambda c: (xhi[:, c, S * u:S * u + S], xlo[:, c, S * u:S * u + S]), u == 0)
                if f == 0 and u > 0:
                    down(u - 1, (u - 1) % 2, SHARED, (hhi_s, hlo_s), u == 1)

            def logits_to_rows(b):
                pe.wait_ge(logT_done, b + 1)
                for t in range(2):
                    at = 256 + E * (2 * b + t)
                    ins = pe.transpose(ps[:, 7, at:at + E], logT[:, P * t:P * t + P], ident[0:E, 0:E])
                return ins

            pe.wait_ge(gate_split, 1)
            pe.wait_ge(x_done, 2 * B)
            for b in range(B):
                if b > 0:
                    pe.wait_ge(xlo_done, B + b)
                    transpose_xn(24 + b, xn_all[:, 2 * b:2 * b + 2, :], bank=6)
                if b == 1:
                    pe.wait_ge(sw_split, 3)
                if b > 0:
                    shared_half(b - 1)
                    logits_to_rows(b - 1)
                pe.wait_ge(xt_done, 24 + b + 1)
                pe.wait_ge(xlo_done, B + b + 1)
                for c in range(DC):
                    ins = split_products(ps[0:E, 7, 0:S], (ghi[:, E * c:E * c + E], glo[:, E * c:E * c + E]),
                                         (xhi[:, c, S * b:S * b + S], xlo[:, c, S * b:S * b + S]),
                                         c == 0, c == DC - 1)
                ins.then_inc(logT_ps, 1)
            shared_half(7)
            logits_to_rows(B - 1).then_inc(rt_pe, 1)

            shared_half(8)
            shared_half(9)
            pe.wait_ge(rt_dve, 5)
            for t in range(2):
                ins = pe.transpose(ps[:, 7, P * t:P * t + P], sc2[:, t, :], ident)
            ins.then_inc(rt_pe, 1)
            for h in range(10, 13):
                shared_half(h)
            pe.wait_ge(rt_dve, 18)
            for t in range(2):
                ins = pe.transpose(ps[:, 7, P * t:P * t + P], posm[:, P * t:P * t + P], ident)
            ins.then_inc(rt_pe, 1)
            for h in range(13, 16):
                shared_half(h)

            for b in range(B):
                d_at, c_at = DISPATCH_AT[b % 2], COMBINE_AT[b % 2]
                pe.wait_ge(g_done, 2 * b + 2)
                pe.wait_ge(nlo_done, b + 1)
                if b == 1:
                    pe.wait_ge(down_done, B)
                elif b > 1:
                    pe.wait_ge(disp_done, DC * (b - 1))
                for c in range(DC):
                    for t in range(2):
                        for part in (nhi, nlo):
                            ins = mm(ps[:, d_at + c, :], part[b % 2][:, t, P * c:P * c + P], G[b % 2][:, t, :],
                                     t == 0 and part is nhi, t == 1 and part is nlo)
                    ins.then_inc(disp_ps, 1)
                if b == 0:
                    down(B - 1, 1, SHARED, (hhi_s, hlo_s))
                pe.wait_ge(gw_done, 2 * b + 2)
                if b >= 2:
                    pe.wait_ge(gwt_done, b - 1)
                for g in range(4):
                    for t in range(2):
                        at = S * (g % 2) + P * t
                        ins = pe.transpose(ps[:, c_at + g // 2, at:at + P], GW[b % 2][:, t, P * g:P * g + P], ident)
                ins.then_inc(gwt_ps, 1)
            pe.wait_ge(disp_done, DC * B)
            pe.wait_ge(gwt_done, B - 1)

            def four_experts(t, first):
                for q in range(4):
                    s = q % 2
                    u = t * 4 + (B + q)
                    pe.wait_ge(gu_split, t * 8 + (2 * q + 2))
                    pe.wait_ge(t_split, t * 4 + (q + 1))

                    def tokens(c, s=s):
                        return thi[s][:, S * c:S * c + S], tlo[s][:, S * c:S * c + S]
                    gate_up(u, 0, s, tokens)
                    if not (first and q == 0):
                        pe.wait_ge(d_split, t * 4 + q)
                        down(u - 1, 1 - s, 1 - s, (hhi_e, hlo_e))
                    elif q == 0:
                        pe.wait_ge(gwt_done, B)
                    gate_up(u, 1, s, tokens)

            four_experts(0, True)
            with pe.Fori(1, E // 4) as t:
                four_experts(t, False)
            def combine(b, groups):
                for t in range(2):
                    for g in groups:
                        ins = mm(ps[:, (6 + b) % 8, D * t:D * t + D], GWT[:, b, g, P * t:P * t + P], EO[:, g, b, :],
                                 g == 0 and t == 0, g == 3 and t == 1)
                if 3 in groups:
                    ins.then_inc(comb_ps, 1)

            for s in range(2):
                pe.wait_ge(eo_moved[s], 64 * 3 * E // 8)
            combine(0, range(3))
            pe.wait_ge(d_split, E)
            down(B + E - 1, 1, 1, (hhi_e, hlo_e))
            for b in range(1, 5):
                combine(b, range(3))
            for s in range(2):
                pe.wait_ge(eo_moved[s], 64 * E // 2)
            pe.wait_ge(down_done, B + E)
            for b in range(5):
                combine(b, (3,))
            for b in range(5, B):
                combine(b, range(4))

        @block.vector
        def _(dve):
            dve.wait_ge(const_in, 32)
            dve.tensor_copy(ones_b, onesf).then_inc(prepared, 1)
            dve.tensor_copy(tri_b, cst[:, C_TRI:C_PAR]).then_inc(prepared, 1)
            dve.tensor_copy(ident_b, ident).then_inc(prepared, 1)

            def stats(n, b):
                for t in range(2):
                    dve.bn_stats(bn[:, t, :], x_sb[:, b * 2 + t, :]).then_inc(stat_done, 1)
                dve.wait_ge(stat_done, n * 2 + 2)
                dve.memset(scrap, 0.0)
                for t in range(2):
                    dve.bn_aggr(mv[:, t, :], bn[:, t, :]).then_inc(mv_done, 1)

            def normalise(i, b, out):
                dve.wait_ge(rstd_done, i + 1)
                for t in range(2):
                    dve.tensor_scalar(out[:, t, :], x_sb[:, b * 2 + t, :], mv[:, t, 0:1], rstd[:, t:t + 1],
                                      ALU.subtract, ALU.mult).then_inc(xn_done, 1)

            def stats_second(i, b):
                dve.wait_ge(x_done, i + 1)
                dve.memset(scrap, 0.0)
                for t in range(2):
                    dve.bn_stats(fbn[:, t, :], x_sb[:, b * 2 + t, :]).then_inc(fstat_done, 1)
                dve.wait_ge(fstat_done, i * 2 + 2)
                dve.memset(scrap, 0.0)
                for t in range(2):
                    dve.bn_aggr(fag[:, t, :], fbn[:, t, :]).then_inc(faggr_done, 1)
                dve.wait_ge(faggr_done, i * 2 + 2)
                dve.tensor_copy(fmv[:, tiles(b), :], fag).then_inc(fmv_done, 1)

            def normalise_second(i, b, out):
                dve.wait_ge(frstd_done, i + 1)
                for t in range(2):
                    dve.tensor_scalar(out[:, t, :], x_sb[:, 2 * b + t, :], fmv[:, 2 * b + t, 0:1],
                                      frstd[:, 2 * b + t:2 * b + t + 1], ALU.subtract, ALU.mult).then_inc(xn_done, 1)

            def low_part(n, b, bank):
                dve.wait_ge(xt_done, n + 1)
                dve.tensor_tensor(xlo[:, :, S * b:S * b + S], ps[:, bank, :].rearrange("p (c t) -> p c t", c=DC),
                                  xhi[:, :, S * b:S * b + S], ALU.subtract).then_inc(xlo_done, 1)

            def add_projection(i, b, layer):
                dve.wait_ge(proj_ps, i + 1)
                dve.tensor_tensor(ytmp.rearrange("p (t d) -> p t d", t=2),
                                  ps[:, 0, :].rearrange("p (t d) -> p t d", t=2),
                                  bp.unsqueeze(1).to_broadcast([P, 2, D]), ALU.add).then_inc(bias_done, 1)
                dve.wait_ge(bias_done, i + 1)
                xt = x_sb[:, tiles(b), :]
                dve.scalar_tensor_tensor(out=xt, in0=ytmp.rearrange("p (t d) -> p t d", t=2),
                                         scalar=tg[:, layer:layer + 1], in1=xt, op0=ALU.mult, op1=ALU.add
                                         ).then_inc(x_done, 1)

            def rotary_b(i, b, s):
                dve.wait_ge(q_perm, b + 1)
                dve.tensor_tensor(qT[0:GR, s], ps_all[0:GR, 1:3, :].rearrange("p a n -> p (a n)")[:, 0:NG * S]
                                  .rearrange("p (g q) -> p g q", g=NG),
                                  ropeB[0:GR].unsqueeze(1).to_broadcast([GR, NG, S]), ALU.mult).then_inc(q_mulB, 1)
                dve.wait_ge(q_mulA, b + 1)
                dve.wait_ge(q_mulB, b + 1)
                dve.tensor_tensor(qT[0:GR, s], qT[0:GR, s], qrot[0:GR], ALU.add).then_inc(q_done, 1)

            for layer in range(2):
                if layer == 0:
                    dve.wait_ge(x_in, 16)
                dve.wait_ge(attn_in, 32 + 16 * layer)
                if layer == 0:
                    dve.tensor_scalar(bqs[0:GR], bq[0:GR], -0.25, None, ALU.mult).then_inc(bqs_done, 1)
                    for b in range(2):
                        stats(b, b)
                        normalise(b, b, xn[:, b])
                if layer == 0:
                    dve.wait_ge(cleared, 7)
                    dve.wait_ge(tanh_done, 1)
                    for b in range(B):
                        dve.wait_ge(v_ps, b + 1)
                        dve.tensor_tensor(V[0:SK, b, :], ps[0:SK, 7 if b % 2 == 0 else 0, 0:D], bv[0:SK], ALU.add
                                          ).then_inc(v_done, 1)
                    dve.wait_ge(x_rest_in, 16)
                    dve.wait_ge(mask_in, 64)
                    dve.tensor_scalar(maskb[:, :, 0:SK], mask_u[:, :, 0:SK], MASKED, None, ALU.mult).then_inc(prepared, 1)
                    dve.tensor_scalar(maskTb, maskT_u, MASKED, None, ALU.mult).then_inc(prepared, 1)
                    dve.tensor_scalar(seen, maskT_u, -1.0, 1.0, ALU.mult, ALU.add).then_inc(prepared, 1)
                else:
                    rotary_b(8, 0, 0)

                def step(i, b, s, first, last, ahead, layer=layer):
                    n = i + 8 * layer

                    def row_max(t, banks):
                        lo, g0 = banks
                        k = NG if t == 0 else (2 if g0 == 0 else 1)
                        src = ps[:, lo:lo + k, 0:GH * SK].rearrange("p g (h k) -> p g h k", k=SK)
                        return dve.tensor_reduce(mpad[:, t, g0:g0 + k, GR:GR + GH], src, AX, ALU.max, negate=True)

                    dve.wait_ge(rowmax_ps, i * 2 + 1)
                    row_max(0, (3, 0)).then_inc(rowmax_done, 1)
                    dve.wait_ge(rowmax_ps, i * 2 + 2)
                    row_max(1, (6, 0))
                    row_max(1, (1, 2)).then_inc(rowmax_done, 1)
                    if not first:
                        add_projection(i - 1, b - 1, layer)
                    if ahead:
                        stats(i + 2, b + 2)
                        dve.wait_ge(xt_ps, n + 1)
                        normalise(i + 2, b + 2, xn[:, s])
                    if not first:
                        stats_second(i - 1, b - 1)
                    if last and layer == 0:
                        for j in range(2):
                            dve.wait_ge(xt_ps, j + 7)
                            normalise_second(j, j, xn[:, j])
                    elif last:
                        for j in range(EARLY):
                            normalise_second(B + j, j, xn_all[:, 2 * j:2 * j + 2, :])
                        for j in range(3):
                            dve.wait_ge(sw_hi, j + 1)
                            dve.tensor_tensor(wlo[SHARED][:, PIECES[j]], raw[1][:, PIECES[j]], whi[SHARED][:, PIECES[j]],
                                              ALU.subtract).then_inc(sw_split, 1)
                    if layer == 1 and not last:
                        rotary_b(i + 1, b + 1, 1 - s)
                    for c in range(DC):
                        bank = 7 if c == 0 else 0
                        rd = rden[:, S * c:S * c + S]
                        dve.wait_ge(pv_ps, i * 2 + (c + 1))
                        dve.reciprocal(rd, ps[:, bank, S:2 * S]).then_inc(rden_done, 1)
                        if layer == 0:
                            dve.wait_ge(rden_done, i * 2 + (c + 1))
                        else:
                            dve.wait_ge(rden_done, b * 4 + (2 * B + 2 * c + 1))
                            dve.tensor_tensor(rd, rd, anyv, ALU.mult).then_inc(rden_done, 1)
                            dve.wait_ge(rden_done, b * 4 + (2 * B + 2 * c + 2))
                        dve.tensor_tensor(attnT[:, c, :], ps[:, bank, 0:S], rd, ALU.mult).then_inc(attn_done, 1)
                    if last and layer == 1:
                        dve.wait_ge(gate_hi, 1)
                        dve.tensor_tensor(glo, gate.rearrange("p c e -> p (c e)"), ghi, ALU.subtract
                                          ).then_inc(gate_split, 1)
                    if last and layer == 0:
                        for j in range(2):
                            low_part(B + j, j, 1 + j)
                    elif last:
                        low_part(3 * B, 0, 6)
                    if last:
                        add_projection(i, b, layer)
                steps(dve, layer, step)
                dve.wait_ge(x_done, B * (layer + 1))
                stats_second(8 * layer + B - 1, B - 1)
                if layer == 1:
                    break

                for b in range(2, B):
                    dve.wait_ge(xt_ps, b + 7)
                    normalise_second(b, b, xn[:, b % 2])
                    if b > 2:
                        low_part(8 + b - 1, b - 1, 1 + (b - 1) % 2)
                low_part(8 + B - 1, B - 1, 1 + (B - 1) % 2)

                def split_patterns(t, s, free):
                    dve.wait_ge(pat_in[s], t * 16 + 16)
                    if not free:
                        dve.wait_ge(ia_ps, t * 16 + (8 * s - 8))
                    dve.tensor_copy(phi[:, s], pat[:, s]).then_inc(phi_done, 1)
                    dve.wait_ge(phi_done, t * 2 + (s + 1))
                    dve.tensor_tensor(plo[:, s], pat[:, s], phi[:, s], ALU.subtract).then_inc(pat_split, 1)

                for s in range(2):
                    split_patterns(0, s, True)
                with dve.Fori(1, 4) as t:
                    for s in range(2):
                        split_patterns(t, s, False)

                count = [0]

                def link(ins):
                    count[0] += 1
                    ins.then_inc(tk_step, 1)
                    dve.wait_ge(tk_step, count[0])

                def top_k(j, data, chunks, k, out):
                    n, tot = 8 * chunks, 9 * j
                    key_, flip_, hi_, lo_, tied_, above_, lower_, eq_, out_ = (
                        a[:, 0:n] for a in (key, flip, khi, klo, tied, above, above_lo, eqb, out))

                    def per_batch(a):
                        return a.unsqueeze(1).to_broadcast([P, chunks, 8])

                    def chunked(a):
                        return a.rearrange("p (c b) -> p c b", b=8)

                    def sum_chunks(src):
                        with nc.allow_low_precision(reason="counts up to 16 are exact in bfloat16"):
                            dve.tensor_reduce(cntb, src.rearrange("p (c b) -> p b c", b=8), AX, ALU.add
                                              ).then_inc(tk_cnt, 1)

                    link(dve.tensor_scalar(key_, data, 0.0, None, ALU.add))
                    link(dve.tensor_scalar(flip_.bitcast(I32), key_.bitcast(I32), 31, -2 ** 31,
                                           ALU.arith_shift_right, ALU.bitwise_or))
                    link(dve.tensor_tensor(key_.bitcast(I32), key_.bitcast(I32), flip_.bitcast(I32), ALU.bitwise_xor))
                    halves = key_.bitcast(U16).rearrange("p (n two) -> p n two", two=2)
                    link(dve.tensor_copy(hi_, halves[:, :, 1]))
                    link(dve.tensor_copy(lo_, halves[:, :, 0]))

                    def search(keys, tot0):
                        link(dve.memset(thr, 0.0))
                        c0 = count[0]
                        part = chunks // 4
                        for it in range(DIGITS):
                            dve.scalar_tensor_tensor(out=chunked(level), in0=digit.unsqueeze(2).to_broadcast([P, RADIX, 8]),
                                                     scalar=float(RADIX ** (DIGITS - 1 - it)),
                                                     in1=thr.unsqueeze(1).to_broadcast([P, RADIX, 8]),
                                                     op0=ALU.mult, op1=ALU.add).then_inc(tk_step, 1)
                            dve.wait_ge(tk_step, it * 3 + (c0 + 1))
                            for h in range(4):
                                dve.tensor_tensor(reached[:, part * h:part * h + part, :].rearrange("p c (j b) -> p c j b", b=8),
                                                  chunked(keys)[:, part * h:part * h + part, :].unsqueeze(2)
                                                  .to_broadcast([P, part, RADIX, 8]),
                                                  chunked(level).unsqueeze(1).to_broadcast([P, part, RADIX, 8]),
                                                  ALU.is_ge).then_inc(tk_cnt, 1)
                            dve.wait_ge(tk_tot, it + (tot0 + 1))
                            dve.scalar_tensor_tensor(out=met, in0=ps[:, 7, 0:P], scalar=float(k), in1=level,
                                                     op0=ALU.is_ge, op1=ALU.mult).then_inc(tk_step, 1)
                            dve.wait_ge(tk_step, it * 3 + (c0 + 2))
                            dve.tensor_reduce(thr, met.rearrange("p (j b) -> p b j", b=8), AX, ALU.max
                                              ).then_inc(tk_step, 1)
                            dve.wait_ge(tk_step, it * 3 + (c0 + 3))
                        count[0] += 3 * DIGITS

                    search(hi_, tot)
                    link(dve.tensor_tensor(chunked(above_), chunked(hi_), per_batch(thr), ALU.is_gt))
                    sum_chunks(above_)
                    link(dve.tensor_tensor(chunked(tied_), chunked(hi_), per_batch(thr), ALU.is_equal))
                    link(dve.tensor_tensor(lo_, lo_, tied_, ALU.mult))
                    search(lo_, tot + 4)
                    link(dve.tensor_tensor(chunked(lower_), chunked(lo_), per_batch(thr), ALU.is_gt))
                    link(dve.tensor_tensor(above_, above_, lower_, ALU.add))
                    sum_chunks(above_)
                    link(dve.tensor_tensor(chunked(eq_), chunked(lo_), per_batch(thr), ALU.is_equal))
                    dve.tensor_tensor(eq_, eq_, tied_, ALU.mult).then_inc(tk_cnt, 1)
                    dve.wait_ge(tk_tot, tot + 9)
                    link(dve.scalar_tensor_tensor(out=out_, in0=ps[:, 7, 0:n], scalar=float(k), in1=eq_,
                                                  op0=ALU.is_le, op1=ALU.mult))
                    link(dve.tensor_tensor(out_, out_, above_, ALU.add))

                for g in range(4):
                    dve.wait_ge(ia_done[g], 16)
                link(dve.tensor_scalar(acts, acts, 1.0 / S, None, ALU.mult))
                top_k(0, acts, 16, TOP_I, selm)
                chunk8 = "p (c b) -> p c b"
                dve.tensor_tensor(wpad[:, :, 0:8], acts.rearrange(chunk8, b=8), selm.rearrange(chunk8, b=8),
                                  ALU.mult).then_inc(tk_cnt, 1)
                dve.wait_ge(pa_done, 1)
                top_k(1, acts[:, 0:64], 8, TOP_P, selm)
                dve.tensor_reduce(pmax, acts[:, 0:64].rearrange("p (c b) -> p b c", b=8), AX, ALU.max
                                  ).then_inc(sm_dve, 1)
                dve.wait_ge(sm_pe, 1)
                dve.tensor_reduce(mx8[0:8, 0:1], ps[0:8, 6, 0:P], AX, ALU.max).then_inc(sm_dve, 1)
                dve.wait_ge(sm_dve, 2)
                dve.tensor_scalar(mxd[0:8, :], ident[0:8, 0:8], mx8[0:8, 0:1], None, ALU.mult).then_inc(sm_dve, 1)
                dve.wait_ge(sm_pe, 2)
                g64, s64 = gtm[:, 0:64].rearrange(chunk8, b=8), selm[:, 0:64].rearrange(chunk8, b=8)
                dve.tensor_copy(rs8, ps[:, 6, 128:136]).then_inc(sm_dve, 1)
                dve.wait_ge(sm_dve, 4)
                dve.tensor_tensor(g64, acts[:, 0:64].rearrange(chunk8, b=8), rs8.unsqueeze(1).to_broadcast([P, 8, 8]),
                                  ALU.subtract).then_inc(sm_dve, 1)
                dve.wait_ge(sm_act, 1)
                dve.tensor_tensor(s64, g64, s64, ALU.mult).then_inc(sm_dve, 1)
                dve.wait_ge(sm_dve, 6)
                dve.tensor_reduce(dsum, selm[:, 0:64].rearrange("p (c b) -> p b c", b=8), AX, ALU.add
                                  ).then_inc(sm_dve, 1)
                dve.wait_ge(sm_pe, 3)
                dve.reciprocal(rs8, ps[:, 6, 136:144]).then_inc(sm_dve, 1)
                dve.wait_ge(sm_dve, 8)
                dve.tensor_tensor(s64, s64, rs8.unsqueeze(1).to_broadcast([P, 8, 8]), ALU.mult).then_inc(sm_dve, 1)
                dve.wait_ge(agg_ps, 1)
                dve.tensor_copy(aggT, ps[:, 5, 0:8]).then_inc(agg_done, 1)
                dve.wait_ge(oa_done, 1)
                top_k(2, acts, 16, TOP_O, selm)
                dve.tensor_tensor(wpad[:, :, 0:8], acts.rearrange(chunk8, b=8), selm.rearrange(chunk8, b=8),
                                  ALU.mult).then_inc(tk_cnt, 1)
                dve.wait_ge(any_ps, 1)
                dve.tensor_scalar(anyv, ps[:, 0, 0:S], 1.0, None, ALU.min).then_inc(any_done, 1)
                for b in range(B):
                    dve.wait_ge(op_rows, b + 1)
                    xt = x_sb[:, 2 * b:2 * b + 2, :]
                    dve.scalar_tensor_tensor(out=xt, in0=ps[:, 1 + b % 2, 0:D].unsqueeze(1).to_broadcast([P, 2, D]),
                                             scalar=tg[:, 2:3], in1=xt, op0=ALU.mult, op1=ALU.add
                                             ).then_inc(x2_done, 1)
                    if 1 <= b <= 2:
                        normalise(B + b - 1, b - 1, xn[:, b - 1])
                    if b < 2:
                        dve.wait_ge(x2_done, b + 1)
                        stats(B + b, b)

            for b in range(B):
                if b >= EARLY:
                    normalise_second(B + b, b, xn_all[:, 2 * b:2 * b + 2, :])
                if b == EARLY:
                    low_part(25, 1, 6)

            def gated(u, s, f, h, reused):
                at = 1024 * s + 512 * f
                dve.wait_ge(gelu_done, u * 2 + (f + 1))
                if reused:
                    dve.wait_ge(h_done, u * 2 + f)
                dve.tensor_tensor(hval, hgl[:, f, :], ps[:, 2 * f + 1, :], ALU.mult).then_inc(hval_done, 1)
                dve.wait_ge(hval_done, u * 2 + (f + 1))
                dve.tensor_copy(h[0][:, at:at + 512], hval).then_inc(hhi_done, 1)
                dve.wait_ge(hhi_done, u * 2 + (f + 1))
                dve.tensor_tensor(h[1][:, at:at + 512], hval, h[0][:, at:at + 512], ALU.subtract).then_inc(h_done, 1)

            def add_shared(u):
                dve.wait_ge(down_ps, u + 1)
                xt = x_sb[:, 2 * u:2 * u + 2, :]
                dve.scalar_tensor_tensor(out=xt, in0=ps[:, 4 + u % 2, :].rearrange("p (t d) -> p t d", t=2),
                                         scalar=tg[:, 3:4], in1=xt, op0=ALU.mult, op1=ALU.add
                                         ).then_inc(down_done, 1)

            def shared_half(h):
                gated(h // 2, h // 2 % 2, h % 2, (hhi_s, hlo_s), h > 0)
                if h % 2 == 0 and h > 0:
                    add_shared(h // 2 - 1)

            def low_weights(x, slot, piece):
                dve.wait_ge(gu_hi, x * 2 + (piece + 1))
                dve.tensor_tensor(wlo[slot][:, PIECES[piece]], raw[slot][:, PIECES[piece]],
                                  whi[slot][:, PIECES[piece]], ALU.subtract).then_inc(gu_split, 1)

            for h in range(8):
                if h > 0 and h + 1 < B:
                    low_part(24 + h + 1, h + 1, 6)
                shared_half(h)
            count = [0]

            def route(ins):
                count[0] += 1
                ins.then_inc(rt_dve, 1)
                dve.wait_ge(rt_dve, count[0])

            logits = ps[:, 7, 256:512].rearrange("p (t e) -> p t e", e=E)
            pr3 = probs.rearrange("p (t e) -> p t e", e=E)
            cols = cum[:, 0:16]
            dve.wait_ge(rt_pe, 1)
            route(dve.tensor_reduce(cols, logits, AX, ALU.max))
            route(dve.tensor_tensor(pr3, logits, cols.unsqueeze(2).to_broadcast([P, 16, E]), ALU.subtract))
            dve.wait_ge(rt_act, 1)
            route(dve.tensor_reduce(cols, pr3, AX, ALU.add))
            route(dve.reciprocal(cum[:, 16:32], cols))
            route(dve.tensor_tensor(sc2.rearrange("p t (b e) -> p b t e", b=B),
                                    probs.rearrange("p (b t e) -> p b t e", b=B, t=2),
                                    cum[:, 16:32].rearrange("p (b t) -> p b t", t=2).unsqueeze(3)
                                    .to_broadcast([P, B, 2, E]), ALU.mult))
            shared_half(8)
            shared_half(9)
            dve.wait_ge(rt_pe, 2)
            route(dve.tensor_copy(work, ps[:, 7, 0:S]))
            for j in range(CAP // 8):
                route(dve.max(mx8, work))
                route(dve.match_replace(work, mx8, work, -1.0))
                if j == 1:
                    shared_half(10)
            shared_half(11)
            route(dve.tensor_scalar(work, work, 0.0, None, ALU.is_lt))
            route(dve.memset(probs, 1.0))
            route(dve.tensor_tensor_scan(cum, probs, work, 0.0, ALU.mult, ALU.add))
            route(dve.tensor_tensor(posm, cum, work, ALU.mult))
            shared_half(12)
            dve.wait_ge(rt_pe, 3)
            route(dve.tensor_copy(posT, ps[:, 7, 0:S].rearrange("p (t m) -> p t m", t=2)))

            def slots_one_hot(b):
                for t in range(2):
                    if b >= 2:
                        dve.wait_ge(disp_ps, DC * (b - 1))
                        dve.wait_ge(gw_done, 2 * (b - 1))
                    dve.tensor_tensor(G[b % 2][:, t].rearrange("p (e s) -> p e s", e=E),
                                      iota.unsqueeze(1).to_broadcast([P, E, 32]),
                                      posT[:, t, E * b:E * b + E].unsqueeze(2).to_broadcast([P, E, 32]), ALU.is_equal
                                      ).then_inc(g_done, 1)

            for h in range(13, 16):
                shared_half(h)
                if h < 15:
                    low_weights(0, 0, h - 13)
                if h == 13:
                    slots_one_hot(0)
            dve.wait_ge(gu_ps, 2 * B)
            add_shared(B - 1)

            for b in range(B):
                s = b % 2
                if b > 0:
                    slots_one_hot(b)
                for t in range(2):
                    dve.wait_ge(g_done, 2 * b + t + 1)
                    if b >= 2:
                        dve.wait_ge(gwt_ps, b - 1)
                    dve.tensor_tensor(GW[s][:, t].rearrange("p (e s) -> p e s", e=E),
                                      G[s][:, t].rearrange("p (e s) -> p e s", e=E),
                                      sc2[:, t, E * b:E * b + E].unsqueeze(2).to_broadcast([P, E, 32]), ALU.mult
                                      ).then_inc(gw_done, 1)

            def two_experts(t, last):
                for s in range(2):
                    for f in range(2):
                        if not (last and s == 1):
                            low_weights(t * 2 + (s + 1), 1 - s, f)
                        gated(t * 2 + (B + s), s, f, (hhi_e, hlo_e), True)

            with dve.Fori(0, E // 2 - 1) as t:
                two_experts(t, False)
            two_experts(E // 2 - 1, True)
            for b in range(B):
                dve.wait_ge(comb_ps, b + 1)
                xt = x_sb[:, 2 * b:2 * b + 2, :]
                dve.scalar_tensor_tensor(out=xt, in0=ps[:, (6 + b) % 8, :].rearrange("p (t d) -> p t d", t=2),
                                         scalar=tg[:, 3:4], in1=xt, op0=ALU.mult, op1=ALU.add).then_inc(y_done, 1)


def kernel(**inputs):
    import numpy as np
    from concourse import bacc
    from concourse.bass_utils import run_bass_kernel_spmd

    a = {k: np.asarray(v) for k, v in inputs.items()}
    f32 = np.float32

    def halves(w):
        return np.ascontiguousarray(w.reshape(DC, P, -1).transpose(1, 0, 2))

    def grouped(w):
        return np.pad(w, ((0, 0), (0, NG * GR - D)))

    def attention(wq, bq, wk, bk, wv, bv, wo, bo):
        cols = [halves(grouped(wq.T)).reshape(P, -1), halves(grouped(wk.T)).reshape(P, -1),
                halves(wv.T).reshape(P, -1), halves(wo.T).reshape(P, -1),
                np.broadcast_to(bv, (P, D)), np.broadcast_to(bo, (P, D))]
        for b in (bq, bk):
            cols.append(np.pad(np.pad(b, (0, NG * GR - D)).reshape(NG, GR).T, ((0, P - GR), (0, 0))))
        return np.concatenate(cols, axis=1)

    const = np.zeros((P, C_END - 4), f32)
    const[:, C_ID:C_ONE] = np.eye(P)
    const[:, C_ONE:C_TRI] = 1.0
    const[:, C_TRI:C_PAR] = np.triu(np.ones((P, P)))
    const[:, C_PAR:C_PAR + 16] = 1.0
    const[:, C_PAR + 48:C_PAR + 64] = 1.0
    const[:, C_PW:C_DIG] = float(RADIX) ** np.arange(DIGITS - 1, -1, -1)
    const[:, C_DIG:C_SEL] = np.arange(RADIX)
    for b in range(B):
        const[b::32, C_SEL + b] = 1.0
    const[:, C_IOTA:C_HM] = np.arange(1, 33)
    for j in range(GH):
        const[HD * j:HD * j + HD, C_HM + j] = 1.0
    for r in range(GR):
        const[r ^ 1, C_PERM + r] = 1.0
    kone = np.zeros((P - GR, NG * GH, SK), f32)
    for h in range(NG * GH):
        kone[h % GH, h, :] = 1.0
    inv = np.exp(np.arange(0, HD, 2, dtype=f32) * f32(-(4.0 * np.log(f32(10.0))) / HD)).astype(f32)
    angle = np.arange(S, dtype=f32)[:, None] * inv
    sin, cos = np.sin(angle).T, np.cos(angle).T
    rope_a, rope_b = np.zeros((GR, S), f32), np.zeros((GR, S), f32)
    for r in range(GR):
        m = (r % HD) // 2
        rope_a[r] = sin[m] if r % 2 == 0 else -sin[m]
        rope_b[r] = -cos[m]

    mask = np.pad(a["mask_1x1xSxS2_bk1"].reshape(S, SK), ((0, 0), (0, 80 - SK)))
    maskT = np.pad(mask.T, ((0, P - 80), (0, 0)))
    arrays = {
        "x": a["x"].reshape(T, D),
        "ctx": halves(a["ctx_1024"].reshape(KB, D).T),
        "gates": np.broadcast_to(np.concatenate([a["g_xattn"], a["g_ffn"]]), (P, 4)),
        "mask": np.ascontiguousarray(mask.reshape(2, P, 80).transpose(1, 0, 2)).view(np.uint32),
        "maskT": np.ascontiguousarray(maskT).view(np.uint32),
        "const": const,
        "kone": kone,
        "ropeA": rope_a,
        "ropeB": rope_b,
        "attn": np.stack([
            attention(*(a["L0_xattn_" + n] for n in ("Wq", "bq", "Wk", "bk", "Wv", "bv", "Wp", "bp"))),
            attention(*(a["L1_xattn_" + n] for n in ("Wq", "bq", "Wk", "bk", "Wv", "bv", "Wo", "bo")))]),
        "pat": a["L0_ffn_input_patterns"].reshape(8, 2, P, DC, P).transpose(0, 4, 1, 3, 2),
        "piw": a["L0_ffn_process_input_weights"].T.reshape(16, P, NP_).transpose(1, 0, 2),
        "pv": a["L0_ffn_process_values"].reshape(8, P, DV).transpose(1, 0, 2),
        "oiw": a["L0_ffn_output_input_weights"].T,
        "op": a["L0_ffn_output_patterns"].reshape(16, P, D).transpose(1, 0, 2),
        "gate": halves(a["L1_ffn_gate_w"].T),
        "wg": a["L1_ffn_Wg"].transpose(0, 2, 1).reshape(E, DC, P, F).transpose(0, 2, 1, 3),
        "wu": a["L1_ffn_Wu"].transpose(0, 2, 1).reshape(E, DC, P, F).transpose(0, 2, 1, 3),
        "wd": a["L1_ffn_Wd"].transpose(0, 2, 1).reshape(E, FC, P, D).transpose(0, 2, 1, 3),
        "sg": halves(a["L1_ffn_Ws_g"].T),
        "su": halves(a["L1_ffn_Ws_u"].T),
        "sd": a["L1_ffn_Ws_d"].T.reshape(FC, P, D).transpose(1, 0, 2),
    }
    arrays = {f"in_{k}": np.ascontiguousarray(v) for k, v in arrays.items()}
    nc = bacc.Bacc("TRN2", target_bir_lowering=False, num_devices=1)
    args = [nc.dram_tensor(k, v.shape, mybir.dt.from_np(v.dtype), kind="ExternalInput").ap()
            for k, v in arrays.items()]
    out = nc.dram_tensor("out_x", [T, D], F32, kind="ExternalOutput").ap()
    flamingo_kernel(nc, *args, out)
    r = run_bass_kernel_spmd(nc, [arrays], core_ids=[0])
    return r.results[0]["out_x"].reshape(B, S, D)
```
